# Optimizing a Trainium2 kernel written in Bass

```python
import numpy as np
import jax
import jax.numpy as jnp

def _softmax(x, axis=-1):
    return jax.nn.softmax(x, axis=axis)

def _gelu(x):
    return jax.nn.gelu(x, approximate=True)

def _silu(x):
    return jax.nn.silu(x)

def _sigmoid(x):
    return jax.nn.sigmoid(x)

def _layernorm(x, axis=-1, eps=1e-05):
    m = jnp.mean(x, axis=axis, keepdims=True)
    v = jnp.var(x, axis=axis, keepdims=True)
    return (x - m) / jnp.sqrt(v + eps)

def _scatter_add(tgt, idx, src, axis=0):
    return tgt.at[idx].add(src)

def _segment_sum(src, seg, n):
    return jax.ops.segment_sum(src, seg, n)
kernel_name = 'mk_decoder_preln_d2_seqx_r8_77a98d'

def setup_inputs(seed: int=0):
    np.random.seed(seed)
    _w = jnp.asarray

    def _rec_inputs():
        import jax
        import jax.numpy as jnp
        _rk = jax.random.key(seed)
        x = -0.0002928 + 1 * jax.random.normal(jax.random.fold_in(_rk, 1), (128, 64, 128), jnp.float32)
        _lenS = 64 - jax.random.randint(jax.random.fold_in(_rk, 7), (128,), 0, max(1, 64 // 4) + 1, jnp.int32)
        _lenS2 = 64 - jax.random.randint(jax.random.fold_in(_rk, 8), (128,), 0, max(1, 64 // 4) + 1, jnp.int32)
        _ctx_1024P = jax.random.normal(jax.random.fold_in(_rk, 11), (128, 16, 128), jnp.float32)
        _ctx_1024c = jax.random.dirichlet(jax.random.fold_in(_rk, 511), 0.3 * jnp.ones((16,), jnp.float32), (128, 64))
        _ctx_1024t = jnp.einsum('bsk,bkd->bsd', _ctx_1024c, _ctx_1024P)
        _ctx_1024t = _ctx_1024t * jax.lax.rsqrt(jnp.mean(jnp.square(_ctx_1024t)) + 1e-12) * 0.953939
        ctx_1024 = -1.39393e-06 + 0.999914 * (_ctx_1024t + 0.3 * jax.random.normal(jax.random.fold_in(_rk, 611), (128, 64, 128), jnp.float32))
        return (x, ctx_1024)
    x, ctx_1024 = _rec_inputs()

    def _L0_attn_setup():
        import jax, jax.numpy as jnp
        import numpy as np
        B, L, D, N = (2, 256, 128, 16)
        DT = 0.1
        key = jax.random.key(seed)
        ks = jax.random.split(key, 10)

        def w(k, shape, scale=0.02):
            return jax.random.normal(k, shape, jnp.float32) * scale
        log_min, log_max = (float(np.log(0.001)), float(np.log(0.1)))
        dt_bias = jax.random.uniform(ks[1], (D,), jnp.float32) * (log_max - log_min) + log_min
        return {'x': jax.random.normal(ks[0], (B, L, D), jnp.float32), 'delta_W': w(ks[2], (D, D)), 'delta_b': jnp.zeros((D,), jnp.float32), 'B_W': w(ks[3], (N, D)), 'B_b': jnp.zeros((N,), jnp.float32), 'C_W': w(ks[4], (N, D)), 'C_b': jnp.zeros((N,), jnp.float32), 'A_log': jnp.zeros((D, N), jnp.float32), 'dt_bias': dt_bias, 'tau': jnp.ones((N,), jnp.float32), 'Wi_W': w(ks[5], (N, D)), 'Wi_b': jnp.zeros((N,), jnp.float32), 'Wr_W': w(ks[6], (N, N)), 'sel_W': w(ks[7], (D, N)), 'sel_b': jnp.zeros((D,), jnp.float32), 'h0': jnp.zeros((1, N), jnp.float32)}
    _L0_attn_all = _L0_attn_setup()
    _L0_attn_in = {k: v for k, v in _L0_attn_all.items() if k in ('delta_W', 'delta_b', 'B_W', 'B_b', 'C_W', 'C_b', 'A_log', 'dt_bias', 'tau', 'Wi_W', 'Wi_b', 'Wr_W', 'sel_W', 'sel_b', 'h0')}
    del _L0_attn_all

    def _L0_xattn_setup():
        import jax, jax.numpy as jnp
        import numpy as np
        EPS_BACKEND = 1e-06
        NORM_EPS = 1e-06
        NUM_HEADS = 4

        def _mlstm_forward(q, k, v, ig_kernel, ig_bias, fg_kernel, fg_bias, outnorm_weight):
            B, S, E = q.shape
            NH = ig_bias.shape[0]
            DH = E // NH
            gate_input = jnp.concatenate([q, k, v], axis=-1)
            igate = gate_input @ ig_kernel + ig_bias
            fgate = gate_input @ fg_kernel + fg_bias
            qh = q.reshape(B, S, NH, DH).transpose(0, 2, 1, 3)
            kh = k.reshape(B, S, NH, DH).transpose(0, 2, 1, 3)
            vh = v.reshape(B, S, NH, DH).transpose(0, 2, 1, 3)
            ig = igate.transpose(0, 2, 1)
            fg = fgate.transpose(0, 2, 1)
            log_fg = jax.nn.log_sigmoid(fg)
            cums = jnp.concatenate([jnp.zeros((B, NH, 1), log_fg.dtype), jnp.cumsum(log_fg, axis=-1)], axis=-1)
            fg_mat = cums[..., :, None] - cums[..., None, :]
            mask = jnp.tril(jnp.ones((S + 1, S + 1), bool))
            fg_mat = jnp.where(mask, fg_mat, -jnp.inf)[..., 1:, 1:]
            log_D = fg_mat + ig[..., None, :]
            max_log_D = jnp.max(log_D, axis=-1, keepdims=True)
            D = jnp.exp(log_D - max_log_D)
            qk = jnp.einsum('bnsd,bntd->bnst', qh, kh) / jnp.sqrt(jnp.float32(DH))
            C = qk * D
            normalizer = jnp.maximum(jnp.abs(C.sum(-1, keepdims=True)), jnp.exp(-max_log_D))
            h = jnp.einsum('bnst,bntd->bnsd', C / (normalizer + EPS_BACKEND), vh)
            h = h.transpose(0, 2, 1, 3)
            mean = h.mean(-1, keepdims=True)
            var = h.var(-1, keepdims=True)
            hn = (h - mean) * jax.lax.rsqrt(var + NORM_EPS) * outnorm_weight
            return hn.reshape(B, S, E)
        key = jax.random.key(seed)
        ks = jax.random.split(key, 8)
        B, S, E, NH = (2, 256, 128, NUM_HEADS)
        DH = E // NH
        q = jax.random.normal(ks[0], (B, S, E), jnp.float32)
        k = jax.random.normal(ks[1], (B, S, E), jnp.float32)
        v = jax.random.normal(ks[2], (B, S, E), jnp.float32)
        ig_kernel = jax.random.normal(ks[3], (3 * E, NH), jnp.float32) * 0.02
        fg_kernel = jax.random.normal(ks[4], (3 * E, NH), jnp.float32) * 0.02
        ig_bias = jax.random.normal(ks[5], (NH,), jnp.float32) * 0.1
        fg_bias = jnp.linspace(3.0, 6.0, NH, dtype=jnp.float32)
        outnorm_weight = jnp.ones((NH, DH), jnp.float32)
        return {'q': q, 'k': k, 'v': v, 'ig_kernel': ig_kernel, 'ig_bias': ig_bias, 'fg_kernel': fg_kernel, 'fg_bias': fg_bias, 'outnorm_weight': outnorm_weight}
    _L0_xattn_all = _L0_xattn_setup()
    _L0_xattn_in = {k: v for k, v in _L0_xattn_all.items() if k in ('ig_kernel', 'ig_bias', 'fg_kernel', 'fg_bias', 'outnorm_weight')}
    del _L0_xattn_all

    def _L0_ffn_setup():
        import jax, jax.numpy as jnp
        import numpy as np
        EMBED = 128
        D_FF = 4 * EMBED
        N_EXPERTS = 8
        TOP_K = 2
        B, S = (2, 128)
        key = jax.random.key(seed)
        ks = jax.random.split(key, 10)
        sc_d = 1.0 / np.sqrt(EMBED)
        sc_h = 1.0 / np.sqrt(D_FF)
        return {'inputs': jax.random.normal(ks[0], (B, S, EMBED), jnp.float32), 'rw1': jax.random.normal(ks[1], (EMBED, D_FF), jnp.float32) * sc_d, 'rb1': jnp.zeros((D_FF,), jnp.float32), 'rw2': jax.random.normal(ks[2], (D_FF, N_EXPERTS), jnp.float32) * sc_h, 'rb2': jnp.zeros((N_EXPERTS,), jnp.float32), 'W1': jax.random.normal(ks[3], (N_EXPERTS, EMBED, D_FF), jnp.float32) * sc_d, 'b1': jnp.zeros((N_EXPERTS, D_FF), jnp.float32), 'W2': jax.random.normal(ks[4], (N_EXPERTS, D_FF, EMBED), jnp.float32) * sc_h, 'b2': jnp.zeros((N_EXPERTS, EMBED), jnp.float32)}
    _L0_ffn_all = _L0_ffn_setup()
    _L0_ffn_in = {k: v for k, v in _L0_ffn_all.items() if k in ('rw1', 'rb1', 'rw2', 'rb2', 'W1', 'b1', 'W2', 'b2')}
    del _L0_ffn_all

    def _L1_attn_setup():
        import jax, jax.numpy as jnp
        import numpy as np
        D_MODEL = 128
        NHEAD = 16
        HEAD_DIM = D_MODEL // NHEAD
        NPOS_MAX = 125
        SEQ = 128
        BATCH = 4

        def _cope(query, attn_logits, pos_emb):
            gates = jax.nn.sigmoid(attn_logits)
            pos = jnp.cumsum(gates[..., ::-1], axis=-1)[..., ::-1]
            pos = jnp.minimum(pos, NPOS_MAX - 1)
            pos_ceil = jnp.ceil(pos).astype(jnp.int32)
            pos_floor = jnp.floor(pos).astype(jnp.int32)
            logits_int = jnp.einsum('hbsd,dn->hbsn', query, pos_emb[0])
            logits_ceil = jnp.take_along_axis(logits_int, pos_ceil, axis=-1)
            logits_floor = jnp.take_along_axis(logits_int, pos_floor, axis=-1)
            w = pos - pos_floor.astype(pos.dtype)
            return logits_ceil * w + logits_floor * (1.0 - w)
        key = jax.random.key(seed)
        ks = jax.random.split(key, 10)
        s = 0.02
        return {'x': jax.random.normal(ks[0], (SEQ, BATCH, D_MODEL), dtype=jnp.float32), 'Wq': jax.random.normal(ks[1], (D_MODEL, D_MODEL), dtype=jnp.float32) * s, 'bq': jnp.zeros((D_MODEL,), dtype=jnp.float32), 'Wk': jax.random.normal(ks[2], (D_MODEL, D_MODEL), dtype=jnp.float32) * s, 'bk': jnp.zeros((D_MODEL,), dtype=jnp.float32), 'Wv': jax.random.normal(ks[3], (D_MODEL, D_MODEL), dtype=jnp.float32) * s, 'bv': jnp.zeros((D_MODEL,), dtype=jnp.float32), 'Wo': jax.random.normal(ks[4], (D_MODEL, D_MODEL), dtype=jnp.float32) * s, 'bo': jnp.zeros((D_MODEL,), dtype=jnp.float32), 'pos_emb': jax.random.normal(ks[5], (1, HEAD_DIM, NPOS_MAX), dtype=jnp.float32) * s}
    _L1_attn_all = _L1_attn_setup()
    _L1_attn_in = {k: v for k, v in _L1_attn_all.items() if k in ('Wq', 'bq', 'Wk', 'bk', 'Wv', 'bv', 'Wo', 'bo', 'pos_emb')}
    del _L1_attn_all

    def _L1_xattn_setup():
        import jax, jax.numpy as jnp
        import numpy as np
        B, S, H, NH = (2, 256, 128, 4)
        DH = H // NH
        EPS = 1e-06

        def _parallel_stabilized(qh, kh, vh, ig, fg):
            log_fg = jax.nn.log_sigmoid(fg)
            cs = jnp.cumsum(log_fg, axis=2)
            ltr = jnp.tril(jnp.ones((qh.shape[2], qh.shape[2]), dtype=bool))
            log_fg_mat = jnp.where(ltr, cs - jnp.swapaxes(cs, 2, 3), -jnp.inf)
            log_D = log_fg_mat + jnp.swapaxes(ig, 2, 3)
            max_log_D = jnp.max(log_D, axis=-1, keepdims=True)
            D = jnp.exp(log_D - max_log_D)
            qk = jnp.einsum('bhsd,bhtd->bhst', qh, kh) / jnp.sqrt(jnp.float32(DH))
            C = qk * D
            normalizer = jnp.maximum(jnp.abs(jnp.sum(C, axis=-1, keepdims=True)), jnp.exp(-max_log_D))
            return jnp.einsum('bhst,bhtd->bhsd', C / (normalizer + EPS), vh)
        key = jax.random.key(seed)
        ks = jax.random.split(key, 6)
        q = jax.random.normal(ks[0], (B, S, H), dtype=jnp.float32)
        k = jax.random.normal(ks[1], (B, S, H), dtype=jnp.float32)
        v = jax.random.normal(ks[2], (B, S, H), dtype=jnp.float32)
        igate_kernel = jax.random.normal(ks[3], (3 * H, NH), dtype=jnp.float32) * 0.02
        fgate_kernel = jax.random.normal(ks[4], (3 * H, NH), dtype=jnp.float32) * 0.02
        igate_bias = jax.random.normal(ks[5], (NH,), dtype=jnp.float32) * 0.1
        fgate_bias = jnp.linspace(3.0, 6.0, NH, dtype=jnp.float32)
        outnorm_scale = jnp.ones((H,), dtype=jnp.float32)
        return {'q': q, 'k': k, 'v': v, 'igate_kernel': igate_kernel, 'igate_bias': igate_bias, 'fgate_kernel': fgate_kernel, 'fgate_bias': fgate_bias, 'outnorm_scale': outnorm_scale}
    _L1_xattn_all = _L1_xattn_setup()
    _L1_xattn_in = {k: v for k, v in _L1_xattn_all.items() if k in ('igate_kernel', 'igate_bias', 'fgate_kernel', 'fgate_bias', 'outnorm_scale')}
    del _L1_xattn_all

    def _L1_ffn_setup():
        import jax, jax.numpy as jnp
        import numpy as np
        E, D, F = (8, 128, 512)
        B, S = (4, 256)

        def _layernorm(x, g, b, eps=1e-05):
            mu = jnp.mean(x, axis=-1, keepdims=True)
            var = jnp.var(x, axis=-1, keepdims=True)
            return (x - mu) * jax.lax.rsqrt(var + eps) * g + b
        key = jax.random.key(seed)
        ks = jax.random.split(key, 5)
        return {'input_features': jax.random.normal(ks[0], (B, S, D), jnp.float32), 'centroids': jax.random.normal(ks[1], (E, D), jnp.float32) * 0.1, 'ln_g': jnp.ones((E, D), jnp.float32), 'ln_b': jnp.zeros((E, D), jnp.float32), 'w1': jax.random.normal(ks[2], (E, F, D), jnp.float32) * (1.0 / np.sqrt(D).astype(np.float32)), 'b1': jnp.zeros((E, F), jnp.float32), 'w2': jax.random.normal(ks[3], (E, D, F), jnp.float32) * (1.0 / np.sqrt(F).astype(np.float32)), 'b2': jnp.zeros((E, D), jnp.float32)}
    _L1_ffn_all = _L1_ffn_setup()
    _L1_ffn_in = {k: v for k, v in _L1_ffn_all.items() if k in ('centroids', 'ln_g', 'ln_b', 'w1', 'b1', 'w2', 'b2')}
    del _L1_ffn_all
    return {'x': x, 'ctx_1024': ctx_1024, 'L0_attn_delta_W': _L0_attn_in['delta_W'], 'L0_attn_delta_b': _L0_attn_in['delta_b'], 'L0_attn_B_W': _L0_attn_in['B_W'], 'L0_attn_B_b': _L0_attn_in['B_b'], 'L0_attn_C_W': _L0_attn_in['C_W'], 'L0_attn_C_b': _L0_attn_in['C_b'], 'L0_attn_A_log': _L0_attn_in['A_log'], 'L0_attn_dt_bias': _L0_attn_in['dt_bias'], 'L0_attn_tau': _L0_attn_in['tau'], 'L0_attn_Wi_W': _L0_attn_in['Wi_W'], 'L0_attn_Wi_b': _L0_attn_in['Wi_b'], 'L0_attn_Wr_W': _L0_attn_in['Wr_W'], 'L0_attn_sel_W': _L0_attn_in['sel_W'], 'L0_attn_sel_b': _L0_attn_in['sel_b'], 'L0_attn_h0': _L0_attn_in['h0'], 'L0_xattn_ig_kernel': _L0_xattn_in['ig_kernel'], 'L0_xattn_ig_bias': _L0_xattn_in['ig_bias'], 'L0_xattn_fg_kernel': _L0_xattn_in['fg_kernel'], 'L0_xattn_fg_bias': _L0_xattn_in['fg_bias'], 'L0_xattn_outnorm_weight': _L0_xattn_in['outnorm_weight'], 'L0_ffn_rw1': _L0_ffn_in['rw1'], 'L0_ffn_rb1': _L0_ffn_in['rb1'], 'L0_ffn_rw2': _L0_ffn_in['rw2'], 'L0_ffn_rb2': _L0_ffn_in['rb2'], 'L0_ffn_W1': _L0_ffn_in['W1'], 'L0_ffn_b1': _L0_ffn_in['b1'], 'L0_ffn_W2': _L0_ffn_in['W2'], 'L0_ffn_b2': _L0_ffn_in['b2'], 'L1_attn_Wq': _L1_attn_in['Wq'], 'L1_attn_bq': _L1_attn_in['bq'], 'L1_attn_Wk': _L1_attn_in['Wk'], 'L1_attn_bk': _L1_attn_in['bk'], 'L1_attn_Wv': _L1_attn_in['Wv'], 'L1_attn_bv': _L1_attn_in['bv'], 'L1_attn_Wo': _L1_attn_in['Wo'], 'L1_attn_bo': _L1_attn_in['bo'], 'L1_attn_pos_emb': _L1_attn_in['pos_emb'], 'L1_xattn_igate_kernel': _L1_xattn_in['igate_kernel'], 'L1_xattn_igate_bias': _L1_xattn_in['igate_bias'], 'L1_xattn_fgate_kernel': _L1_xattn_in['fgate_kernel'], 'L1_xattn_fgate_bias': _L1_xattn_in['fgate_bias'], 'L1_xattn_outnorm_scale': _L1_xattn_in['outnorm_scale'], 'L1_ffn_centroids': _L1_ffn_in['centroids'], 'L1_ffn_ln_g': _L1_ffn_in['ln_g'], 'L1_ffn_ln_b': _L1_ffn_in['ln_b'], 'L1_ffn_w1': _L1_ffn_in['w1'], 'L1_ffn_b1': _L1_ffn_in['b1'], 'L1_ffn_w2': _L1_ffn_in['w2'], 'L1_ffn_b2': _L1_ffn_in['b2']}

def reference(x, ctx_1024, L0_attn_delta_W, L0_attn_delta_b, L0_attn_B_W, L0_attn_B_b, L0_attn_C_W, L0_attn_C_b, L0_attn_A_log, L0_attn_dt_bias, L0_attn_tau, L0_attn_Wi_W, L0_attn_Wi_b, L0_attn_Wr_W, L0_attn_sel_W, L0_attn_sel_b, L0_attn_h0, L0_xattn_ig_kernel, L0_xattn_ig_bias, L0_xattn_fg_kernel, L0_xattn_fg_bias, L0_xattn_outnorm_weight, L0_ffn_rw1, L0_ffn_rb1, L0_ffn_rw2, L0_ffn_rb2, L0_ffn_W1, L0_ffn_b1, L0_ffn_W2, L0_ffn_b2, L1_attn_Wq, L1_attn_bq, L1_attn_Wk, L1_attn_bk, L1_attn_Wv, L1_attn_bv, L1_attn_Wo, L1_attn_bo, L1_attn_pos_emb, L1_xattn_igate_kernel, L1_xattn_igate_bias, L1_xattn_fgate_kernel, L1_xattn_fgate_bias, L1_xattn_outnorm_scale, L1_ffn_centroids, L1_ffn_ln_g, L1_ffn_ln_b, L1_ffn_w1, L1_ffn_b1, L1_ffn_w2, L1_ffn_b2):
    import jax
    import jax.numpy as jnp

    def _L0_attn_ref(x, delta_W, delta_b, B_W, B_b, C_W, C_b, A_log, dt_bias, tau, Wi_W, Wi_b, Wr_W, sel_W, sel_b, h0):
        import jax, jax.numpy as jnp
        import numpy as np
        B, L, D, N = (2, 256, 128, 16)
        DT = 0.1
        Bsz, Ls, Dm = x.shape
        Ns = A_log.shape[1]
        gc = x.mean(axis=1)
        inp_sig = gc @ Wi_W.T + Wi_b
        cur = jnp.broadcast_to(h0, (Bsz, Ns))
        rec = cur @ Wr_W.T
        tau_c = jnp.clip(tau, 0.1, 10.0)
        dh_dt = (-cur + jnp.tanh(inp_sig + rec)) / tau_c[None, :]
        new_h = cur + DT * dh_dt
        sel = jax.nn.sigmoid(new_h @ sel_W.T + sel_b)
        xs = x * sel[:, None, :]
        delta = jax.nn.softplus(xs @ delta_W.T + delta_b + dt_bias)
        Bm = xs @ B_W.T + B_b
        Cm = xs @ C_W.T + C_b
        A = -jnp.exp(A_log)
        A_d = jnp.exp(A[None, None] * delta[..., None])
        factor = jnp.where(jnp.abs(A)[None, None] < 1e-06, delta[..., None], (A_d - 1.0) / A[None, None])
        B_d = factor * Bm[:, :, None, :]

        def step(h, inputs):
            Ad_t, Bd_t, x_t, C_t = inputs
            h = Ad_t * h + Bd_t * x_t[..., None]
            y = jnp.einsum('bdn,bn->bd', h, C_t)
            return (h, y)
        h_init = jnp.zeros((Bsz, Dm, Ns), x.dtype)
        _, ys = jax.lax.scan(step, h_init, (A_d.transpose(1, 0, 2, 3), B_d.transpose(1, 0, 2, 3), xs.transpose(1, 0, 2), Cm.transpose(1, 0, 2)))
        return ys.transpose(1, 0, 2)

    def _L0_xattn_ref(q, k, v, ig_kernel, ig_bias, fg_kernel, fg_bias, outnorm_weight):
        import jax, jax.numpy as jnp
        import numpy as np
        EPS_BACKEND = 1e-06
        NORM_EPS = 1e-06
        NUM_HEADS = 4

        def _mlstm_forward(q, k, v, ig_kernel, ig_bias, fg_kernel, fg_bias, outnorm_weight):
            B, S, E = q.shape
            NH = ig_bias.shape[0]
            DH = E // NH
            gate_input = jnp.concatenate([q, k, v], axis=-1)
            igate = gate_input @ ig_kernel + ig_bias
            fgate = gate_input @ fg_kernel + fg_bias
            qh = q.reshape(B, S, NH, DH).transpose(0, 2, 1, 3)
            kh = k.reshape(B, S, NH, DH).transpose(0, 2, 1, 3)
            vh = v.reshape(B, S, NH, DH).transpose(0, 2, 1, 3)
            ig = igate.transpose(0, 2, 1)
            fg = fgate.transpose(0, 2, 1)
            log_fg = jax.nn.log_sigmoid(fg)
            cums = jnp.concatenate([jnp.zeros((B, NH, 1), log_fg.dtype), jnp.cumsum(log_fg, axis=-1)], axis=-1)
            fg_mat = cums[..., :, None] - cums[..., None, :]
            mask = jnp.tril(jnp.ones((S + 1, S + 1), bool))
            fg_mat = jnp.where(mask, fg_mat, -jnp.inf)[..., 1:, 1:]
            log_D = fg_mat + ig[..., None, :]
            max_log_D = jnp.max(log_D, axis=-1, keepdims=True)
            D = jnp.exp(log_D - max_log_D)
            qk = jnp.einsum('bnsd,bntd->bnst', qh, kh) / jnp.sqrt(jnp.float32(DH))
            C = qk * D
            normalizer = jnp.maximum(jnp.abs(C.sum(-1, keepdims=True)), jnp.exp(-max_log_D))
            h = jnp.einsum('bnst,bntd->bnsd', C / (normalizer + EPS_BACKEND), vh)
            h = h.transpose(0, 2, 1, 3)
            mean = h.mean(-1, keepdims=True)
            var = h.var(-1, keepdims=True)
            hn = (h - mean) * jax.lax.rsqrt(var + NORM_EPS) * outnorm_weight
            return hn.reshape(B, S, E)
        return _mlstm_forward(q, k, v, ig_kernel, ig_bias, fg_kernel, fg_bias, outnorm_weight)

    def _L0_ffn_ref(inputs, rw1, rb1, rw2, rb2, W1, b1, W2, b2):
        import jax, jax.numpy as jnp
        import numpy as np
        EMBED = 128
        D_FF = 4 * EMBED
        N_EXPERTS = 8
        TOP_K = 2
        B, S = (2, 128)
        Bb, Ss, D = inputs.shape
        T = Bb * Ss
        xf = inputs.reshape(T, D)
        score = jax.nn.relu(xf @ rw1 + rb1) @ rw2 + rb2
        _, topi = jax.lax.top_k(score, TOP_K)
        mask = jnp.zeros(score.shape, bool).at[jnp.arange(T)[:, None], topi].set(True)
        gate = jax.nn.softmax(jnp.where(mask, score, -jnp.inf), axis=-1)
        out = jnp.zeros_like(xf)
        for e in range(N_EXPERTS):
            h = jax.nn.relu(xf @ W1[e] + b1[e])
            y = h @ W2[e] + b2[e]
            out = out + gate[:, e:e + 1] * y
        return out.reshape(Bb, Ss, D)

    def _L1_attn_ref(x, Wq, bq, Wk, bk, Wv, bv, Wo, bo, pos_emb):
        import jax, jax.numpy as jnp
        import numpy as np
        D_MODEL = 128
        NHEAD = 16
        HEAD_DIM = D_MODEL // NHEAD
        NPOS_MAX = 125
        SEQ = 128
        BATCH = 4

        def _cope(query, attn_logits, pos_emb):
            gates = jax.nn.sigmoid(attn_logits)
            pos = jnp.cumsum(gates[..., ::-1], axis=-1)[..., ::-1]
            pos = jnp.minimum(pos, NPOS_MAX - 1)
            pos_ceil = jnp.ceil(pos).astype(jnp.int32)
            pos_floor = jnp.floor(pos).astype(jnp.int32)
            logits_int = jnp.einsum('hbsd,dn->hbsn', query, pos_emb[0])
            logits_ceil = jnp.take_along_axis(logits_int, pos_ceil, axis=-1)
            logits_floor = jnp.take_along_axis(logits_int, pos_floor, axis=-1)
            w = pos - pos_floor.astype(pos.dtype)
            return logits_ceil * w + logits_floor * (1.0 - w)
        S, B, _ = x.shape

        def split_heads(t):
            return t.reshape(S, B, NHEAD, HEAD_DIM).transpose(2, 1, 0, 3)
        q = split_heads(x @ Wq + bq)
        k = split_heads(x @ Wk + bk)
        v = split_heads(x @ Wv + bv)
        scale = 1.0 / HEAD_DIM ** 0.5
        attn_logits = jnp.einsum('hbsd,hbtd->hbst', q, k) * scale
        attn_logits = attn_logits + _cope(q, attn_logits, pos_emb)
        attn = jax.nn.softmax(attn_logits, axis=-1)
        out = jnp.einsum('hbst,hbtd->hbsd', attn, v)
        out = out.transpose(2, 1, 0, 3).reshape(S, B, D_MODEL)
        return out @ Wo + bo

    def _L1_xattn_ref(q, k, v, igate_kernel, igate_bias, fgate_kernel, fgate_bias, outnorm_scale):
        import jax, jax.numpy as jnp
        import numpy as np
        B, S, H, NH = (2, 256, 128, 4)
        DH = H // NH
        EPS = 1e-06

        def _parallel_stabilized(qh, kh, vh, ig, fg):
            log_fg = jax.nn.log_sigmoid(fg)
            cs = jnp.cumsum(log_fg, axis=2)
            ltr = jnp.tril(jnp.ones((qh.shape[2], qh.shape[2]), dtype=bool))
            log_fg_mat = jnp.where(ltr, cs - jnp.swapaxes(cs, 2, 3), -jnp.inf)
            log_D = log_fg_mat + jnp.swapaxes(ig, 2, 3)
            max_log_D = jnp.max(log_D, axis=-1, keepdims=True)
            D = jnp.exp(log_D - max_log_D)
            qk = jnp.einsum('bhsd,bhtd->bhst', qh, kh) / jnp.sqrt(jnp.float32(DH))
            C = qk * D
            normalizer = jnp.maximum(jnp.abs(jnp.sum(C, axis=-1, keepdims=True)), jnp.exp(-max_log_D))
            return jnp.einsum('bhst,bhtd->bhsd', C / (normalizer + EPS), vh)
        Bq, Sq, Hq = q.shape
        x = jnp.concatenate([q, k, v], axis=-1)
        ig = x @ igate_kernel + igate_bias
        fg = x @ fgate_kernel + fgate_bias
        ig = jnp.transpose(ig, (0, 2, 1))[..., None]
        fg = jnp.transpose(fg, (0, 2, 1))[..., None]
        qh = jnp.transpose(q.reshape(Bq, Sq, NH, DH), (0, 2, 1, 3))
        kh = jnp.transpose(k.reshape(Bq, Sq, NH, DH), (0, 2, 1, 3))
        vh = jnp.transpose(v.reshape(Bq, Sq, NH, DH), (0, 2, 1, 3))
        h = _parallel_stabilized(qh, kh, vh, ig, fg)
        mean = jnp.mean(h, axis=-1, keepdims=True)
        var = jnp.mean((h - mean) ** 2, axis=-1, keepdims=True)
        h_norm = (h - mean) * jax.lax.rsqrt(var + 1e-05)
        h_norm = h_norm * outnorm_scale.reshape(1, NH, 1, DH)
        out = jnp.transpose(h_norm, (0, 2, 1, 3)).reshape(Bq, Sq, Hq)
        return out

    def _L1_ffn_ref(input_features, centroids, ln_g, ln_b, w1, b1, w2, b2):
        import jax, jax.numpy as jnp
        import numpy as np
        E, D, F = (8, 128, 512)
        B, S = (4, 256)

        def _layernorm(x, g, b, eps=1e-05):
            mu = jnp.mean(x, axis=-1, keepdims=True)
            var = jnp.var(x, axis=-1, keepdims=True)
            return (x - mu) * jax.lax.rsqrt(var + eps) * g + b
        Bf, Sf, Df = input_features.shape
        x = input_features.reshape(-1, Df)
        aff = x @ centroids.T
        assign = jnp.argmax(aff, axis=1)
        order = jnp.argsort(assign)
        xs = x[order]
        es = assign[order]
        alpha = jax.nn.sigmoid(jnp.take_along_axis(aff[order], es[:, None], axis=1))
        nE = centroids.shape[0]
        y = jnp.zeros_like(xs)
        for e in range(nE):
            h = _layernorm(xs, ln_g[e], ln_b[e])
            h = jax.nn.relu(h @ w1[e].T + b1[e])
            ye = xs + h @ w2[e].T + b2[e]
            y = y + jnp.where((es == e)[:, None], ye, 0.0)
        out_sorted = alpha * y + (1.0 - alpha) * xs
        inv = jnp.argsort(order)
        return out_sorted[inv].reshape(Bf, Sf, Df)
    x = x + _L0_attn_ref(_layernorm(x, axis=-1), L0_attn_delta_W, L0_attn_delta_b, L0_attn_B_W, L0_attn_B_b, L0_attn_C_W, L0_attn_C_b, L0_attn_A_log, L0_attn_dt_bias, L0_attn_tau, L0_attn_Wi_W, L0_attn_Wi_b, L0_attn_Wr_W, L0_attn_sel_W, L0_attn_sel_b, L0_attn_h0)
    x = x + _L0_xattn_ref(_layernorm(x, axis=-1), ctx_1024, ctx_1024, L0_xattn_ig_kernel, L0_xattn_ig_bias, L0_xattn_fg_kernel, L0_xattn_fg_bias, L0_xattn_outnorm_weight)
    x = x + _L0_ffn_ref(_layernorm(x, axis=-1), L0_ffn_rw1, L0_ffn_rb1, L0_ffn_rw2, L0_ffn_rb2, L0_ffn_W1, L0_ffn_b1, L0_ffn_W2, L0_ffn_b2)
    x = x + _L1_attn_ref(_layernorm(x, axis=-1), L1_attn_Wq, L1_attn_bq, L1_attn_Wk, L1_attn_bk, L1_attn_Wv, L1_attn_bv, L1_attn_Wo, L1_attn_bo, L1_attn_pos_emb)
    x = x + _L1_xattn_ref(_layernorm(x, axis=-1), ctx_1024, ctx_1024, L1_xattn_igate_kernel, L1_xattn_igate_bias, L1_xattn_fgate_kernel, L1_xattn_fgate_bias, L1_xattn_outnorm_scale)
    x = x + _L1_ffn_ref(_layernorm(x, axis=-1), L1_ffn_centroids, L1_ffn_ln_g, L1_ffn_ln_b, L1_ffn_w1, L1_ffn_b1, L1_ffn_w2, L1_ffn_b2)
    return x

_drawn_inputs = setup_inputs


def setup_inputs(seed=0):
    import zlib

    import numpy as np

    out = dict(_drawn_inputs(seed))
    spreads = {'L0_attn_delta_b': (0.0, 2.0),
     'L0_attn_B_b': (0.0, 2.0),
     'L0_attn_C_b': (0.0, 2.0),
     'L0_attn_A_log': (0.0, 2.0),
     'L0_attn_tau': (1.0, 0.6),
     'L0_attn_Wi_b': (0.0, 2.0),
     'L0_attn_sel_b': (0.0, 2.0),
     'L0_attn_h0': (0.0, 2.0),
     'L0_xattn_outnorm_weight': (1.0, 0.2),
     'L0_ffn_rb1': (0.0, 0.1),
     'L0_ffn_rb2': (0.0, 0.1),
     'L0_ffn_b1': (0.0, 0.1),
     'L0_ffn_b2': (0.0, 0.1),
     'L1_attn_bq': (0.0, 0.8),
     'L1_attn_bk': (0.0, 0.8),
     'L1_attn_bv': (0.0, 0.378),
     'L1_attn_bo': (0.0, 0.1),
     'L1_xattn_outnorm_scale': (1.0, 0.2),
     'L1_ffn_ln_g': (1.0, 0.2),
     'L1_ffn_ln_b': (0.0, 0.489),
     'L1_ffn_b1': (0.0, 0.496),
     'L1_ffn_b2': (0.0, 0.35)}
    factors = {'L0_attn_delta_W': 64.0,
     'L0_attn_B_W': 30.856,
     'L0_attn_C_W': 32.976,
     'L0_attn_dt_bias': 34.632,
     'L0_attn_Wi_W': 64.0,
     'L0_attn_Wr_W': 64.0,
     'L0_attn_sel_W': 64.0,
     'L0_xattn_ig_bias': 64.0,
     'L1_attn_Wq': 8.0,
     'L1_attn_Wk': 8.0,
     'L1_attn_Wv': 5.423,
     'L1_attn_pos_emb': 8.0,
     'L1_xattn_igate_bias': 64.0,
     'L1_xattn_fgate_kernel': 4.36}
    for name, (base, spread) in spreads.items():
        noise = np.random.default_rng([zlib.crc32(name.encode()), seed]).standard_normal(out[name].shape)
        drawn = base * np.exp(spread * noise) if base else spread * noise
        out[name] = jnp.asarray(drawn.astype(out[name].dtype))
    for name, factor in factors.items():
        out[name] = (out[name] * factor).astype(out[name].dtype)
    return out
```

```python
from contextlib import ExitStack

import numpy as np
import concourse.bass as bass
from concourse import mybir

ALU = mybir.AluOpType
ACT = mybir.ActivationFunctionType
AX = mybir.AxisListType
F32 = mybir.dt.float32
BF16 = mybir.dt.bfloat16
I32 = mybir.dt.int32
I16 = mybir.dt.int16
U32 = mybir.dt.uint32

P = 128
A, S, D = 128, 64, 128
TOK = A * S
T = 4
GT = T * P
G = TOK // GT
N = 16
NH = 4
DH = D // NH
E, F = 8, 512
FT = F // P
AH, AD = 16, 8
A_COLS = S


class Phase:

    def __init__(self, nc, tag):
        self.nc, self.tag, self.stack, self.taken = nc, tag, ExitStack(), []

    def __enter__(self):
        return self

    def __exit__(self, *what):
        self.stack.close()
        if self.taken and what[0] is None:
            self.nc.clear_and_free_semaphores(self.taken)
            self.nc.all_engine_barrier()
        return False

    def sb(self, name, shape, dtype=F32):
        return self.stack.enter_context(self.nc.sbuf_tensor(f"{self.tag}_{name}", shape, dtype))

    def psum(self, name, shape):
        return self.stack.enter_context(self.nc.psum_tensor(f"{self.tag}_{name}", shape, F32))

    def sem(self, name):
        self.taken.append(self.nc.alloc_semaphore(f"{self.tag}_{name}"))
        return self.taken[-1]

    def sems(self, *names):
        return {n: self.sem(n) for n in names}

    def block(self):
        return self.stack.enter_context(self.nc.Block())


def hold(engine, sem, value, const):
    engine.wait_ge(sem, value)
    engine.sem_inc(const["passed"], 1)


def ln_stats(dve, x, stats, mean_var):
    for t in range(T):
        dve.bn_stats(stats[:, t, :], x[:, t, :])
    dve.drain()
    for t in range(T):
        last = dve.bn_aggr(mean_var[:, t, :], stats[:, t, :])
    return last


def ln_rstd(pool, mean_var, eps, minus_half, rstd):
    pool.tensor_tensor(rstd, mean_var[:, :, 1], eps, ALU.add)
    pool.drain()
    return pool.tensor_tensor(rstd, rstd, minus_half, ALU.pow)


def ln_apply(dve, out, x, mean_var, rstd):
    for t in range(T):
        last = dve.tensor_scalar(out[:, t, :], x[:, t, :], mean_var[:, t, 0:1], rstd[:, t:t + 1],
                                 ALU.subtract, ALU.mult)
    return last


def token_groups(x):
    return x.rearrange("a s d -> (a s) d").rearrange("(g t p) d -> g p t d", p=P, t=T)


def phase_norm_in(nc, w, x, xn_t, const):
    with Phase(nc, "ni") as ph:
        x_in = ph.sb("x_in", [P, 2, T, D])
        xn = ph.sb("xn", [P, 2, T, D])
        stats = ph.sb("stats", [P, 2, T, 6])
        mean_var = ph.sb("mean_var", [P, 2, T, 2])
        rstd = ph.sb("rstd", [P, 2, T])
        tr = ph.psum("tr", [P, 2, GT])
        x_loaded = [ph.sem("x_loaded0"), ph.sem("x_loaded1")]
        x_free, stats_done, rstd_done = ph.sem("x_free"), ph.sem("stats_done"), ph.sem("rstd_done")
        normed, turned, kept = ph.sem("normed"), ph.sem("turned"), ph.sem("kept")
        src = token_groups(x)
        block = ph.block()

        @block.sync
        def _(sp):
            with sp.Fori(0, G // 2) as i:
                for j in range(2):
                    sp.wait_ge(x_free, i * 2 + (j + 1))
                    sp.dma_start(x_in[:, j], src[i * 2 + j]).then_inc(x_loaded[j], 16)

        @block.vector
        def _(dve):
            dve.sem_inc(x_free, 2)
            with dve.Fori(0, G // 2) as i:
                for j in range(2):
                    dve.wait_ge(x_loaded[j], i * 16 + 16)
                    ln_stats(dve, x_in[:, j], stats[:, j], mean_var[:, j]).then_inc(stats_done, 1)
                    dve.wait_ge(turned, i * 2 + (j + 1))
                    dve.wait_ge(rstd_done, i * 2 + (j + 1))
                    ln_apply(dve, xn[:, j], x_in[:, j], mean_var[:, j], rstd[:, j])
                    dve.drain().then_inc(normed, 1)
                    dve.sem_inc(x_free, 1)

        @block.gpsimd
        def _(pool):
            with pool.Fori(0, G // 2) as i:
                for j in range(2):
                    pool.wait_ge(stats_done, i * 2 + (j + 1))
                    ln_rstd(pool, mean_var[:, j], const["eps5"], const["minus_half"],
                            rstd[:, j]).then_inc(rstd_done, 1)

        @block.tensor
        def _(pe):
            pe.sem_inc(turned, 2)
            with pe.Fori(0, G // 2) as i:
                for j in range(2):
                    pe.wait_ge(normed, i * 2 + (j + 1))
                    pe.wait_ge(kept, i * 2 + (j + 1))
                    for t in range(T):
                        last = pe.transpose(tr[:, j, t * P:(t + 1) * P], xn[:, j, t, :], const["ident"])
                    last.then_inc(turned, 1)

        @block.scalar
        def _(act):
            act.sem_inc(kept, 2)
            with act.Fori(0, G // 2) as i:
                for j in range(2):
                    hold(act, turned, i * 2 + (j + 3), const)
                    act.activation(xn_t[:, bass.ds((i * 2 + j) * GT, GT)], tr[:, j, :], ACT.Copy).then_inc(kept, 1)


def phase_select(nc, w, xn_t, const, delta, split, guard, log_free):
    with Phase(nc, "se") as ph:
        wi_t = ph.sb("wi_t", [D, N])
        wr_t = ph.sb("wr_t", [N, N])
        sel_t = ph.sb("sel_t", [N, D])
        cols = ph.sb("cols", [N, 8])
        h0, tau, wi_b, c1, c2, th_bias = (cols[:, k:k + 1] for k in range(6))
        dcols = ph.sb("dcols", [D, 4])
        means = ph.sb("means", [D, A])
        th = ph.sb("th", [N, A])
        sel = ph.sb("sel", [D, A])
        delta_wt = ph.sb("delta_wt", [D, D])
        bc_wt = ph.sb("bc_wt", [D, 3 * 2 * N])
        bc_bias = ph.sb("bc_bias", [3 * 2 * N, 1])
        tmp = log_free
        R = 3 * 2 * N
        full = ph.sb("full", [R, 2, GT])
        part = ph.sb("part", [R, 2, GT], BF16)
        pz = ph.psum("pz", [P, 2, GT])
        pbc = ph.psum("pbc", [R, 2, GT])
        p_rec, p_sig, p_sel = (ph.psum(n, [P, 512]) for n in ("p_rec", "p_sig", "p_sel"))
        loaded, summed, psig, thd, newh = (ph.sem(n) for n in ("loaded", "summed", "psig", "thd", "newh"))
        col_ready, psel, seld, gated = (ph.sem(n) for n in ("col_ready", "psel", "seld", "gated"))
        z_ready, z_kept, bc_ready, bc_kept = (ph.sem(n) for n in ("z_ready", "z_kept", "bc_ready", "bc_kept"))
        logs = ph.sem("logs")
        rec_ready = ph.sem("rec_ready")
        block = ph.block()
        n_loads = 14

        @block.sync
        def _(sp):
            for dst, src in ((wi_t[:, :], w["wi_t"]), (wr_t[:, :], w["wr_t"]), (sel_t[:, :], w["sel_t"]),
                             (h0, w["h0"]), (tau, w["tau"]), (wi_b, w["wi_b"]),
                             (dcols[:, 0:1], w["sel_b"]), (dcols[:, 1:2], w["delta_b"]),
                             (dcols[:, 2:3], w["dt_bias"]), (delta_wt[:, :], w["delta_wt"]),
                             (bc_wt[:, :], w["bc_wt"]), (bc_bias[:, :], w["bc_bias"]),
                             (guard["a_log"][:, :], w["a_log"]), (guard["bc_pick"][:, :], w["bc_pick"])):
                sp.dma_start(dst, src).then_inc(loaded, 16)

        @block.tensor
        def _(pe):
            pe.wait_ge(loaded, 16 * n_loads)
            pe.matmul(p_rec[0:N, 0:1], wr_t[:, :], h0, start=True, stop=True).then_inc(rec_ready, 1)
            pe.wait_ge(summed, 1)
            pe.matmul(p_sig[0:N, 0:A], wi_t[:, :], means[:, :], start=True, stop=True).then_inc(psig, 1)
            pe.wait_ge(newh, 1)
            pe.matmul(p_sel[:, 0:A], sel_t[:, :], th[:, :], start=True, stop=True).then_inc(psel, 1)
            pe.wait_ge(gated, 1)
            with pe.Fori(0, G // 2) as i:
                for j in range(2):
                    xs = xn_t[:, bass.ds((i * 2 + j) * GT, GT)]
                    pe.wait_ge(z_kept, i * 2 + (j + 1))
                    pe.matmul(pz[:, j], delta_wt[:, :], xs, start=True, stop=True).then_inc(z_ready, 1)
                    pe.wait_ge(bc_kept, i * 2 + (j + 1))
                    pe.matmul(pbc[:, j], bc_wt[:, :], xs, start=True, stop=True).then_inc(bc_ready, 1)

        @block.scalar
        def _(act):
            act.wait_ge(loaded, 16 * n_loads)
            act.activation(guard["a"][:, :], guard["a_log"][:, :], ACT.Exp).then_inc(col_ready, 1)
            act.wait_ge(psig, 1)
            act.wait_ge(col_ready, 2)
            act.activation(th[:, :], p_sig[0:N, 0:A], ACT.Tanh, bias=th_bias, scale=1.0 / S).then_inc(thd, 1)
            act.wait_ge(psel, 1)
            act.activation(sel[:, :], p_sel[:, 0:A], ACT.Sigmoid, bias=dcols[:, 0:1]).then_inc(seld, 1)
            act.sem_inc(z_kept, 2)
            with act.Fori(0, G // 2) as i:
                for j in range(2):
                    hold(act, z_ready, i * 2 + (j + 1), const)
                    act.activation(delta[:, bass.ds((i * 2 + j) * GT, GT)], pz[:, j], ACT.Identity,
                                   bias=dcols[:, 3:4]).then_inc(z_kept, 1)
            act.drain()
            for func, scale, bias, src in ((ACT.Abs, 1.0, 0.0, delta), (ACT.Exp, -1.0, 0.0, tmp), (ACT.Ln, 1.0, 1.0, tmp)):
                for q in range(4):
                    c = slice(q * TOK // 4, (q + 1) * TOK // 4)
                    last = act.activation(tmp[:, c], src[:, c], func, scale=scale, bias=bias)
                act.drain()
            act.drain().then_inc(logs, 1)

        @block.vector
        def _(dve):
            dve.wait_ge(loaded, 16 * n_loads)
            dve.tensor_reduce(means[:, :], xn_t[:, :].rearrange("d (a s) -> d a s", s=S), AX.X, ALU.add).then_inc(summed, 1)
            dve.tensor_scalar(c1, tau, 0.1, 10.0, ALU.max, ALU.min)
            dve.drain()
            dve.reciprocal(c1, c1)
            dve.wait_ge(rec_ready, 1)
            dve.tensor_tensor(th_bias, p_rec[0:N, 0:1], wi_b, ALU.add)
            dve.drain()
            dve.tensor_scalar(c1, c1, 0.1, None, ALU.mult)
            dve.tensor_tensor(dcols[:, 3:4], dcols[:, 1:2], dcols[:, 2:3], ALU.add)
            dve.drain().then_inc(col_ready, 1)
            dve.tensor_tensor(c2, c1, h0, ALU.mult)
            dve.drain()
            dve.tensor_tensor(c2, h0, c2, ALU.subtract)
            dve.drain()
            dve.wait_ge(thd, 1)
            dve.tensor_scalar(th[:, :], th[:, :], c1, c2, ALU.mult, ALU.add).then_inc(newh, 1)
            dve.wait_ge(col_ready, 2)
            dve.tensor_scalar(guard["near0"][:, :], guard["a"][:, :], 1e-6, None, ALU.is_lt)
            dve.tensor_scalar(guard["inv"][:, :], guard["a"][:, :], 1e-30, None, ALU.max)
            dve.drain()
            dve.reciprocal(guard["inv"][:, :], guard["inv"][:, :])
            dve.tensor_scalar(guard["far"][:, :], guard["near0"][:, :], -1.0, 1.0, ALU.mult, ALU.add)
            dve.tensor_scalar(guard["a"][:, :], guard["a"][:, :], -1.0, None, ALU.mult)
            dve.drain()
            dve.tensor_tensor(guard["inv"][:, :], guard["inv"][:, :], guard["far"][:, :], ALU.mult)
            dve.drain()
            dve.tensor_scalar(guard["minus_inv"][:, :], guard["inv"][:, :], -1.0, None, ALU.mult)
            dve.wait_ge(seld, 1)
            xs3 = xn_t[:, :].rearrange("d (a s) -> d a s", s=S)
            dve.tensor_tensor(xs3, xs3, sel[:, :].rearrange("d (a o) -> d a o", o=1).broadcast_to((D, A, S)),
                              ALU.mult)
            dve.drain().then_inc(gated, 1)
            dve.sem_inc(bc_kept, 2)
            with dve.Fori(0, G // 2) as i:
                for j in range(2):
                    cols_ = bass.ds((i * 2 + j) * GT, GT)
                    dve.wait_ge(bc_ready, i * 2 + (j + 1))
                    dve.tensor_scalar(full[:, j], pbc[:, j], bc_bias[:, 0:1], None, ALU.add).then_inc(bc_kept, 1)
                    dve.drain()
                    dve.tensor_copy(part[:, j], full[:, j])
                    dve.drain()
                    dve.tensor_copy(split[0:32, cols_], part[0:32, j])
                    dve.tensor_tensor(full[:, j], full[:, j], part[:, j], ALU.subtract)
                    dve.drain()
                    dve.tensor_copy(part[:, j], full[:, j])
                    dve.drain()
                    dve.tensor_copy(split[32:64, cols_], part[32:64, j])
                    dve.tensor_tensor(split[64:R, cols_], full[64:R, j], part[64:R, j], ALU.subtract)
            dve.wait_ge(logs, 1)
            dve.scalar_tensor_tensor(delta[:, :], delta[:, :], 0.0, tmp[:, :], ALU.max, ALU.add)
            dve.drain()


def phase_scan(nc, w, xn_t, const, delta, split, guard):
    CH = 1024
    HALF = CH // 2
    with Phase(nc, "sc") as ph:
        decay = ph.sb("decay", [D, 2, CH])
        num = ph.sb("num", [D, 2, CH])
        wx = ph.sb("wx", [D, 2, CH])
        drive = ph.sb("drive", [D, 2, CH])
        h = ph.sb("h", [D, 2, CH])
        hc = ph.sb("hc", [D, 2, CH])
        pb = ph.psum("pb", [P, 2, CH])
        pc = ph.psum("pc", [P, CH])
        py = ph.psum("py", [P, CH])
        names = ("b_ready", "b_used", "c_ready", "hc_done", "y_added", "exp_done", "num_done", "drive_done",
                 "reset_done", "scanned", "y_kept")
        (b_ready, b_used, c_ready, hc_done, y_added, exp_done, num_done, drive_done, reset_done, scanned,
         y_kept) = (ph.sem(n) for n in names)
        block = ph.block()
        pick = guard["bc_pick"]

        @block.tensor
        def _(pe):
            with pe.Fori(0, TOK // CH) as c:
                def broadcast(out, which, n, done):
                    col = (which * N + n) * P
                    for q in range(2):
                        last = pe.matmul(out[:, q * HALF:(q + 1) * HALF], pick[:, col:col + P],
                                         split[:, bass.ds(c * CH + q * HALF, HALF)], start=True, stop=True)
                    last.then_inc(done, 1)

                def add_state(n):
                    for q in range(2):
                        cols = slice(q * HALF, (q + 1) * HALF)
                        last = pe.matmul(py[:, cols], const["ident"], hc[:, n % 2, cols], start=(n == 0),
                                         stop=(n == N - 1))
                    last.then_inc(y_added, 1)

                def broadcast_b(n):
                    pe.wait_ge(b_used, c * N + (n + 1))
                    broadcast(pb[:, n % 2], 0, n, b_ready)

                broadcast_b(0)
                for n in range(N):
                    if n < N - 1:
                        broadcast_b(n + 1)
                    pe.wait_ge(hc_done, c * N + (n + 1))
                    broadcast(pc, 1, n, c_ready)
                    if n == 0:
                        pe.wait_ge(y_kept, c + 1)
                    else:
                        add_state(n - 1)
                pe.wait_ge(hc_done, c * N + (N + 1))
                add_state(N - 1)

        @block.scalar
        def _(act):
            act.sem_inc(y_kept, 1)
            with act.Fori(0, TOK // CH) as c:
                for n in range(N):
                    s = n % 2
                    hold(act, scanned, c * N + (n + 1), const)
                    act.activation(decay[:, s], delta[:, bass.ds(c * CH, CH)], ACT.Exp,
                                   scale=guard["a"][:, n:n + 1])
                    act.drain()
                    act.activation(num[:, s], decay[:, s], ACT.Identity, scale=guard["minus_inv"][:, n:n + 1],
                                   bias=guard["inv"][:, n:n + 1]).then_inc(exp_done, 1)
                hold(act, y_added, c * N + (N + 2), const)
                act.activation(xn_t[:, bass.ds(c * CH, CH)], py[:, :], ACT.Copy).then_inc(y_kept, 1)

        @block.gpsimd
        def _(pool):
            with pool.Fori(0, TOK // CH) as c:
                for n in range(N):
                    s = n % 2
                    pool.wait_ge(num_done, c * N + (n + 1))
                    pool.tensor_tensor(drive[:, s], num[:, s], wx[:, s], ALU.mult).then_inc(drive_done, 1)
                    first = decay[:, s].rearrange("d (a t) -> d a t", t=S)[:, :, 0:1]
                    pool.memset(first, 0.0).then_inc(reset_done, 1)

        @block.vector
        def _(dve):
            dve.sem_inc(b_used, 2)
            dve.sem_inc(scanned, 2)
            dve.sem_inc(hc_done, 1)
            dve.sem_inc(y_added, 2)
            with dve.Fori(0, TOK // CH) as c:
                def drive_in(n):
                    s = n % 2
                    dve.wait_ge(b_ready, c * N + (n + 1))
                    dve.tensor_tensor(wx[:, s], pb[:, s], xn_t[:, bass.ds(c * CH, CH)], ALU.mult).then_inc(b_used, 1)
                    dve.wait_ge(exp_done, c * N + (n + 1))
                    dve.scalar_tensor_tensor(num[:, s], delta[:, bass.ds(c * CH, CH)], guard["near0"][:, n:n + 1],
                                             num[:, s], ALU.mult, ALU.add)
                    dve.drain().then_inc(num_done, 1)

                def scan_out(n):
                    s = n % 2
                    dve.wait_ge(drive_done, c * N + (n + 1))
                    dve.wait_ge(reset_done, c * N + (n + 1))
                    dve.tensor_tensor_scan(h[:, s], decay[:, s], drive[:, s], 0.0, ALU.mult, ALU.add)
                    dve.drain().then_inc(scanned, 1)
                    dve.wait_ge(y_added, c * N + (n + 1))
                    dve.wait_ge(c_ready, c * N + (n + 1))
                    dve.tensor_tensor(hc[:, s], pc[:, :], h[:, s], ALU.mult).then_inc(hc_done, 1)

                for n in range(N):
                    drive_in(n)
                    if n:
                        scan_out(n - 1)
                scan_out(N - 1)


def pipelined(engine, front, back):
    front(0, 0, 0)
    with engine.Fori(0, G // 2 - 1) as i:
        for j in range(2):
            front(i * 2 + (j + 1), 1 - j, i + j)
            back(i * 2 + j, j, i)
    front(G - 1, 1, G // 2 - 1)
    back(G - 2, 0, G // 2 - 1)
    back(G - 1, 1, G // 2 - 1)


def phase_mlstm(nc, w, tag, x, ctx, out, const, eps, scan_out=None):
    K = 8
    SCALE = float(DH) ** -0.5
    with Phase(nc, tag) as ph:
        gate_w = ph.sb("gate_w", [D, 3, 2 * NH])
        gate_b = ph.sb("gate_b", [P, T, 2 * NH])
        norm_w = ph.sb("norm_w", [P, D])
        seq_tri = ph.sb("seq_tri", [P, P])
        mask = ph.sb("mask", [P, GT], BF16)
        ident_b = ph.sb("ident_b", [P, P], BF16)
        minus_pick = ph.sb("minus_pick", [T * NH, T * NH * P])
        x_in = ph.sb("x_in", [P, 2, T, D])
        c_in = ph.sb("c_in", [P, 2, T, D])
        y_in = ph.sb("y_in", [P, 2, GT]) if scan_out is not None else None
        xr = ph.sb("xr", [P, 2, T, D])
        cv = ph.sb("cv", [P, 2, T, NH, DH + 1])
        qn = ph.sb("qn", [P, T, D])
        stats, mean_var, rstd = ph.sb("stats", [P, T, 6]), ph.sb("mean_var", [P, T, 2]), ph.sb("rstd", [P, T])
        qt = ph.sb("qt", [D, 2, GT])
        ct = ph.sb("ct", [D, 2, GT])
        gates = ph.sb("gates", [P, T, 2 * NH])
        soft = ph.sb("soft", [P, T, NH])
        logf = ph.sb("logf", [P, T, NH])
        cs = ph.sb("cs", [P, 2, T, NH])
        u = ph.sb("u", [P, 2, T, NH])
        ut = ph.sb("ut", [T * NH, P])
        mt = ph.sb("mt", [T * NH, 2, P])
        msum = ph.sb("msum", [P, T, NH])
        floor = ph.sb("floor", [P, 2, T * NH])
        dm = ph.sb("dm", [P, 2, GT])
        cm = ph.sb("cm", [P, 2, GT])
        den = ph.sb("den", [P, T * NH])
        hb = ph.sb("hb", [P, T * NH, DH])
        sq = ph.sb("sq", [P, T * NH, DH])
        msq = ph.sb("msq", [P, T * NH])
        hrstd = ph.sb("hrstd", [P, T * NH])
        eps_h = ph.sb("eps_h", [P, T * NH])
        half_h = ph.sb("half_h", [P, T * NH])
        xo = ph.sb("xo", [P, 2, T, D])
        pt0, pt1, pg = ph.psum("pt0", [P, GT]), ph.psum("pt1", [P, GT]), ph.psum("pg", [P, GT])
        pd, pq = ph.psum("pd", [P, 2, GT]), ph.psum("pq", [P, GT])
        ph_ = ph.psum("ph", [P, 2, GT])
        x_loaded = [ph.sem("x_loaded0"), ph.sem("x_loaded1")]
        c_loaded = [ph.sem("c_loaded0"), ph.sem("c_loaded1")]
        stored = [ph.sem("stored0"), ph.sem("stored1")]
        s = ph.sems("w_loaded", "w_ready", "x_used", "y_staged", "y_turned", "stats_done", "rstd_done", "normed",
                    "q_turned", "c_turned", "c_copied", "q_kept", "c_kept", "gates_in", "gates_done", "log_done",
                    "logf_done", "cs_ready", "u_ready", "ut_ready", "m_ready", "mt_ready", "msum_done",
                    "floor_done", "d_ready", "exp_done", "q_ready", "c_done", "pv_done", "h_read", "sq_done",
                    "hrstd_done", "summed")
        src, csrc, dst = token_groups(x), token_groups(ctx), token_groups(out)
        block = ph.block()
        n_loads = 7

        @block.sync
        def _(sp):
            for to, frm in ((gate_w[:, :, :], w["gate_w"]), (gate_b[:, :, :], w["gate_b"]),
                            (norm_w[:, :], w["norm_w"]), (seq_tri[:, :], w["seq_tri"]), (mask[:, :], w["mask"]),
                            (ident_b[:, :], w["ident_b"]), (minus_pick[:, :], w["minus_pick"])):
                sp.dma_start(to, frm).then_inc(s["w_loaded"], 16)

            def load(g, j, half):
                sp.wait_ge(s["x_used"], g + 1)
                sp.wait_ge(s["c_copied"], g + 1)
                sp.wait_ge(s["c_turned"], g + 1)
                sp.dma_start(x_in[:, j], src[g]).then_inc(x_loaded[j], 16)
                sp.dma_start(c_in[:, j], csrc[g]).then_inc(c_loaded[j], 16)

            def store(g, j, half):
                sp.wait_ge(s["summed"], g + 1)
                sp.dma_start(dst[g], xo[:, j]).then_inc(stored[j], 16)

            load(0, 0, 0)
            load(1, 1, 0)
            with sp.Fori(0, G // 2 - 1) as i:
                for j in range(2):
                    load(i * 2 + (j + 2), j, i + 1)
                    store(i * 2 + j, j, i)
            store(G - 2, 0, G // 2 - 1)
            store(G - 1, 1, G // 2 - 1)
            for j in range(2):
                sp.wait_ge(stored[j], 16 * (G // 2 + 1))

        @block.tensor
        def _(pe):
            pe.sem_inc(s["c_turned"], 2)
            pe.sem_inc(s["pv_done"], 2)
            pe.wait_ge(s["w_loaded"], 16 * n_loads)

            def front(g, j, half):
                if y_in is not None:
                    pe.wait_ge(s["y_staged"], g + 1)
                    pe.wait_ge(s["q_kept"], g + 1)
                    for t in range(T):
                        last = pe.transpose(pt0[:, t * P:(t + 1) * P], y_in[:, j, t * P:(t + 1) * P], const["ident"])
                    last.then_inc(s["y_turned"], 1)
                pe.wait_ge(c_loaded[j], half * 16 + 16)
                pe.wait_ge(s["c_kept"], g + 1)
                for t in range(T):
                    last = pe.transpose(pt1[:, t * P:(t + 1) * P], c_in[:, j, t, :], const["ident"])
                last.then_inc(s["c_turned"], 1)
                pe.wait_ge(s["q_kept"], g + 1)
                pe.wait_ge(s["normed"], g + 1)
                for t in range(T):
                    last = pe.transpose(pt0[:, t * P:(t + 1) * P], qn[:, t, :], const["ident"])
                last.then_inc(s["q_turned"], 1)
                pe.wait_ge(s["q_kept"], g + 2)
                pe.wait_ge(s["c_kept"], g + 2)
                pe.wait_ge(s["msum_done"], g + 1)
                for t in range(T):
                    tok = slice(t * P, (t + 1) * P)
                    o = pg[:, t * 2 * NH:(t + 1) * 2 * NH]
                    pe.matmul(o, qt[:, j, tok], gate_w[:, 0, :], start=True, stop=False)
                    pe.matmul(o, ct[:, j, tok], gate_w[:, 1, :], start=False, stop=False)
                    last = pe.matmul(o, ct[:, j, tok], gate_w[:, 2, :], start=False, stop=True)
                last.then_inc(s["gates_in"], 1)
                pe.wait_ge(s["logf_done"], g + 1)
                pe.matmul(pg[:, 32:32 + T * NH], seq_tri[:, :], logf[:, :, :].rearrange("p t h -> p (t h)"),
                          start=True, stop=True).then_inc(s["cs_ready"], 1)
                pe.wait_ge(s["u_ready"], g + 1)
                pe.transpose(pg[0:T * NH, 64:64 + P], u[:, j].rearrange("p t h -> p (t h)"),
                             const["ident"]).then_inc(s["ut_ready"], 1)
                hold(pe, s["m_ready"], g + 1, const)
                pe.transpose(pg[:, 192:192 + T * NH], mt[:, j], const["ident"][0:T * NH, 0:T * NH])\
                  .then_inc(s["mt_ready"], 1)

            def back(g, j, half):
                def pv(h):
                    pe.wait_ge(s["c_done"], g * NH + (h + 1 + K))
                    if h == 0:
                        pe.wait_ge(s["h_read"], g + 1)
                    for t in range(T):
                        o = ph_[:, t // 2, ((t % 2) * NH + h) * (DH + 1):((t % 2) * NH + h + 1) * (DH + 1)]
                        last = pe.matmul(o, cm[:, h % 2, t * P:(t + 1) * P], cv[:, j, t, h, :], start=True, stop=True)
                    last.then_inc(s["pv_done"], 1)

                for h in range(NH):
                    rows = slice(h * DH, (h + 1) * DH)
                    pe.wait_ge(s["exp_done"], g * NH + (h + 1))
                    pe.matmul(pd[:, h % 2], ident_b[:, :], mask[:, :], start=True, stop=False)
                    for t in range(T):
                        k = t * NH + h
                        last = pe.matmul(pd[:, h % 2, t * P:(t + 1) * P], minus_pick[:, k * P:(k + 1) * P],
                                         mt[:, j], start=False, stop=(t == T - 1))
                    last.then_inc(s["d_ready"], 1)
                    pe.wait_ge(s["c_done"], g * NH + (h + K))
                    for t in range(T):
                        tok = slice(t * P, (t + 1) * P)
                        last = pe.matmul(pq[:, tok], ct[rows, j, tok], qt[rows, j, tok], start=True, stop=True)
                    last.then_inc(s["q_ready"], 1)
                    if h:
                        pv(h - 1)
                pv(NH - 1)

            pipelined(pe, front, back)

        @block.scalar
        def _(act):
            act.sem_inc(s["q_kept"], 1)
            act.sem_inc(s["c_kept"], 1)
            act.sem_inc(s["exp_done"], 2)

            def front(g, j, half):
                if y_in is not None:
                    hold(act, s["y_turned"], g + 1, const)
                    act.activation(y_in[:, j], scan_out[:, bass.ds(g * GT, GT)], ACT.Copy).then_inc(s["y_staged"], 1)
                act.wait_ge(s["c_turned"], g + 3)
                act.wait_ge(s["c_done"], g * NH + (K - NH))
                act.activation(ct[:, j], pt1[:, :], ACT.Copy).then_inc(s["c_kept"], 1)
                act.wait_ge(s["q_turned"], g + 1)
                act.activation(qt[:, j], pt0[:, :], ACT.Copy).then_inc(s["q_kept"], 1)
                act.wait_ge(s["gates_done"], g + 1)
                act.activation(soft[:, :, :], gates[:, :, NH:], ACT.Abs)
                act.drain()
                act.activation(soft[:, :, :], soft[:, :, :], ACT.Exp, scale=-1.0)
                act.drain()
                act.activation(soft[:, :, :], soft[:, :, :], ACT.Ln, bias=1.0).then_inc(s["log_done"], 1)
                act.wait_ge(s["msum_done"], g + 2)
                act.activation(floor[:, j], msum[:, :, :].rearrange("p t h -> p (t h)"), ACT.Exp, scale=-1.0)\
                   .then_inc(s["floor_done"], 1)

            def back(g, j, half):
                for h in range(NH):
                    act.wait_ge(s["c_done"], g * NH + (h + K - 1))
                    act.wait_ge(s["d_ready"], g * NH + (h + 1))
                    for t in range(T):
                        tok = slice(t * P, (t + 1) * P)
                        last = act.activation(dm[:, h % 2, tok], pd[:, h % 2, tok], ACT.Exp,
                                              bias=u[:, j, t, h:h + 1])
                    last.then_inc(s["exp_done"], 1)

            pipelined(act, front, back)

        @block.gpsimd
        def _(pool):
            pool.sem_inc(s["c_copied"], 2)
            pool.memset(cv[:, :, :, :, :].rearrange("p j t h d -> p (j t h) d")[:, :, DH:DH + 1], 1.0)
            pool.memset(eps_h[:, :], DH * eps)
            pool.memset(half_h[:, :], -0.5)
            pool.drain()

            def front(g, j, half):
                pool.wait_ge(s["pv_done"], g * NH + (2 - NH)) if not isinstance(g, int) or g else None
                hold(pool, c_loaded[j], half * 16 + 16, const)
                pool.tensor_copy(cv[:, j].rearrange("p t h d -> p (t h) d")[:, :, 0:DH],
                                 c_in[:, j].rearrange("p t (h d) -> p (t h) d", h=NH)).then_inc(s["c_copied"], 1)
                pool.wait_ge(s["stats_done"], g + 1)
                ln_rstd(pool, mean_var[:, :, :], const["eps5"], const["minus_half"], rstd[:, :]).then_inc(s["rstd_done"], 1)

            def back(g, j, half):
                pool.wait_ge(s["sq_done"], g + 1)
                pool.tensor_tensor(hrstd[:, :], msq[:, :], eps_h[:, :], ALU.add)
                pool.drain()
                pool.tensor_tensor(hrstd[:, :], hrstd[:, :], half_h[:, :], ALU.pow).then_inc(s["hrstd_done"], 1)

            pipelined(pool, front, back)

        @block.vector
        def _(dve):
            dve.sem_inc(s["x_used"], 2)
            dve.sem_inc(s["y_turned"], 2)
            dve.sem_inc(s["c_done"], K)
            dve.sem_inc(s["msum_done"], 1)
            dve.sem_inc(s["h_read"], 1)
            dve.sem_inc(stored[0], 16)
            dve.sem_inc(stored[1], 16)
            dve.wait_ge(s["w_loaded"], 16 * n_loads)
            dve.tensor_scalar(norm_w[:, :], norm_w[:, :], float(DH) ** 0.5, None, ALU.mult)
            dve.drain()

            def front(g, j, half):
                dve.wait_ge(x_loaded[j], half * 16 + 16)
                if y_in is None:
                    dve.tensor_copy(xr[:, j], x_in[:, j])
                else:
                    dve.wait_ge(s["y_turned"], g + 3)
                    dve.tensor_tensor(xr[:, j], x_in[:, j], pt0[:, :].rearrange("p (t d) -> p t d", t=T), ALU.add)
                dve.drain().then_inc(s["x_used"], 1)
                ln_stats(dve, xr[:, j], stats, mean_var)
                dve.drain().then_inc(s["stats_done"], 1)
                dve.wait_ge(s["q_turned"], g) if not isinstance(g, int) or g else None
                dve.wait_ge(s["rstd_done"], g + 1)
                ln_apply(dve, qn, xr[:, j], mean_var, rstd)
                dve.drain().then_inc(s["normed"], 1)
                dve.wait_ge(s["gates_in"], g + 1)
                dve.tensor_tensor(gates[:, :, :], pg[:, 0:T * 2 * NH].rearrange("p (t h) -> p t h", t=T),
                                  gate_b[:, :, :], ALU.add)
                dve.drain().then_inc(s["gates_done"], 1)
                dve.wait_ge(s["log_done"], g + 1)
                dve.scalar_tensor_tensor(logf[:, :, :], gates[:, :, NH:], 0.0, soft[:, :, :], ALU.min, ALU.subtract)
                dve.drain().then_inc(s["logf_done"], 1)
                dve.wait_ge(s["cs_ready"], g + 1)
                run = pg[:, 32:32 + T * NH].rearrange("p (t h) -> p t h", t=T)
                dve.tensor_copy(cs[:, j], run)
                dve.tensor_tensor(u[:, j], gates[:, :, 0:NH], run, ALU.subtract)
                dve.drain().then_inc(s["u_ready"], 1)
                dve.wait_ge(s["ut_ready"], g + 1)
                dve.tensor_copy(ut[:, :], pg[0:T * NH, 64:64 + P])
                dve.drain()
                for q in range(P // S):
                    c = slice(q * S, (q + 1) * S)
                    dve.tensor_tensor_scan(mt[:, j, c], ut[:, c], ut[:, c], -3e38, ALU.max, ALU.max)
                dve.drain().then_inc(s["m_ready"], 1)
                dve.wait_ge(s["mt_ready"], g + 1)
                dve.wait_ge(s["floor_done"], g) if not isinstance(g, int) or g else None
                dve.tensor_tensor(msum[:, :, :], cs[:, j], pg[:, 192:192 + T * NH].rearrange("p (t h) -> p t h", t=T),
                                  ALU.add)
                dve.drain().then_inc(s["msum_done"], 1)

            def back(g, j, half):
                for h in range(NH):
                    dve.wait_ge(s["pv_done"], g * NH + (h + 1))
                    dve.wait_ge(s["q_ready"], g * NH + (h + 1))
                    dve.wait_ge(s["exp_done"], g * NH + (h + 3))
                    dve.scalar_tensor_tensor(cm[:, h % 2], pq[:, :], SCALE, dm[:, h % 2], ALU.mult, ALU.mult)\
                       .then_inc(s["c_done"], 1)
                dve.wait_ge(s["pv_done"], g * NH + (NH + 2))
                dve.wait_ge(s["floor_done"], g + 1)
                heads = [ph_[:, b, 0:2 * NH * (DH + 1)].rearrange("p (k d) -> p k d", d=DH + 1) for b in range(2)]
                part = [slice(b * 2 * NH, (b + 1) * 2 * NH) for b in range(2)]
                for b in range(2):
                    dve.scalar_tensor_tensor(den[:, part[b]], heads[b][:, :, DH], -1.0, floor[:, j, part[b]],
                                             ALU.mult, ALU.max)
                dve.drain()
                for b in range(2):
                    dve.tensor_tensor(den[:, part[b]], heads[b][:, :, DH], den[:, part[b]], ALU.max)
                dve.drain()
                dve.tensor_scalar(den[:, :], den[:, :], 1e-6, None, ALU.add)
                dve.drain()
                dve.reciprocal(den[:, :], den[:, :])
                dve.drain()

                def each(a, k=T * NH):
                    return a.rearrange("p (k o) -> p k o", o=1).broadcast_to((P, k, DH))

                for b in range(2):
                    dve.tensor_tensor(hb[:, part[b]], heads[b][:, :, 0:DH], each(den[:, part[b]], 2 * NH), ALU.mult)
                dve.drain().then_inc(s["h_read"], 1)
                dve.tensor_reduce(msq[:, :], hb[:, :, :], AX.X, ALU.add)
                dve.drain()
                dve.tensor_scalar(msq[:, :], msq[:, :], 1.0 / DH, None, ALU.mult)
                dve.drain()
                dve.tensor_tensor(hb[:, :, :], hb[:, :, :], each(msq[:, :]), ALU.subtract)
                dve.drain()
                dve.tensor_tensor(sq[:, :, :], hb[:, :, :], hb[:, :, :], ALU.mult)
                dve.drain()
                dve.tensor_reduce(msq[:, :], sq[:, :, :], AX.X, ALU.add)
                dve.drain().then_inc(s["sq_done"], 1)
                by_tile = hb[:, :, :].rearrange("p (t h) d -> p t (h d)", t=T)
                wide = norm_w[:, :].rearrange("p (o d) -> p o d", o=1).broadcast_to((P, T, D))
                dve.tensor_tensor(by_tile, by_tile, wide, ALU.mult)
                dve.drain()
                dve.wait_ge(s["hrstd_done"], g + 1)
                dve.tensor_tensor(hb[:, :, :], hb[:, :, :], each(hrstd[:, :]), ALU.mult)
                dve.drain()
                dve.wait_ge(stored[j], half * 16 + 16)
                dve.tensor_tensor(xo[:, j], xr[:, j], by_tile, ALU.add)
                dve.drain().then_inc(s["summed"], 1)

            pipelined(dve, front, back)


def column_groups(x):
    return x.rearrange("a (g t) d -> g a t d", t=T)


def phase_experts(nc, w, tag, x, out, const, routed):
    with Phase(nc, tag) as ph:
        w1 = ph.sb("w1", [D, E, F])
        w2 = ph.sb("w2", [P, E, FT, D])
        b1 = ph.sb("b1", [P, E, FT])
        b2 = ph.sb("b2", [E, D])
        iota = ph.sb("iota", [P, E])
        if routed:
            rw1 = ph.sb("rw1", [D, F])
            rb1 = ph.sb("rb1", [P, FT])
            rw2 = ph.sb("rw2", [P, FT, E])
            rb2 = ph.sb("rb2", [P, T, E])
            rh = ph.sb("rh", [P, FT, GT])
        else:
            cent = ph.sb("cent", [D, E])
            ln_g = ph.sb("ln_g", [D, E])
            ln_b = ph.sb("ln_b", [D, E])
            z = ph.sb("z", [P, T, D])
            zt = ph.sb("zt", [D, 2, GT])
        x_in = ph.sb("x_in", [P, 2, T, D])
        xf = ph.sb("xf", [P, 2, T, D])
        xft = ph.sb("xft", [D, 2, GT])
        stats, mean_var, rstd = ph.sb("stats", [P, T, 6]), ph.sb("mean_var", [P, T, 2]), ph.sb("rstd", [P, T])
        score = ph.sb("score", [P, T, E])
        top = ph.sb("top", [P, T, 8])
        top_i = ph.sb("top_i", [P, T, 8], U32)
        top_f = ph.sb("top_f", [P, T, 8])
        share = ph.sb("share", [P, 3, T])
        gate = ph.sb("gate", [P, 2, T, E])
        gate2 = ph.sb("gate2", [P, T, E])
        gate_t = ph.sb("gate_t", [E, 2, GT])
        hid = ph.sb("hid", [P, 2, FT, GT])
        xo = ph.sb("xo", [P, 2, T, D])
        pf, py = ph.psum("pf", [P, 2, GT]), ph.psum("py", [P, 2, GT])
        pt, pr, pg = ph.psum("pt", [P, GT]), ph.psum("pr", [P, 2, GT]), ph.psum("pg", [P, GT])
        x_loaded = [ph.sem("x_loaded0"), ph.sem("x_loaded1")]
        stored = [ph.sem("stored0"), ph.sem("stored1")]
        s = ph.sems("w_loaded", "w_bias", "w_ready", "x_used", "stats_done", "rstd_done", "normed", "turned", "kept",
                    "r_ready", "r_kept", "scored", "gap_done", "exp_done", "gated", "gate_turned", "gate_kept",
                    "h_ready", "h_kept", "y_ready", "y_used", "summed")
        NLN = 1 if routed else 2
        src, dst = column_groups(x), column_groups(out)
        block = ph.block()
        loads = [(w1[:, :, :], w["w1"]), (w2[:, :, :, :], w["w2"]), (b1[:, :, :], w["b1"]), (b2[:, :], w["b2"]),
                 (iota[:, :], w["iota"])]
        if routed:
            loads += [(rw1[:, :], w["rw1"]), (rb1[:, :], w["rb1"]), (rw2[:, :, :], w["rw2"]), (rb2[:, :, :], w["rb2"])]
        else:
            loads += [(cent[:, :], w["cent"]), (ln_g[:, :], w["ln_g"]), (ln_b[:, :], w["ln_b"])]

        def in_step(back, front):
            def body(g, j, half, nxt):
                steps = front(*nxt) if nxt else []
                for e in range(E + 1):
                    back(g, j, half, e)
                    if e < len(steps):
                        steps[e]()
            return body

        def run(engine, front, back):
            body = in_step(back, front)
            for step in front(0, 0, 0):
                step()
            with engine.Fori(0, G // 2 - 1) as i:
                for j in range(2):
                    body(i * 2 + j, j, i, (i * 2 + (j + 1), 1 - j, i + j))
            body(G - 2, 0, G // 2 - 1, (G - 1, 1, G // 2 - 1))
            body(G - 1, 1, G // 2 - 1, None)

        @block.sync
        def _(sp):
            def load(g, j):
                sp.wait_ge(s["x_used"], g + 1)
                sp.dma_start(x_in[:, j], src[g]).then_inc(x_loaded[j], 16)

            load(0, 0)
            for to, frm in loads:
                sp.dma_start(to, frm).then_inc(s["w_loaded"], 16)
            load(1, 1)

            def store(g, j):
                sp.wait_ge(s["summed"], g + 1)
                sp.dma_start(dst[g], xo[:, j]).then_inc(stored[j], 16)

            with sp.Fori(0, G // 2 - 1) as i:
                for j in range(2):
                    store(i * 2 + j, j)
                    load(i * 2 + (j + 2), j)
            store(G - 2, 0)
            store(G - 1, 1)
            for j in range(2):
                sp.wait_ge(stored[j], 16 * (G // 2 + 1))

        @block.gpsimd
        def _(pool):
            def front(g, j, half):
                def step():
                    for k in range(NLN):
                        pool.wait_ge(s["stats_done"], g * NLN + (k + 1))
                        ln_rstd(pool, mean_var[:, :, :], const["eps5"], const["minus_half"], rstd[:, :])\
                            .then_inc(s["rstd_done"], 1)
                return [step]

            run(pool, front, lambda g, j, half, e: None)

        @block.tensor
        def _(pe):
            pe.sem_inc(s["turned"], 1)
            pe.sem_inc(s["y_ready"], 1)
            pe.wait_ge(s["w_loaded"], 16 * len(loads))
            if not routed:
                for e in range(E):
                    for f in range(FT):
                        last = pe.matmul(pg[:, e * FT + f:e * FT + f + 1], w1[:, e, f * P:(f + 1) * P],
                                         ln_b[:, e:e + 1], start=True, stop=True)
                last.then_inc(s["w_bias"], 1)
                pe.wait_ge(s["w_ready"], 1)

            def front(g, j, half):
                def turn():
                    pe.wait_ge(s["gate_kept"], g + 1)
                    pe.wait_ge(s["normed"], g + 1)
                    for t in range(T):
                        last = pe.transpose(pt[:, t * P:(t + 1) * P], xf[:, j, t, :], const["ident"])
                    if not routed:
                        pe.wait_ge(s["kept"], g + 1)
                        for t in range(T):
                            last = pe.transpose(pr[:, 0, t * P:(t + 1) * P], z[:, t, :], const["ident"])
                    last.then_inc(s["turned"], 1)

                def route(f):
                    pe.wait_ge(s["kept"], g + 2)
                    pe.wait_ge(s["r_kept"], g * FT + (f + 1))
                    pe.matmul(pr[:, f % 2], rw1[:, f * P:(f + 1) * P], xft[:, j], start=True, stop=True)\
                      .then_inc(s["r_ready"], 1)

                def scores():
                    if routed:
                        pe.wait_ge(s["r_kept"], g * FT + (FT + 2))
                    else:
                        pe.wait_ge(s["kept"], g + 2)
                    pe.wait_ge(s["gated"], g + 1)
                    for t in range(T):
                        tok = slice(t * P, (t + 1) * P)
                        o = pg[:, t * E:(t + 1) * E]
                        if routed:
                            for f in range(FT):
                                last = pe.matmul(o, rh[:, f, tok], rw2[:, f, :], start=(f == 0), stop=(f == FT - 1))
                        else:
                            last = pe.matmul(o, xft[:, j, tok], cent[:, :], start=True, stop=True)
                    last.then_inc(s["scored"], 1)

                def turn_gates():
                    pe.wait_ge(s["gated"], g + 2)
                    for t in range(T):
                        last = pe.transpose(pt[0:E, t * P:(t + 1) * P], gate[:, j, t, :], const["ident"])
                    last.then_inc(s["gate_turned"], 1)

                if routed:
                    return [turn, lambda: (route(0), route(1)), lambda: (route(2), route(3)), scores, lambda: None,
                            turn_gates]
                return [turn, scores, lambda: None, turn_gates]

            def back(g, j, half, e):
                def second(v):
                    pe.wait_ge(s["y_used"], g * (E + 1) + (v + 1))
                    if v == 0:
                        pe.wait_ge(s["gate_kept"], g + 2)
                    else:
                        pe.wait_ge(s["h_kept"], g * E * FT + ((v - 1) * FT + FT + 2))
                    for t in range(T):
                        tok = slice(t * P, (t + 1) * P)
                        o = py[:, (g_par(j) + v) % 2, tok]
                        if v == 0:
                            last = pe.matmul(o, gate_t[:, j, tok], b2[:, :], start=True, stop=True)
                        else:
                            for f in range(FT):
                                last = pe.matmul(o, hid[:, (v - 1) % 2, f, tok], w2[:, v - 1, f, :],
                                                 start=(f == 0), stop=(f == FT - 1))
                    last.then_inc(s["y_ready"], 1)

                if e < E:
                    for f in range(FT):
                        pe.wait_ge(s["h_kept"], g * E * FT + (e * FT + f + 1))
                        pe.matmul(pf[:, f % 2], w1[:, e, f * P:(f + 1) * P], (xft if routed else zt)[:, j],
                                  start=True, stop=True).then_inc(s["h_ready"], 1)
                second(e)

            run(pe, front, back)

        @block.scalar
        def _(act):
            act.sem_inc(s["kept"], 1)
            act.sem_inc(s["gate_kept"], 1)
            act.sem_inc(s["r_kept"], 2)
            act.sem_inc(s["h_kept"], 2)

            def front(g, j, half):
                def keep():
                    act.wait_ge(s["turned"], g + 2)
                    if not routed:
                        act.activation(zt[:, j], pr[:, 0], ACT.Copy)
                    act.activation(xft[:, j], pt[:, :], ACT.Copy)
                    act.drain().then_inc(s["kept"], 1)

                def relu(f):
                    act.wait_ge(s["r_ready"], g * FT + (f + 1))
                    act.activation(rh[:, f], pr[:, f % 2], ACT.Relu, bias=rb1[:, f:f + 1]).then_inc(s["r_kept"], 1)

                def shares():
                    act.wait_ge(s["gap_done"], g + 1)
                    act.activation(share[:, 1], share[:, 0], ACT.Exp).then_inc(s["exp_done"], 1)

                def keep_gates():
                    act.wait_ge(s["gate_turned"], g + 1)
                    act.activation(gate_t[:, j], pt[0:E, :], ACT.Copy).then_inc(s["gate_kept"], 1)

                if routed:
                    return [keep, lambda: (relu(0), relu(1)), lambda: (relu(2), relu(3)), lambda: None, shares,
                            keep_gates]
                return [keep, lambda: None, shares, keep_gates]

            def back(g, j, half, e):
                if e == E:
                    return
                for f in range(FT):
                    if f == 0:
                        act.wait_ge(s["y_ready"], g * (E + 1) + e)if e or not isinstance(g, int) or g else None
                    act.wait_ge(s["h_ready"], g * E * FT + (e * FT + f + 1))
                    act.activation(hid[:, e % 2, f], pf[:, f % 2], ACT.Relu, bias=b1[:, e, f:f + 1])\
                       .then_inc(s["h_kept"], 1)

            act.wait_ge(s["w_loaded"], 16 * len(loads))
            if not routed:
                act.wait_ge(s["w_ready"], 1)
            run(act, front, back)

        @block.vector
        def _(dve):
            dve.sem_inc(s["x_used"], 2)
            dve.sem_inc(s["gated"], 1)
            dve.sem_inc(s["y_used"], 2)
            dve.sem_inc(stored[0], 16)
            dve.sem_inc(stored[1], 16)
            dve.wait_ge(s["w_loaded"], 16 * len(loads))
            if not routed:
                dve.wait_ge(s["w_bias"], 1)
                b1_all = b1[:, :, :].rearrange("p e f -> p (e f)")
                dve.tensor_tensor(b1_all, b1_all, pg[:, 0:E * FT], ALU.add)
                for e in range(E):
                    dve.tensor_scalar(w1[:, e, :], w1[:, e, :], ln_g[:, e:e + 1], None, ALU.mult)
                dve.drain().then_inc(s["w_ready"], 1)

            def front(g, j, half):
                def norm():
                    dve.wait_ge(x_loaded[j], half * 16 + 16)
                    ln_stats(dve, x_in[:, j], stats, mean_var)
                    dve.drain().then_inc(s["stats_done"], 1)
                    dve.wait_ge(s["rstd_done"], g * NLN + 1)
                    ln_apply(dve, xf[:, j], x_in[:, j], mean_var, rstd)
                    dve.drain()
                    if not routed:
                        ln_stats(dve, xf[:, j], stats, mean_var)
                        dve.drain().then_inc(s["stats_done"], 1)
                        dve.wait_ge(s["rstd_done"], g * NLN + 2)
                        dve.wait_ge(s["turned"], g + 1)
                        ln_apply(dve, z, xf[:, j], mean_var, rstd)
                        dve.drain()
                    dve.drain().then_inc(s["normed"], 1)

                def pick():
                    dve.wait_ge(s["scored"], g + 1)
                    now = pg[:, 0:T * E].rearrange("p (t e) -> p t e", t=T)
                    if routed:
                        dve.tensor_tensor(score[:, :, :], now, rb2[:, :, :], ALU.add)
                    else:
                        dve.tensor_copy(score[:, :, :], now)
                    dve.drain()
                    for t in range(T):
                        dve.max(top[:, t, :], score[:, t, :])
                    dve.drain()
                    for t in range(T):
                        dve.max_index(top_i[:, t, :], top[:, t, :], score[:, t, :])
                    if routed:
                        dve.tensor_tensor(share[:, 0], top[:, :, 1], top[:, :, 0], ALU.subtract)
                    else:
                        dve.tensor_scalar(share[:, 0], top[:, :, 0], -1.0, None, ALU.mult)
                    dve.drain().then_inc(s["gap_done"], 1)
                    dve.tensor_copy(top_f[:, :, :], top_i[:, :, :])
                    dve.drain()

                def gates():
                    dve.wait_ge(s["exp_done"], g + 1)
                    dve.tensor_scalar(share[:, 2], share[:, 1], 1.0, None, ALU.add)
                    dve.drain()
                    dve.reciprocal(share[:, 2], share[:, 2])
                    dve.drain()
                    if routed:
                        dve.tensor_tensor(share[:, 1], share[:, 1], share[:, 2], ALU.mult)
                        dve.drain()
                    for t in range(T):
                        dve.tensor_scalar(gate[:, j, t, :], iota[:, :], top_f[:, t, 0:1], share[:, 2, t:t + 1],
                                          ALU.is_equal, ALU.mult)
                        if routed:
                            dve.tensor_scalar(gate2[:, t, :], iota[:, :], top_f[:, t, 1:2], share[:, 1, t:t + 1],
                                              ALU.is_equal, ALU.mult)
                    dve.drain()
                    if routed:
                        dve.tensor_tensor(gate[:, j], gate[:, j], gate2[:, :, :], ALU.add)
                        dve.drain()
                    dve.drain().then_inc(s["gated"], 1)

                if routed:
                    return [norm, lambda: None, lambda: None, pick, gates]
                return [norm, pick, gates]

            def back(g, j, half, e):
                v = e
                dve.wait_ge(s["y_ready"], g * (E + 1) + (v + 2))
                y = py[:, (g_par(j) + v) % 2].rearrange("p (t d) -> p t d", t=T)
                if v == 0:
                    hold(dve, stored[j], half * 16 + 16, const)
                    dve.tensor_tensor(xo[:, j], y, x_in[:, j], ALU.add)
                    dve.drain().then_inc(s["x_used"], 1)
                    if not routed:
                        dve.tensor_tensor(xo[:, j], xo[:, j], xf[:, j], ALU.add)
                        dve.drain()
                    dve.sem_inc(s["y_used"], 1)
                else:
                    for t in range(T):
                        dve.scalar_tensor_tensor(xo[:, j, t], y[:, t], gate[:, j, t, v - 1:v], xo[:, j, t],
                                                 ALU.mult, ALU.add)
                    dve.drain().then_inc(s["y_used"], 1)
                if v == E:
                    dve.sem_inc(s["summed"], 1)

            run(dve, front, back)


def g_par(j):
    return (E + 1) * j % 2


def phase_cope(nc, w, x, out, const):
    HG = 4
    NG = AH // HG
    W = P + 1
    ONE = 1 << 17
    UX, UZ = 3 * NG, NG
    with Phase(nc, "at") as ph:
        wq, wk, wv, wo = (ph.sb(n, [D, D]) for n in ("wq", "wk", "wv", "wo"))
        cols = ph.sb("cols", [D, 4 + 2 * HG])
        bv = ph.sb("bv", [P, T, D])
        bo = ph.sb("bo", [P, T, D])
        pos = ph.sb("pos", [D, P])
        tri = ph.sb("tri", [P, P])
        offset = ph.sb("offset", [3, HG * P], BF16)
        ones = ph.sb("ones", [3, P], BF16)
        least = ph.sb("least", [P, P])
        x_in = ph.sb("x_in", [P, 2, T, D])
        xb = ph.sb("xb", [P, 2, T, D])
        xa = ph.sb("xa", [P, T, D])
        xat = ph.sb("xat", [D, GT])
        stats, mean_var, rstd = ph.sb("stats", [P, T, 6]), ph.sb("mean_var", [P, T, 2]), ph.sb("rstd", [P, T])
        qz = ph.sb("qz", [D, 2, HG, GT])
        kt = ph.sb("kt", [D, 2, GT])
        va = ph.sb("va", [P, 2, T, AH, AD + 1])
        th = ph.sb("th", [P, AH, P])
        vint = ph.sb("vint", [P, 2, AH, P], I32)
        sh = ph.sb("sh", [P, 2, AH, W], I16)
        bit = ph.sb("bit", [P, 7, AH, W], I16)
        tab = ph.sb("tab", [P, 2, AH, W])
        lg = ph.sb("lg", [P, 2, AH, P])
        step = ph.sb("step", [P, AH, P])
        at = ph.sb("at", [P, AH, P])
        mx = ph.sb("mx", [P, 2, AH])
        pr = ph.sb("pr", [P, 2, AH, P])
        prt = ph.sb("prt", [P, AH, P])
        rec = ph.sb("rec", [P, AH])
        o = ph.sb("o", [P, D])
        ot = ph.sb("ot", [D, P])
        xo = ph.sb("xo", [P, 2, T, D])
        pa, pv = ph.psum("pa", [P, 2, HG * P]), ph.psum("pv", [P, AH, P])
        pm, pz = ph.psum("pm", [P, GT]), ph.psum("pz", [P, GT])
        x_loaded = [ph.sem("x_loaded0"), ph.sem("x_loaded1")]
        stored = [ph.sem("stored0"), ph.sem("stored1")]
        s = ph.sems("w_loaded", "w_ready", "x_used", "xb_done", "stats_done", "rstd_done", "normed", "m_ready", "m_kept",
                    "v_added", "a_ready", "a_used", "tanh_done", "kept", "rounded", "v_ready", "v_read", "routed",
                    "step_done", "upper_done", "sum_done", "at_done", "max_done", "exp_done", "o_ready", "o_done",
                    "ot_ready", "ot_kept", "wo_ready", "added")
        src, dst = column_groups(x), column_groups(out)
        block = ph.block()
        loads = [(wq[:, :], w["wq"]), (wk[:, :], w["wk"]), (wv[:, :], w["wv"]), (wo[:, :], w["wo"]),
                 (cols[:, 0:1], w["bq"]), (cols[:, 1:2], w["bk"]), (cols[:, 4:4 + HG], w["head_mask"]),
                 (bv[:, :, :], w["bv"]), (bo[:, :, :], w["bo"]), (pos[:, :], w["pos"]), (tri[:, :], w["tri"]),
                 (offset[:, :], w["offset"]), (ones[:, :], w["ones"]), (least[:, :], w["least"])]
        SCALE = float(AD) ** -0.5

        def run(engine, fill, main, front):
            for k in range(3):
                front(0, 0, 0, k)
            fill(0, 0, 0, 0)

            def group(g, gs, own, half, first=False, last=False):
                for t in range(T):
                    nxt = (g, t + 1, gs, 0) if t < T - 1 else (g + 1, 0, 1 - gs, 0)
                    f = None if last and t == T - 1 else (lambda n=nxt: fill(*n))
                    prev = (g, t - 1, gs, own) if t else (g - 1, T - 1, 1 - gs, None)
                    main(g, t, gs, f, None if first and t == 0 else prev)
                    if t < 3 and not last:
                        front(g + 1, 1 - gs, half, t)

            group(0, 0, 0, 0, first=True)
            with engine.Fori(0, G // 2 - 1) as i:
                group(i * 2 + 1, 1, i, i + 1)
                group(i * 2 + 2, 0, i + 1, i + 1)
            group(G - 1, 1, G // 2 - 1, None, last=True)
            main(G, 0, 0, None, (G - 1, T - 1, 1, None), only_drain=True)

        def fills_before(g, t):
            c = g * (T * (UX + UZ)) + t * (UX + UZ)
            return 0 if isinstance(g, int) and g == 0 and t == 0 else \
                UX if isinstance(g, int) and g == 0 and t == 1 else c - 2 * UZ

        def drains_before(g, t):
            if isinstance(g, int) and g == G - 1 and t >= T - 2:
                return A_COLS * UX + (A_COLS - (2 if t == T - 2 else 1)) * UZ
            return g * (T * (UX + UZ)) + (t * (UX + UZ) + 3 * UX)

        @block.sync
        def _(sp):
            def load(g, j):
                sp.wait_ge(s["x_used"], g + 1)
                sp.wait_ge(s["xb_done"], g + 1)
                sp.dma_start(x_in[:, j], src[g]).then_inc(x_loaded[j], 16)

            load(0, 0)
            for to, frm in loads:
                sp.dma_start(to, frm).then_inc(s["w_loaded"], 16)
            load(1, 1)

            def store(g, j):
                sp.wait_ge(s["added"], g * T + (T + 1))
                sp.dma_start(dst[g], xo[:, j]).then_inc(stored[j], 16)

            with sp.Fori(0, G // 2 - 1) as i:
                for j in range(2):
                    load(i * 2 + (j + 2), j)
                    store(i * 2 + j, j)
            store(G - 2, 0)
            store(G - 1, 1)
            for j in range(2):
                sp.wait_ge(stored[j], 16 * (G // 2 + 1))

        @block.gpsimd
        def _(pool):
            pool.sem_inc(s["xb_done"], 2)
            pool.memset(va[:, :, :, :, :].rearrange("p j t h d -> p (j t h) d")[:, :, AD:AD + 1], 1.0)
            pool.drain()
            pool.wait_ge(s["w_loaded"], 16 * len(loads))

            def front(g, gs, half, k):
                if k:
                    return
                pool.wait_ge(s["stats_done"], g + 1)
                ln_rstd(pool, mean_var[:, :, :], const["eps5"], const["minus_half"], rstd[:, :]).then_inc(s["rstd_done"], 1)
                pool.wait_ge(s["added"], g * T + (1 - T)) if not isinstance(g, int) or g > 1 else None
                pool.tensor_tensor(xb[:, gs], x_in[:, gs], bo[:, :, :], ALU.add).then_inc(s["xb_done"], 1)

            def main(g, t, gs, fill, prev, only_drain=False):
                if only_drain:
                    return
                c = t % 2
                pool.wait_ge(s["routed"], g * T + (t + 1))
                pool.tensor_tensor(step[:, :, :], tab[:, c, :, 0:P], tab[:, c, :, 1:W], ALU.subtract)\
                    .then_inc(s["step_done"], 1)
                pool.wait_ge(s["upper_done"], g * T + (t + 1))
                pool.tensor_tensor(lg[:, c], lg[:, c], tab[:, c, :, 0:P], ALU.add).then_inc(s["sum_done"], 1)

            run(pool, lambda *a: None, main, front)

        @block.tensor
        def _(pe):
            pe.sem_inc(s["o_ready"], 1)
            pe.wait_ge(s["w_loaded"], 16 * len(loads))

            def front(g, gs, half, k):
                if k == 0:
                    pe.wait_ge(s["v_added"], g + 1)
                    pe.wait_ge(s["normed"], g + 1)
                    for t in range(T):
                        last = pe.transpose(pm[:, t * P:(t + 1) * P], xa[:, t, :], const["ident"])
                    last.then_inc(s["m_ready"], 1)
                if k == 1:
                    pe.wait_ge(s["m_kept"], g * 3 + 1)
                    pe.matmul(pm[:, :], wq[:, :], xat[:, :], start=True, stop=True).then_inc(s["m_ready"], 1)
                if k == 2:
                    pe.wait_ge(s["m_kept"], g * 3 + 2)
                    pe.matmul(pm[:, :], wk[:, :], xat[:, :], start=True, stop=True).then_inc(s["m_ready"], 1)
                    pe.wait_ge(s["m_kept"], g * 3 + 3)
                    for t in range(T):
                        tok = slice(t * P, (t + 1) * P)
                        last = pe.matmul(pm[:, tok], xat[:, tok], wv[:, :], start=True, stop=True)
                    last.then_inc(s["m_ready"], 1)

            def fill(g, t, gs, _):
                col = slice(t * P, (t + 1) * P)
                base = fills_before(g, t)
                n = 0
                for which in range(3):
                    for hg in range(NG):
                        rows = slice(hg * 32, hg * 32 + 32)
                        pe.wait_ge(s["a_used"], base + (n + 1))
                        if n == 0:
                            pe.wait_ge(s["m_kept"], g * 3 + 3)
                        bank = pa[:, n % 2]
                        if which == 0:
                            last = pe.matmul(bank.rearrange("p (h q) -> p h q", h=HG), kt[rows, gs, col],
                                             qz[rows, gs, :, col], start=True, stop=True)
                        else:
                            for h in range(HG):
                                last = pe.matmul(bank[:, h * P:(h + 1) * P], qz[rows, gs, h, col],
                                                 pos[rows, :] if which == 1 else kt[rows, gs, col],
                                                 start=True, stop=True)
                        last.then_inc(s["a_ready"], 1)
                        n += 1

            def positions(g, t):
                pe.wait_ge(s["v_read"], g * T + (t + 1))
                pe.wait_ge(s["rounded"], g * T + (t + 1))
                for hg in range(NG):
                    bank = pv[:, hg * HG:(hg + 1) * HG, :]
                    pe.matmul(bank, ones[:, :], offset[:, :].rearrange("k (h t) -> k h t", h=HG), start=True, stop=False)
                    for h in range(HG):
                        last = pe.matmul(pv[:, hg * HG + h, :], th[:, hg * HG + h, :], tri[:, :], start=False,
                                         stop=(h == HG - 1))
                last.then_inc(s["v_ready"], 1)

            def main(g, t, gs, do_fill, prev, only_drain=False):
                if do_fill:
                    do_fill()
                if prev:
                    pg_, pt_, pgs, phalf = prev
                    c = pt_ % 2
                    pe.wait_ge(s["exp_done"], pg_ * T + (pt_ + 1))
                    for hg in range(NG):
                        pe.wait_ge(s["a_used"], drains_before(pg_, pt_) + (hg + 1))
                        for h in range(HG):
                            last = pe.transpose(pa[:, hg % 2, h * P:(h + 1) * P], pr[:, c, hg * HG + h, :],
                                                const["ident"])
                        last.then_inc(s["a_ready"], 1)
                    pe.wait_ge(s["a_used"], drains_before(pg_, pt_) + (NG + 2))
                    pe.wait_ge(s["added"], pg_ * T + (pt_ + 1))
                    pe.wait_ge(s["v_added"], pg_ + 2)
                    for h in range(AH):
                        last = pe.matmul(pz[:, h * (AD + 1):(h + 1) * (AD + 1)], prt[:, h, :], va[:, pgs, pt_, h, :],
                                         start=True, stop=True)
                    last.then_inc(s["o_ready"], 1)
                if do_fill:
                    positions(*((g, t + 1) if t < T - 1 else (g + 1, 0)))
                if prev:
                    pe.wait_ge(s["o_done"], pg_ * T + (pt_ + 1))
                    pe.transpose(pz[:, 0:P], o[:, :], const["ident"]).then_inc(s["ot_ready"], 1)
                    pe.wait_ge(s["ot_kept"], pg_ * T + (pt_ + 1))
                    pe.matmul(pz[:, P:2 * P], ot[:, :], wo[:, :], start=True, stop=True).then_inc(s["wo_ready"], 1)

            def first_fill(g, t, gs, z):
                fill(g, t, gs, z)
                if isinstance(g, int) and g == 0 and t == 0:
                    positions(g, t)

            run(pe, first_fill, main, front)

        @block.scalar
        def _(act):
            act.sem_inc(s["a_used"], 2)
            act.wait_ge(s["w_loaded"], 16 * len(loads))
            act.wait_ge(s["w_ready"], 1)

            def front(g, gs, half, k):
                act.wait_ge(s["m_ready"], g * 4 + (k + 1))
                if k == 0:
                    act.activation(xat[:, :], pm[:, :], ACT.Copy).then_inc(s["m_kept"], 1)
                if k == 1:
                    for h in range(HG):
                        last = act.activation(qz[:, gs, h, :], pm[:, :], ACT.Identity, scale=cols[:, 4 + h:5 + h],
                                              bias=cols[:, 4 + HG + h:5 + HG + h])
                    last.then_inc(s["m_kept"], 1)
                if k == 2:
                    act.activation(kt[:, gs], pm[:, :], ACT.Identity, scale=SCALE, bias=cols[:, 2:3])\
                       .then_inc(s["m_kept"], 1)

            def fill(g, t, gs, _):
                c = t % 2
                base = fills_before(g, t)
                act.wait_ge(s["v_ready"], g * T + t) if not isinstance(g, int) or g or t else None
                for n in range(UX):
                    hg = n % NG
                    heads = slice(hg * HG, (hg + 1) * HG)
                    if n == NG:
                        act.wait_ge(s["at_done"], g * T + (t + 1))
                    act.wait_ge(s["a_ready"], base + (n + 1))
                    bank = pa[:, n % 2].rearrange("p (h q) -> p h q", h=HG)
                    if n < NG:
                        last = act.activation(th[:, heads, :], bank, ACT.Tanh, scale=0.5)
                    elif n < 2 * NG:
                        last = act.activation(tab[:, c, heads, 1:W], bank, ACT.Copy)
                    else:
                        last = act.activation(lg[:, c, heads, :], bank, ACT.Copy)
                    last.then_inc(s["a_used"], 1)
                    if n == NG - 1:
                        act.drain().then_inc(s["tanh_done"], 1)
                act.drain().then_inc(s["kept"], 1)

            def main(g, t, gs, do_fill, prev, only_drain=False):
                if do_fill:
                    do_fill()
                if prev:
                    pg_, pt_, pgs, phalf = prev
                    act.wait_ge(s["o_ready"], pg_ * T + (pt_ + 1))
                    for hg in range(NG):
                        act.wait_ge(s["a_ready"], drains_before(pg_, pt_) + (hg + 1))
                        act.activation(prt[:, hg * HG:(hg + 1) * HG, :],
                                       pa[:, hg % 2].rearrange("p (h q) -> p h q", h=HG), ACT.Copy).then_inc(s["a_used"], 1)
                    act.wait_ge(s["ot_ready"], pg_ * T + (pt_ + 1))
                    act.activation(ot[:, :], pz[:, 0:P], ACT.Copy).then_inc(s["ot_kept"], 1)
                if only_drain:
                    return
                c = t % 2
                act.wait_ge(s["max_done"], g * T + (t + 1))
                for h in range(AH):
                    last = act.activation(pr[:, c, h, :], at[:, h, :], ACT.Exp, bias=mx[:, c, h:h + 1])
                last.then_inc(s["exp_done"], 1)

            run(act, fill, main, front)

        @block.vector
        def _(dve):
            dve.sem_inc(s["x_used"], 2)
            dve.sem_inc(s["v_added"], 1)
            dve.sem_inc(s["v_read"], 1)
            dve.sem_inc(s["at_done"], 2)
            dve.sem_inc(s["added"], 1)
            dve.sem_inc(stored[0], 16)
            dve.sem_inc(stored[1], 16)
            dve.memset(tab[:, :, :, 0:1].rearrange("p c h o -> p (c h) o"), 0.0)
            dve.wait_ge(s["w_loaded"], 16 * len(loads))
            dve.tensor_scalar(cols[:, 2:3], cols[:, 1:2], SCALE, None, ALU.mult)
            dve.tensor_scalar(cols[:, 4 + HG:4 + 2 * HG], cols[:, 4:4 + HG], cols[:, 0:1], None, ALU.mult)
            dve.drain().then_inc(s["w_ready"], 1)

            def front(g, gs, half, k):
                if k == 0:
                    dve.wait_ge(x_loaded[gs], half * 16 + 16)
                    ln_stats(dve, x_in[:, gs], stats, mean_var)
                    dve.drain().then_inc(s["stats_done"], 1)
                    dve.wait_ge(s["rstd_done"], g + 1)
                    ln_apply(dve, xa, x_in[:, gs], mean_var, rstd)
                    dve.drain().then_inc(s["normed"], 1)
                    dve.sem_inc(s["x_used"], 1)
                if k == 2:
                    dve.wait_ge(s["m_ready"], g * 4 + 4)
                    dve.tensor_tensor(va[:, gs].rearrange("p t h d -> p (t h) d")[:, :, 0:AD],
                                      pm[:, :].rearrange("p (k d) -> p k d", d=AD),
                                      bv[:, :, :].rearrange("p t (h d) -> p (t h) d", h=AH), ALU.add)
                    dve.drain().then_inc(s["v_added"], 1)

            def round_gates(g, t):
                dve.wait_ge(s["tanh_done"], g * T + (t + 1))
                dve.tensor_scalar(th[:, :, :], th[:, :, :], 129.0, -129.0, ALU.add, ALU.add)
                dve.drain().then_inc(s["rounded"], 1)

            def shifts(g, t):
                c = t % 2
                dve.wait_ge(s["v_ready"], g * T + (t + 1))
                dve.scalar_tensor_tensor(vint[:, c], pv[:, :, :], float(ONE),
                                         least[:, :].rearrange("p (o t) -> p o t", o=1).broadcast_to((P, AH, P)),
                                         ALU.mult, ALU.max)
                dve.drain().then_inc(s["v_read"], 1)
                upper = vint[:, c].bitcast(I16).rearrange("p h (t w) -> p h t w", w=2)[:, :, :, 1]
                dve.tensor_copy(sh[:, c, :, 1:W], upper)
                dve.drain()
                dve.tensor_copy(sh[:, c, :, 0:1], sh[:, c, :, 1:2])
                dve.drain()

            def fill(g, t, gs, _):
                if isinstance(g, int) and g == 0 and t == 0:
                    round_gates(g, t)
                    shifts(g, t)

            def main(g, t, gs, do_fill, prev, only_drain=False):
                if not only_drain:
                    c = t % 2
                    for k in range(7):
                        dve.tensor_scalar(bit[:, k], sh[:, c], 2 << k, None, ALU.bitwise_and)
                    dve.tensor_scalar(vint[:, c], vint[:, c], ONE - 1, None, ALU.bitwise_and)
                    dve.drain()
                    hold(dve, s["kept"], g * T + (t + 1), const)
                    for k in range(6, 0, -1):
                        n = W - (1 << k)
                        dve.copy_predicated(tab[:, c, :, 0:n], bit[:, k, :, 0:n], tab[:, c, :, 1 << k:W])
                        dve.drain()
                    dve.sem_inc(s["routed"], 1)
                    nxt = (g, t + 1) if t < T - 1 else (g + 1, 0)
                    if do_fill:
                        round_gates(*nxt)
                if prev:
                    pg_, pt_, pgs, phalf = prev
                    dve.wait_ge(s["o_ready"], pg_ * T + (pt_ + 2))
                    got = pz[:, 0:AH * (AD + 1)].rearrange("p (h d) -> p h d", h=AH)
                    dve.reciprocal(rec[:, :], got[:, :, AD])
                    dve.drain()
                    dve.tensor_tensor(o[:, :].rearrange("p (h d) -> p h d", h=AH), got[:, :, 0:AD],
                                      rec[:, :].rearrange("p (h o) -> p h o", o=1).broadcast_to((P, AH, AD)), ALU.mult)
                    dve.drain().then_inc(s["o_done"], 1)
                if not only_drain:
                    if do_fill:
                        shifts(*nxt)
                    hold(dve, s["step_done"], g * T + (t + 1), const)
                    dve.copy_predicated(tab[:, c, :, 0:P], bit[:, 0, :, 1:W], tab[:, c, :, 1:W])
                    dve.drain().then_inc(s["upper_done"], 1)
                    dve.copy_predicated(step[:, :, 0:P - 1], bit[:, 0, :, 1:P], step[:, :, 1:P])
                    dve.drain()
                    dve.scalar_tensor_tensor(step[:, :, :], vint[:, c], 1.0, step[:, :, :], ALU.add, ALU.mult)
                if prev:
                    dve.wait_ge(s["wo_ready"], pg_ * T + (pt_ + 1))
                    if pt_ == 0:
                        hold(dve, stored[pgs], phalf * 16 + 16, const)
                    dve.tensor_tensor(xo[:, pgs, pt_, :], pz[:, P:2 * P], xb[:, pgs, pt_, :], ALU.add)
                    dve.drain().then_inc(s["added"], 1)
                if not only_drain:
                    dve.drain()
                    dve.wait_ge(s["exp_done"], g * T + t) if not isinstance(g, int) or g or t else None
                    dve.wait_ge(s["sum_done"], g * T + (t + 1))
                    dve.scalar_tensor_tensor(at[:, :, :], step[:, :, :], -1.0 / ONE, lg[:, c], ALU.mult, ALU.add)
                    dve.drain().then_inc(s["at_done"], 1)
                    dve.tensor_reduce(mx[:, c], at[:, :, :], AX.X, ALU.max, negate=True)
                    dve.drain().then_inc(s["max_done"], 1)

            run(dve, fill, main, front)


def build(nc, w, x, ctx, out):
    x2, x3, x4, x5 = (nc.dram_tensor(n, (A, S, D), F32, kind="Internal").ap() for n in ("x2", "x3", "x4", "x5"))
    with Phase(nc, "all") as keep:
        ident = keep.sb("ident", [P, P])
        small = keep.sb("small", [P, 3 * T])
        const = {"ident": ident[:, :], "minus_half": small[:, 0:T], "eps5": small[:, T:2 * T],
                 "eps6": small[:, 2 * T:3 * T]}
        ready = keep.sem("const_ready")
        const["passed"] = keep.sem("passed")
        with nc.Block() as block:
            @block.sync
            def _(sp):
                sp.dma_start(ident[:, :], w["ident"]).then_inc(ready, 16)
                sp.wait_ge(ready, 16)

            @block.vector
            def _(dve):
                dve.memset(const["minus_half"], -0.5)
                dve.memset(const["eps5"], 1e-5)
                dve.memset(const["eps6"], 1e-6)
                dve.drain()
        with Phase(nc, "L0") as l0:
            xn_t = l0.sb("xn_t", [D, TOK])
            phase_norm_in(nc, w, x, xn_t, const)
            with Phase(nc, "sk") as sk:
                delta = sk.sb("delta", [D, TOK])
                split = sk.sb("split", [6 * N, TOK], BF16)
                guard = {k: sk.sb("g_" + k, [D, N]) for k in ("a_log", "a", "inv", "minus_inv", "near0", "far")}
                guard["bc_pick"] = sk.sb("bc_pick", [6 * N, 2 * N * P], BF16)
                with Phase(nc, "tmp") as tm:
                    tmp = tm.sb("tmp", [P, TOK])
                    phase_select(nc, w, xn_t, const, delta, split, guard, tmp)
                phase_scan(nc, w, xn_t, const, delta, split, guard)
            phase_mlstm(nc, mlstm_weights(w, "l0"), "m0", x, ctx, x2, const, 1e-6, xn_t)
        phase_experts(nc, expert_weights(w, "l0"), "f0", x2, x3, const, True)
        phase_cope(nc, {k[3:]: v for k, v in w.items() if k.startswith("at_")}, x3, x4, const)
        phase_mlstm(nc, mlstm_weights(w, "l1"), "m1", x4, ctx, x5, const, 1e-5)
        phase_experts(nc, expert_weights(w, "l1"), "f1", x5, out, const, False)


def expert_weights(w, layer):
    return {k[len(layer) + 2:]: v for k, v in w.items() if k.startswith(layer + "f_")} | {"iota": w["iota"]}


def mlstm_weights(w, layer):
    own = {k: w[f"{layer}_{k}"] for k in ("gate_w", "gate_b", "norm_w")}
    return own | {k: w[k] for k in ("seq_tri", "mask", "ident_b", "minus_pick")}


def host_inputs(inputs):
    bf16 = np.dtype("bfloat16")
    f = {k: np.ascontiguousarray(v) for k, v in inputs.items()}
    col = lambda a: np.ascontiguousarray(a.reshape(-1, 1))
    tr = lambda a: np.ascontiguousarray(np.swapaxes(a, -1, -2))
    bc = np.concatenate([f["L0_attn_B_W"], f["L0_attn_C_W"]])
    bcb = np.concatenate([f["L0_attn_B_b"], f["L0_attn_C_b"]])
    pick = np.zeros((6 * N, 2 * N, P), bf16)
    for k in range(3):
        for n in range(2 * N):
            pick[k * 2 * N + n, n, :] = 1
    w = {
        "ident": np.eye(P, dtype=np.float32),
        "wi_t": tr(f["L0_attn_Wi_W"]), "wr_t": tr(f["L0_attn_Wr_W"]), "sel_t": tr(f["L0_attn_sel_W"]),
        "h0": col(f["L0_attn_h0"]), "tau": col(f["L0_attn_tau"]), "wi_b": col(f["L0_attn_Wi_b"]),
        "sel_b": col(f["L0_attn_sel_b"]), "delta_b": col(f["L0_attn_delta_b"]),
        "dt_bias": col(f["L0_attn_dt_bias"]), "delta_wt": tr(f["L0_attn_delta_W"]),
        "bc_wt": np.concatenate([tr(bc)] * 3, axis=1), "bc_bias": col(np.concatenate([bcb] * 3)),
        "a_log": f["L0_attn_A_log"], "bc_pick": pick.reshape(6 * N, 2 * N * P),
    }
    rows = lambda a, n: np.ascontiguousarray(np.broadcast_to(a.reshape(-1), (n, a.size)))
    for layer, pre, ig, fg, norm in (("l0", "L0_xattn_", "ig_", "fg_", "outnorm_weight"),
                                     ("l1", "L1_xattn_", "igate_", "fgate_", "outnorm_scale")):
        kern = np.concatenate([f[pre + ig + "kernel"], f[pre + fg + "kernel"]], axis=1)
        bias = np.concatenate([f[pre + ig + "bias"], f[pre + fg + "bias"]])
        w[layer + "_gate_w"] = np.ascontiguousarray(kern.reshape(3, D, 2 * NH).transpose(1, 0, 2))
        w[layer + "_gate_b"] = rows(np.tile(bias, T), P).reshape(P, T, 2 * NH)
        w[layer + "_norm_w"] = rows(f[pre + norm], P)
    by_f = lambda a: np.ascontiguousarray(a.reshape(*a.shape[:-1], FT, P).transpose(-1, *range(a.ndim)))
    w["iota"] = rows(np.arange(E, dtype=np.float32), P)
    w1, w2 = f["L0_ffn_W1"], f["L0_ffn_W2"]
    w["l0f_w1"] = np.ascontiguousarray(w1.transpose(1, 0, 2))
    w["l0f_w2"] = np.ascontiguousarray(w2.reshape(E, FT, P, D).transpose(2, 0, 1, 3))
    w["l0f_b1"], w["l0f_b2"] = by_f(f["L0_ffn_b1"]), f["L0_ffn_b2"]
    w["l0f_rw1"], w["l0f_rb1"] = f["L0_ffn_rw1"], by_f(f["L0_ffn_rb1"])
    w["l0f_rw2"] = np.ascontiguousarray(f["L0_ffn_rw2"].reshape(FT, P, E).transpose(1, 0, 2))
    w["l0f_rb2"] = rows(np.tile(f["L0_ffn_rb2"], T), P).reshape(P, T, E)
    w1, w2 = tr(f["L1_ffn_w1"]), tr(f["L1_ffn_w2"])
    w["l1f_w1"] = np.ascontiguousarray(w1.transpose(1, 0, 2))
    w["l1f_w2"] = np.ascontiguousarray(w2.reshape(E, FT, P, D).transpose(2, 0, 1, 3))
    w["l1f_b1"], w["l1f_b2"] = by_f(f["L1_ffn_b1"]), f["L1_ffn_b2"]
    w["l1f_cent"], w["l1f_ln_g"], w["l1f_ln_b"] = (tr(f["L1_ffn_" + k]) for k in ("centroids", "ln_g", "ln_b"))
    for k in ("q", "k", "v", "o"):
        w["at_w" + k] = f["L1_attn_W" + k]
    w["at_bq"], w["at_bk"] = col(f["L1_attn_bq"]), col(f["L1_attn_bk"])
    w["at_bv"], w["at_bo"] = (rows(np.tile(f["L1_attn_b" + k], T), P).reshape(P, T, D) for k in "vo")
    w["at_head_mask"] = (np.arange(D)[:, None] % 32 // AD == np.arange(4)[None, :]).astype(np.float32)
    pos = np.zeros((AD, P), np.float32)
    npos = f["L1_attn_pos_emb"].shape[-1]
    pos[:, P - npos:] = f["L1_attn_pos_emb"][0][:, ::-1]
    w["at_pos"] = np.tile(pos, (AH, 1))
    t, s_ = np.arange(P)[:, None], np.arange(P)[None, :]
    w["at_tri"] = np.where(t >= s_, -0.5, 0.0).astype(np.float32)
    off = (P - np.arange(P)) / 2 - 2.0 ** -17
    parts = []
    for _ in range(3):
        parts.append(off.astype(bf16))
        off = off - parts[-1].astype(np.float64)
    w["at_offset"] = np.tile(np.stack(parts), (1, 4))
    w["at_ones"] = np.ones((3, P), bf16)
    w["at_least"] = rows((np.maximum(0, P - 1 - (npos - 2) - np.arange(P)) * 2.0 ** 17).astype(np.float32), P)
    t, s_ = np.arange(P)[:, None], np.arange(P)[None, :]
    seen = (t // S == s_ // S) & (t <= s_)
    w["seq_tri"] = seen.astype(np.float32)
    w["mask"] = np.tile(np.where(seen, 0.0, -1e30), (1, T)).astype(bf16)
    w["ident_b"] = np.eye(P).astype(bf16)
    w["minus_pick"] = -np.repeat(np.eye(T * NH, dtype=np.float32), P, axis=1)
    return {"x": f["x"], "ctx": f["ctx_1024"]}, w


def kernel(**inputs):
    import concourse.bacc as bacc
    from concourse.bass_utils import run_bass_kernel_spmd

    nc = bacc.Bacc("TRN2", target_bir_lowering=False, num_devices=1)
    data, w = host_inputs(inputs)
    arrays = {f"in_{k}": v for k, v in {**data, **w}.items()}
    aps = {k: nc.dram_tensor(k, v.shape, mybir.dt.from_np(v.dtype), kind="ExternalInput").ap() for k, v in arrays.items()}
    out = nc.dram_tensor("out_0", (A, S, D), F32, kind="ExternalOutput").ap()
    build(nc, {k: aps[f"in_{k}"] for k in w}, aps["in_x"], aps["in_ctx"], out)
    r = run_bass_kernel_spmd(nc, [arrays], core_ids=[0])
    return r.results[0]["out_0"]
```

```python
from contextlib import ExitStack

import numpy as np
import concourse.bass as bass
from concourse import mybir

ALU = mybir.AluOpType
ACT = mybir.ActivationFunctionType
AX = mybir.AxisListType
F32 = mybir.dt.float32
BF16 = mybir.dt.bfloat16
I32 = mybir.dt.int32
F32R = mybir.dt.float32r
I16 = mybir.dt.int16
U32 = mybir.dt.uint32

P = 128
A, S, D = 128, 64, 128
TOK = A * S
T = 4
GT = T * P
G = TOK // GT
N = 16
NH = 4
DH = D // NH
E, F = 8, 512
FT = F // P
AH, AD = 16, 8
A_COLS = S


class Phase:

    def __init__(self, nc, tag):
        self.nc, self.tag, self.stack, self.taken = nc, tag, ExitStack(), []

    def __enter__(self):
        return self

    def __exit__(self, *what):
        self.stack.close()
        if self.taken and what[0] is None:
            self.nc.clear_and_free_semaphores(self.taken)
            self.nc.all_engine_barrier()
        return False

    def sb(self, name, shape, dtype=F32):
        return self.stack.enter_context(self.nc.sbuf_tensor(f"{self.tag}_{name}", shape, dtype))

    def psum(self, name, shape):
        return self.stack.enter_context(self.nc.psum_tensor(f"{self.tag}_{name}", shape, F32))

    def sem(self, name):
        self.taken.append(self.nc.alloc_semaphore(f"{self.tag}_{name}"))
        return self.taken[-1]

    def sems(self, *names):
        return {n: self.sem(n) for n in names}

    def block(self):
        return self.stack.enter_context(self.nc.Block())


def hold(engine, sem, value, const):
    engine.wait_ge(sem, value)
    engine.sem_inc(const["passed"], 1)


def ln_stats(dve, x, stats, mean_var):
    for t in range(T):
        dve.bn_stats(stats[:, t, :], x[:, t, :])
    dve.drain()
    for t in range(T):
        last = dve.bn_aggr(mean_var[:, t, :], stats[:, t, :])
    return last


def ln_rstd(pool, mean_var, eps, minus_half, rstd):
    pool.tensor_tensor(rstd, mean_var[:, :, 1], eps, ALU.add)
    pool.drain()
    return pool.tensor_tensor(rstd, rstd, minus_half, ALU.pow)


def ln_apply(dve, out, x, mean_var, rstd):
    for t in range(T):
        last = dve.tensor_scalar(out[:, t, :], x[:, t, :], mean_var[:, t, 0:1], rstd[:, t:t + 1],
                                 ALU.subtract, ALU.mult)
    return last


def split_12(dve, high, low, x):
    dve.tensor_copy(high.bitcast(F32R), x)
    dve.drain()
    return dve.tensor_tensor(low.bitcast(F32R), x, high, ALU.subtract)


def split_product(pe, out, high, low, xh, xl):
    pe.matmul(out, low.bitcast(F32R), xh.bitcast(F32R), start=True, stop=False)
    pe.matmul(out, high.bitcast(F32R), xl.bitcast(F32R), start=False, stop=False)
    return pe.matmul(out, high.bitcast(F32R), xh.bitcast(F32R), start=False, stop=True)


def token_groups(x):
    return x.rearrange("a s d -> (a s) d").rearrange("(g t p) d -> g p t d", p=P, t=T)


def phase_norm_in(nc, w, x, xn_t, const):
    with Phase(nc, "ni") as ph:
        x_in = ph.sb("x_in", [P, 2, T, D])
        xn = ph.sb("xn", [P, 2, T, D])
        stats = ph.sb("stats", [P, 2, T, 6])
        mean_var = ph.sb("mean_var", [P, 2, T, 2])
        rstd = ph.sb("rstd", [P, 2, T])
        tr = ph.psum("tr", [P, 2, GT])
        x_loaded = [ph.sem("x_loaded0"), ph.sem("x_loaded1")]
        x_free, stats_done, rstd_done = ph.sem("x_free"), ph.sem("stats_done"), ph.sem("rstd_done")
        normed, turned, kept = ph.sem("normed"), ph.sem("turned"), ph.sem("kept")
        src = token_groups(x)
        block = ph.block()

        @block.sync
        def _(sp):
            with sp.Fori(0, G // 2) as i:
                for j in range(2):
                    sp.wait_ge(x_free, i * 2 + (j + 1))
                    sp.dma_start(x_in[:, j], src[i * 2 + j]).then_inc(x_loaded[j], 16)

        @block.vector
        def _(dve):
            dve.sem_inc(x_free, 2)
            with dve.Fori(0, G // 2) as i:
                for j in range(2):
                    dve.wait_ge(x_loaded[j], i * 16 + 16)
                    ln_stats(dve, x_in[:, j], stats[:, j], mean_var[:, j]).then_inc(stats_done, 1)
                    dve.wait_ge(turned, i * 2 + (j + 1))
                    dve.wait_ge(rstd_done, i * 2 + (j + 1))
                    ln_apply(dve, xn[:, j], x_in[:, j], mean_var[:, j], rstd[:, j])
                    dve.drain().then_inc(normed, 1)
                    dve.sem_inc(x_free, 1)

        @block.gpsimd
        def _(pool):
            with pool.Fori(0, G // 2) as i:
                for j in range(2):
                    pool.wait_ge(stats_done, i * 2 + (j + 1))
                    ln_rstd(pool, mean_var[:, j], const["eps5"], const["minus_half"],
                            rstd[:, j]).then_inc(rstd_done, 1)

        @block.tensor
        def _(pe):
            pe.sem_inc(turned, 2)
            with pe.Fori(0, G // 2) as i:
                for j in range(2):
                    pe.wait_ge(normed, i * 2 + (j + 1))
                    pe.wait_ge(kept, i * 2 + (j + 1))
                    for t in range(T):
                        last = pe.transpose(tr[:, j, t * P:(t + 1) * P], xn[:, j, t, :], const["ident"])
                    last.then_inc(turned, 1)

        @block.scalar
        def _(act):
            act.sem_inc(kept, 2)
            with act.Fori(0, G // 2) as i:
                for j in range(2):
                    hold(act, turned, i * 2 + (j + 3), const)
                    act.activation(xn_t[:, bass.ds((i * 2 + j) * GT, GT)], tr[:, j, :], ACT.Copy).then_inc(kept, 1)


def phase_select(nc, w, xn_t, const, delta, split, guard, tmp):
    with Phase(nc, "se") as ph:
        wi_t = ph.sb("wi_t", [D, N])
        wr_t = ph.sb("wr_t", [N, N])
        sel_t = ph.sb("sel_t", [N, D])
        cols = ph.sb("cols", [N, 8])
        h0, tau, wi_b, c1, c2, th_bias = (cols[:, k:k + 1] for k in range(6))
        dcols = ph.sb("dcols", [D, 4])
        means = ph.sb("means", [D, A])
        th = ph.sb("th", [N, A])
        sel = ph.sb("sel", [D, A])
        delta_wt = ph.sb("delta_wt", [D, D])
        bc_wt = ph.sb("bc_wt", [D, 3 * 2 * N])
        bc_bias = ph.sb("bc_bias", [3 * 2 * N, 1])
        R = 3 * 2 * N
        full = ph.sb("full", [R, 2, GT])
        part = ph.sb("part", [R, 2, GT], BF16)
        pz = ph.psum("pz", [P, 2, GT])
        pbc = ph.psum("pbc", [R, 2, GT])
        p_rec, p_sig, p_sel = (ph.psum(n, [P, 512]) for n in ("p_rec", "p_sig", "p_sel"))
        loaded, summed, psig, thd, newh = (ph.sem(n) for n in ("loaded", "summed", "psig", "thd", "newh"))
        col_ready, psel, seld, gated = (ph.sem(n) for n in ("col_ready", "psel", "seld", "gated"))
        z_ready, z_kept, bc_ready, bc_kept = (ph.sem(n) for n in ("z_ready", "z_kept", "bc_ready", "bc_kept"))
        logs = ph.sem("logs")
        rec_ready = ph.sem("rec_ready")
        quarters = [slice(q * TOK // 4, (q + 1) * TOK // 4) for q in range(4)]
        block = ph.block()
        n_loads = 14

        @block.sync
        def _(sp):
            for dst, src in ((wi_t[:, :], w["wi_t"]), (wr_t[:, :], w["wr_t"]), (sel_t[:, :], w["sel_t"]),
                             (h0, w["h0"]), (tau, w["tau"]), (wi_b, w["wi_b"]),
                             (dcols[:, 0:1], w["sel_b"]), (dcols[:, 1:2], w["delta_b"]),
                             (dcols[:, 2:3], w["dt_bias"]), (delta_wt[:, :], w["delta_wt"]),
                             (bc_wt[:, :], w["bc_wt"]), (bc_bias[:, :], w["bc_bias"]),
                             (guard["a_log"][:, :], w["a_log"]), (guard["bc_pick"][:, :], w["bc_pick"])):
                sp.dma_start(dst, src).then_inc(loaded, 16)

        @block.tensor
        def _(pe):
            pe.wait_ge(loaded, 16 * n_loads)
            pe.matmul(p_rec[0:N, 0:1], wr_t[:, :], h0, start=True, stop=True).then_inc(rec_ready, 1)
            pe.wait_ge(summed, 1)
            pe.matmul(p_sig[0:N, 0:A], wi_t[:, :], means[:, :], start=True, stop=True).then_inc(psig, 1)
            pe.wait_ge(newh, 1)
            pe.matmul(p_sel[:, 0:A], sel_t[:, :], th[:, :], start=True, stop=True).then_inc(psel, 1)
            pe.wait_ge(gated, 1)
            with pe.Fori(0, G // 2) as i:
                for j in range(2):
                    xs = xn_t[:, bass.ds((i * 2 + j) * GT, GT)]
                    pe.wait_ge(z_kept, i * 2 + (j + 1))
                    pe.matmul(pz[:, j], delta_wt[:, :], xs, start=True, stop=True).then_inc(z_ready, 1)
                    pe.wait_ge(bc_kept, i * 2 + (j + 1))
                    pe.matmul(pbc[:, j], bc_wt[:, :], xs, start=True, stop=True).then_inc(bc_ready, 1)

        @block.scalar
        def _(act):
            act.wait_ge(loaded, 16 * n_loads)
            act.activation(guard["a"][:, :], guard["a_log"][:, :], ACT.Exp).then_inc(col_ready, 1)
            act.wait_ge(psig, 1)
            act.wait_ge(col_ready, 2)
            act.activation(th[:, :], p_sig[0:N, 0:A], ACT.Tanh, bias=th_bias, scale=1.0 / S).then_inc(thd, 1)
            act.wait_ge(psel, 1)
            act.activation(sel[:, :], p_sel[:, 0:A], ACT.Sigmoid, bias=dcols[:, 0:1]).then_inc(seld, 1)
            act.sem_inc(z_kept, 2)
            with act.Fori(0, G // 2) as i:
                for j in range(2):
                    hold(act, z_ready, i * 2 + (j + 1), const)
                    cols_ = bass.ds((i * 2 + j) * GT, GT)
                    act.activation(tmp[:, cols_], pz[:, j], ACT.Abs, bias=dcols[:, 3:4])
                    act.activation(delta[:, cols_], pz[:, j], ACT.Identity, bias=dcols[:, 3:4]).then_inc(z_kept, 1)
                    act.drain()
                    act.activation(tmp[:, cols_], tmp[:, cols_], ACT.Exp, scale=-1.0)
            act.drain()
            for c in quarters:
                act.activation(tmp[:, c], tmp[:, c], ACT.Ln, bias=1.0).then_inc(logs, 1)

        @block.vector
        def _(dve):
            dve.wait_ge(loaded, 16 * n_loads)
            dve.tensor_reduce(means[:, :], xn_t[:, :].rearrange("d (a s) -> d a s", s=S), AX.X, ALU.add).then_inc(summed, 1)
            dve.tensor_scalar(c1, tau, 0.1, 10.0, ALU.max, ALU.min)
            dve.drain()
            dve.reciprocal(c1, c1)
            dve.wait_ge(rec_ready, 1)
            dve.tensor_tensor(th_bias, p_rec[0:N, 0:1], wi_b, ALU.add)
            dve.drain()
            dve.tensor_scalar(c1, c1, 0.1, None, ALU.mult)
            dve.tensor_tensor(dcols[:, 3:4], dcols[:, 1:2], dcols[:, 2:3], ALU.add)
            dve.drain().then_inc(col_ready, 1)
            dve.tensor_tensor(c2, c1, h0, ALU.mult)
            dve.drain()
            dve.tensor_tensor(c2, h0, c2, ALU.subtract)
            dve.drain()
            dve.wait_ge(thd, 1)
            dve.tensor_scalar(th[:, :], th[:, :], c1, c2, ALU.mult, ALU.add).then_inc(newh, 1)
            dve.wait_ge(col_ready, 2)
            dve.tensor_scalar(guard["near0"][:, :], guard["a"][:, :], 1e-6, None, ALU.is_lt)
            dve.tensor_scalar(guard["inv"][:, :], guard["a"][:, :], 1e-30, None, ALU.max)
            dve.drain()
            dve.reciprocal(guard["inv"][:, :], guard["inv"][:, :])
            dve.tensor_scalar(guard["far"][:, :], guard["near0"][:, :], -1.0, 1.0, ALU.mult, ALU.add)
            dve.tensor_scalar(guard["a"][:, :], guard["a"][:, :], -1.0, None, ALU.mult)
            dve.drain()
            dve.tensor_tensor(guard["inv"][:, :], guard["inv"][:, :], guard["far"][:, :], ALU.mult)
            dve.drain()
            dve.tensor_scalar(guard["minus_inv"][:, :], guard["inv"][:, :], -1.0, None, ALU.mult)
            dve.wait_ge(seld, 1)
            xs3 = xn_t[:, :].rearrange("d (a s) -> d a s", s=S)
            dve.tensor_tensor(xs3, xs3, sel[:, :].rearrange("d (a o) -> d a o", o=1).broadcast_to((D, A, S)),
                              ALU.mult)
            dve.drain().then_inc(gated, 1)
            dve.sem_inc(bc_kept, 2)
            with dve.Fori(0, G // 2) as i:
                for j in range(2):
                    cols_ = bass.ds((i * 2 + j) * GT, GT)
                    dve.wait_ge(bc_ready, i * 2 + (j + 1))
                    dve.tensor_scalar(full[:, j], pbc[:, j], bc_bias[:, 0:1], None, ALU.add).then_inc(bc_kept, 1)
                    dve.drain()
                    dve.tensor_copy(part[:, j], full[:, j])
                    dve.drain()
                    dve.tensor_copy(split[0:32, cols_], part[0:32, j])
                    dve.tensor_tensor(full[:, j], full[:, j], part[:, j], ALU.subtract)
                    dve.drain()
                    dve.tensor_copy(part[:, j], full[:, j])
                    dve.drain()
                    dve.tensor_copy(split[32:64, cols_], part[32:64, j])
                    dve.tensor_tensor(split[64:R, cols_], full[64:R, j], part[64:R, j], ALU.subtract)
            for k, c in enumerate(quarters):
                dve.wait_ge(logs, k + 1)
                dve.scalar_tensor_tensor(delta[:, c], delta[:, c], 0.0, tmp[:, c], ALU.max, ALU.add)
            dve.drain()


def phase_scan(nc, w, xn_t, const, delta, split, guard):
    CH = 1024
    HALF = CH // 2
    with Phase(nc, "sc") as ph:
        decay = ph.sb("decay", [D, 2, CH])
        num = ph.sb("num", [D, 2, CH])
        wx = ph.sb("wx", [D, 2, CH])
        drive = ph.sb("drive", [D, 2, CH])
        h = ph.sb("h", [D, 2, CH])
        hc = ph.sb("hc", [D, 2, CH])
        pb = ph.psum("pb", [P, 2, CH])
        pc = ph.psum("pc", [P, CH])
        py = ph.psum("py", [P, CH])
        names = ("b_ready", "b_used", "c_ready", "hc_done", "y_added", "exp_done", "num_done", "drive_done",
                 "reset_done", "scanned", "y_kept")
        (b_ready, b_used, c_ready, hc_done, y_added, exp_done, num_done, drive_done, reset_done, scanned,
         y_kept) = (ph.sem(n) for n in names)
        block = ph.block()
        pick = guard["bc_pick"]

        def chunks(engine, chunk):
            chunk(0, True, False)
            with engine.Fori(0, TOK // CH - 2) as i:
                chunk(i + 1, False, False)
            chunk(TOK // CH - 1, False, True)

        @block.tensor
        def _(pe):
            def broadcast(c, out, which, n, done):
                col = (which * N + n) * P
                for q in range(2):
                    last = pe.matmul(out[:, q * HALF:(q + 1) * HALF], pick[:, col:col + P],
                                     split[:, bass.ds(c * CH + q * HALF, HALF)], start=True, stop=True)
                last.then_inc(done, 1)

            def add_state(n):
                for q in range(2):
                    cols = slice(q * HALF, (q + 1) * HALF)
                    last = pe.matmul(py[:, cols], const["ident"], hc[:, n % 2, cols], start=(n == 0),
                                     stop=(n == N - 1))
                last.then_inc(y_added, 1)

            def broadcast_b(c, n):
                pe.wait_ge(b_used, c * N + (n + 1))
                broadcast(c, pb[:, n % 2], 0, n, b_ready)

            def chunk(c, first, last):
                if first:
                    broadcast_b(c, 0)
                for n in range(N):
                    if n < N - 1:
                        broadcast_b(c, n + 1)
                    elif not last:
                        broadcast_b(c + 1, 0)
                    pe.wait_ge(hc_done, c * N + (n + 1))
                    broadcast(c, pc, 1, n, c_ready)
                    if n == 1:
                        pe.wait_ge(y_kept, c + 1)
                    if n or not first:
                        add_state((n - 1) % N)
                if last:
                    pe.wait_ge(hc_done, c * N + (N + 1))
                    add_state(N - 1)

            chunks(pe, chunk)

        @block.scalar
        def _(act):
            act.sem_inc(y_kept, 1)

            def keep_y(c):
                hold(act, y_added, c * N + (N + 2), const)
                act.activation(xn_t[:, bass.ds(c * CH, CH)], py[:, :], ACT.Copy).then_inc(y_kept, 1)

            def chunk(c, first, last):
                for n in range(N):
                    s = n % 2
                    hold(act, scanned, c * N + (n + 1), const)
                    act.activation(decay[:, s], delta[:, bass.ds(c * CH, CH)], ACT.Exp,
                                   scale=guard["a"][:, n:n + 1])
                    act.drain()
                    act.activation(num[:, s], decay[:, s], ACT.Identity, scale=guard["minus_inv"][:, n:n + 1],
                                   bias=guard["inv"][:, n:n + 1]).then_inc(exp_done, 1)
                    if n == 1 and not first:
                        keep_y(c - 1)
                if last:
                    keep_y(c)

            chunks(act, chunk)

        @block.gpsimd
        def _(pool):
            with pool.Fori(0, TOK // CH) as c:
                for n in range(N):
                    s = n % 2
                    pool.wait_ge(num_done, c * N + (n + 1))
                    pool.tensor_tensor(drive[:, s], num[:, s], wx[:, s], ALU.mult).then_inc(drive_done, 1)
                    first = decay[:, s].rearrange("d (a t) -> d a t", t=S)[:, :, 0:1]
                    pool.memset(first, 0.0).then_inc(reset_done, 1)

        @block.vector
        def _(dve):
            dve.sem_inc(b_used, 2)
            dve.sem_inc(scanned, 2)
            dve.sem_inc(hc_done, 1)
            dve.sem_inc(y_added, 2)

            def drive_in(c, n):
                s = n % 2
                dve.wait_ge(b_ready, c * N + (n + 1))
                dve.tensor_tensor(wx[:, s], pb[:, s], xn_t[:, bass.ds(c * CH, CH)], ALU.mult).then_inc(b_used, 1)
                dve.wait_ge(exp_done, c * N + (n + 1))
                dve.scalar_tensor_tensor(num[:, s], delta[:, bass.ds(c * CH, CH)], guard["near0"][:, n:n + 1],
                                         num[:, s], ALU.mult, ALU.add)
                dve.drain().then_inc(num_done, 1)

            def scan_out(c, n):
                s = n % 2
                dve.wait_ge(drive_done, c * N + (n + 1))
                dve.wait_ge(reset_done, c * N + (n + 1))
                dve.tensor_tensor_scan(h[:, s], decay[:, s], drive[:, s], 0.0, ALU.mult, ALU.add)
                dve.drain().then_inc(scanned, 1)
                dve.wait_ge(y_added, c * N + (n + 1))
                dve.wait_ge(c_ready, c * N + (n + 1))
                dve.tensor_tensor(hc[:, s], pc[:, :], h[:, s], ALU.mult).then_inc(hc_done, 1)

            def chunk(c, first, last):
                for n in range(N):
                    drive_in(c, n)
                    if n:
                        scan_out(c, n - 1)
                    elif not first:
                        scan_out(c - 1, N - 1)
                if last:
                    scan_out(c, N - 1)

            chunks(dve, chunk)


def pipelined(engine, front, back, tail):
    def together(now, ahead, behind):
        streams = [part(*group) if group else [] for part, group in ((back, now), (front, ahead), (tail, behind))]
        for k in range(max(len(steps) for steps in streams)):
            for steps in streams:
                if k < len(steps) and steps[k]:
                    steps[k]()

    together(None, (0, 0, 0), None)
    together((0, 0, 0), (1, 1, 0), None)
    with engine.Fori(0, G // 2 - 1) as i:
        together((i * 2 + 1, 1, i), (i * 2 + 2, 0, i + 1), (i * 2, 0, i))
        together((i * 2 + 2, 0, i + 1), (i * 2 + 3, 1, i + 1), (i * 2 + 1, 1, i))
    together((G - 1, 1, G // 2 - 1), None, (G - 2, 0, G // 2 - 1))
    together(None, None, (G - 1, 1, G // 2 - 1))


def phase_mlstm(nc, w, tag, x, ctx, out, const, eps, ahead, scan_out=None):
    K = 8
    SCALE = float(DH) ** -0.5
    with Phase(nc, tag) as ph:
        gate_w = ph.sb("gate_w", [D, 3, 2 * NH])
        gate_b = ph.sb("gate_b", [P, T, 2 * NH])
        norm_w = ph.sb("norm_w", [P, D])
        seq_tri = ph.sb("seq_tri", [P, P])
        mask = ph.sb("mask", [P, GT], BF16)
        ident_b = ph.sb("ident_b", [P, P], BF16)
        minus_pick = ph.sb("minus_pick", [P, T * NH * P])
        x_in = ph.sb("x_in", [P, 2, T, D])
        c_in = ph.sb("c_in", [P, 2, T, D])
        y_in = ph.sb("y_in", [P, 2, GT]) if scan_out is not None else None
        xr = ph.sb("xr", [P, 2, T, D])
        cv = ph.sb("cv", [P, 2, T, NH, DH + 1])
        qn = ph.sb("qn", [P, T, D])
        stats, mean_var, rstd = ph.sb("stats", [P, T, 6]), ph.sb("mean_var", [P, T, 2]), ph.sb("rstd", [P, T])
        qt = ph.sb("qt", [D, 2, GT])
        ct = ph.sb("ct", [D, 2, GT])
        qz = ph.sb("qz", [D, 2, NH, GT])
        gates = ph.sb("gates", [P, T, 2 * NH])
        soft = ph.sb("soft", [P, T, NH])
        logf = ph.sb("logf", [P, T, NH])
        cs = ph.sb("cs", [P, 2, T, NH])
        u = ph.sb("u", [P, 2, T, NH])
        ut = ph.sb("ut", [T * NH, P])
        mt = ph.sb("mt", [P, 2, P])
        msum = ph.sb("msum", [P, T, NH])
        floor = ph.sb("floor", [P, 2, T * NH])
        dm = ph.sb("dm", [P, 2, GT])
        cm = ph.sb("cm", [P, 2, GT])
        den = ph.sb("den", [P, T * NH])
        hb = ph.sb("hb", [P, T * NH, DH])
        sq = ph.sb("sq", [P, T * NH, DH])
        msq = ph.sb("msq", [P, T * NH])
        hrstd = ph.sb("hrstd", [P, T * NH])
        eps_h = ph.sb("eps_h", [P, T * NH])
        half_h = ph.sb("half_h", [P, T * NH])
        xo = ph.sb("xo", [P, 2, T, D])
        pt0, pt1, pg = ph.psum("pt0", [P, GT]), ph.psum("pt1", [P, GT]), ph.psum("pg", [P, GT])
        pd, pq = ph.psum("pd", [P, 2, GT]), ph.psum("pq", [P, GT])
        ph_ = ph.psum("ph", [P, 2, GT])
        x_loaded = [ph.sem("x_loaded0"), ph.sem("x_loaded1")]
        c_loaded = [ph.sem("c_loaded0"), ph.sem("c_loaded1")]
        stored = [ph.sem("stored0"), ph.sem("stored1")]
        s = ph.sems("w_loaded", "ahead_loaded", "w_ready", "x_used", "y_staged", "y_turned", "stats_done", "rstd_done", "normed",
                    "q_turned", "c_turned", "c_copied", "q_kept", "heads_kept", "c_kept", "gates_in", "gates_done", "log_done",
                    "logf_done", "cs_ready", "u_ready", "ut_ready", "m_ready", "mt_ready", "msum_done",
                    "floor_done", "d_ready", "exp_done", "q_ready", "c_done", "pv_done", "h_read", "sq_done",
                    "hrstd_done", "res_kept", "summed")
        src, csrc, dst = token_groups(x), token_groups(ctx), token_groups(out)
        block = ph.block()
        n_loads = 7

        @block.sync
        def _(sp):
            for to, frm in ((gate_w[:, :, :], w["gate_w"]), (gate_b[:, :, :], w["gate_b"]),
                            (norm_w[:, :], w["norm_w"]), (seq_tri[:, :], w["seq_tri"]), (mask[:, :], w["mask"]),
                            (ident_b[:, :], w["ident_b"]), (minus_pick[:, :], w["minus_pick"])):
                sp.dma_start(to, frm).then_inc(s["w_loaded"], 16)

            def load(g, j, half):
                sp.wait_ge(s["x_used"], g + 1)
                sp.wait_ge(s["c_copied"], g + 1)
                sp.wait_ge(s["c_turned"], g + 1)
                sp.dma_start(x_in[:, j], src[g]).then_inc(x_loaded[j], 16)
                sp.dma_start(c_in[:, j], csrc[g]).then_inc(c_loaded[j], 16)

            def store(g, j, half):
                sp.wait_ge(s["summed"], g + 1)
                sp.dma_start(dst[g], xo[:, j]).then_inc(stored[j], 16)

            load(0, 0, 0)
            load(1, 1, 0)
            for to, frm in ahead:
                sp.dma_start(to, frm).then_inc(s["ahead_loaded"], 16)
            with sp.Fori(0, G // 2 - 1) as i:
                for j in range(2):
                    load(i * 2 + (j + 2), j, i + 1)
                    store(i * 2 + j, j, i)
            store(G - 2, 0, G // 2 - 1)
            store(G - 1, 1, G // 2 - 1)
            sp.wait_ge(s["ahead_loaded"], 16 * len(ahead))
            for j in range(2):
                sp.wait_ge(stored[j], 16 * (G // 2 + 1))

        @block.tensor
        def _(pe):
            pe.sem_inc(s["c_turned"], 2)
            pe.sem_inc(s["pv_done"], 2)
            pe.wait_ge(s["w_loaded"], 16 * n_loads)

            def front(g, j, half):
                def turn_inputs():
                    if y_in is not None:
                        pe.wait_ge(s["y_staged"], g + 1)
                        pe.wait_ge(s["q_kept"], g + 1)
                        for t in range(T):
                            last = pe.transpose(pt0[:, t * P:(t + 1) * P], y_in[:, j, t * P:(t + 1) * P], const["ident"])
                        last.then_inc(s["y_turned"], 1)
                    pe.wait_ge(c_loaded[j], half * 16 + 16)
                    pe.wait_ge(s["c_kept"], g + 1)
                    for t in range(T):
                        last = pe.transpose(pt1[:, t * P:(t + 1) * P], c_in[:, j, t, :], const["ident"])
                    last.then_inc(s["c_turned"], 1)

                def turn_q():
                    pe.wait_ge(s["q_kept"], g + 1)
                    pe.wait_ge(s["normed"], g + 1)
                    for t in range(T):
                        last = pe.transpose(pt0[:, t * P:(t + 1) * P], qn[:, t, :], const["ident"])
                    last.then_inc(s["q_turned"], 1)

                def gate_products():
                    pe.wait_ge(s["q_kept"], g + 2)
                    pe.wait_ge(s["c_kept"], g + 2)
                    pe.wait_ge(s["msum_done"], g + 1)
                    for t in range(T):
                        tok = slice(t * P, (t + 1) * P)
                        o = pg[:, t * 2 * NH:(t + 1) * 2 * NH]
                        pe.matmul(o, qt[:, j, tok], gate_w[:, 0, :], start=True, stop=False)
                        pe.matmul(o, ct[:, j, tok], gate_w[:, 1, :], start=False, stop=False)
                        last = pe.matmul(o, ct[:, j, tok], gate_w[:, 2, :], start=False, stop=True)
                    last.then_inc(s["gates_in"], 1)

                def running_sums():
                    pe.wait_ge(s["logf_done"], g + 1)
                    pe.matmul(pg[:, 32:32 + T * NH], seq_tri[:, :], logf[:, :, :].rearrange("p t h -> p (t h)"),
                              start=True, stop=True).then_inc(s["cs_ready"], 1)

                def turn_u():
                    pe.wait_ge(s["u_ready"], g + 1)
                    pe.transpose(pg[0:T * NH, 64:64 + P], u[:, j].rearrange("p t h -> p (t h)"),
                                 const["ident"]).then_inc(s["ut_ready"], 1)

                def turn_maxima():
                    hold(pe, s["m_ready"], g + 1, const)
                    pe.transpose(pg[:, 192:192 + T * NH], mt[0:T * NH, j], const["ident"][0:T * NH, 0:T * NH])\
                      .then_inc(s["mt_ready"], 1)

                return [turn_inputs, turn_q, gate_products, running_sums, turn_u, turn_maxima]

            def back(g, j, half):
                def pv(h):
                    pe.wait_ge(s["c_done"], g * NH + (h + 1 + K))
                    if h == 0:
                        pe.wait_ge(s["c_copied"], g + 3)
                        pe.wait_ge(s["h_read"], g + 1)
                    for t in range(T):
                        o = ph_[:, t // 2, ((t % 2) * NH + h) * (DH + 1):((t % 2) * NH + h + 1) * (DH + 1)]
                        last = pe.matmul(o, cm[:, h % 2, t * P:(t + 1) * P], cv[:, j, t, h, :], start=True, stop=True)
                    last.then_inc(s["pv_done"], 1)

                def head(h):
                    pe.wait_ge(s["exp_done"], g * NH + (h + 1))
                    pe.matmul(pd[:, h % 2], ident_b[:, :], mask[:, :], start=True, stop=False)
                    for t in range(T):
                        k = t * NH + h
                        last = pe.matmul(pd[:, h % 2, t * P:(t + 1) * P], minus_pick[:, k * P:(k + 1) * P],
                                         mt[:, j], start=False, stop=(t == T - 1))
                    last.then_inc(s["d_ready"], 1)
                    pe.wait_ge(s["heads_kept"], g + 1)
                    pe.wait_ge(s["c_done"], g * NH + (h + K))
                    for t in range(T):
                        tok = slice(t * P, (t + 1) * P)
                        last = pe.matmul(pq[:, tok], ct[:, j, tok], qz[:, j, h, tok], start=True, stop=True)
                    last.then_inc(s["q_ready"], 1)
                    if h:
                        pv(h - 1)

                return [lambda: head(0), lambda: head(1), lambda: head(2), lambda: head(3), lambda: pv(NH - 1)]

            pipelined(pe, front, back, lambda g, j, half: [])

        @block.scalar
        def _(act):
            act.sem_inc(s["q_kept"], 1)
            act.sem_inc(s["c_kept"], 1)
            act.sem_inc(s["exp_done"], 2)
            act.wait_ge(s["w_ready"], 1)

            def front(g, j, half):
                def stage():
                    if y_in is not None:
                        hold(act, s["y_turned"], g + 1, const)
                        act.activation(y_in[:, j], scan_out[:, bass.ds(g * GT, GT)], ACT.Copy).then_inc(s["y_staged"], 1)
                    act.wait_ge(s["c_turned"], g + 3)
                    act.wait_ge(s["c_done"], g * NH + (K - NH))
                    act.activation(ct[:, j], pt1[:, :], ACT.Copy).then_inc(s["c_kept"], 1)

                def keep_q():
                    act.wait_ge(s["q_turned"], g + 1)
                    act.activation(qt[:, j], pt0[:, :], ACT.Copy).then_inc(s["q_kept"], 1)
                    act.drain()
                    for h in range(NH):
                        rows = slice(h * DH, (h + 1) * DH)
                        last = act.activation(qz[rows, j, h, :], qt[rows, j], ACT.Copy)
                    last.then_inc(s["heads_kept"], 1)

                def log_gates():
                    act.wait_ge(s["gates_done"], g + 1)
                    act.activation(soft[:, :, :], gates[:, :, NH:], ACT.Abs)
                    act.drain()
                    act.activation(soft[:, :, :], soft[:, :, :], ACT.Exp, scale=-1.0)
                    act.drain()
                    act.activation(soft[:, :, :], soft[:, :, :], ACT.Ln, bias=1.0).then_inc(s["log_done"], 1)

                def floors():
                    act.wait_ge(s["h_read"], g) if not isinstance(g, int) or g else None
                    act.wait_ge(s["msum_done"], g + 2)
                    act.activation(floor[:, j], msum[:, :, :].rearrange("p t h -> p (t h)"), ACT.Exp, scale=-1.0)\
                       .then_inc(s["floor_done"], 1)

                return [stage, keep_q, log_gates, None, None, None, floors]

            def back(g, j, half):
                def head(h):
                    act.wait_ge(s["c_done"], g * NH + (h + K - 1))
                    act.wait_ge(s["d_ready"], g * NH + (h + 1))
                    for t in range(T):
                        tok = slice(t * P, (t + 1) * P)
                        last = act.activation(dm[:, h % 2, tok], pd[:, h % 2, tok], ACT.Exp,
                                              bias=u[:, j, t, h:h + 1])
                    last.then_inc(s["exp_done"], 1)

                def residual():
                    hold(act, stored[j], half * 16 + 16, const)
                    act.wait_ge(s["x_used"], g + 3)
                    act.activation(xo[:, j], xr[:, j], ACT.Copy).then_inc(s["res_kept"], 1)

                return [lambda: head(0), lambda: (head(1), residual()), lambda: head(2), lambda: head(3)]

            pipelined(act, front, back, lambda g, j, half: [])

        @block.gpsimd
        def _(pool):
            pool.sem_inc(s["c_copied"], 2)
            pool.memset(cv[:, :, :, :, :].rearrange("p j t h d -> p (j t h) d")[:, :, DH:DH + 1], 1.0)
            pool.memset(eps_h[:, :], DH * eps)
            pool.memset(half_h[:, :], -0.5)
            pool.drain()

            def front(g, j, half):
                def rstds():
                    pool.wait_ge(s["stats_done"], g + 1)
                    ln_rstd(pool, mean_var[:, :, :], const["eps5"], const["minus_half"], rstd[:, :])\
                        .then_inc(s["rstd_done"], 1)

                def stage():
                    pool.wait_ge(s["pv_done"], g * NH + (2 - NH)) if not isinstance(g, int) or g else None
                    hold(pool, c_loaded[j], half * 16 + 16, const)
                    pool.tensor_copy(cv[:, j].rearrange("p t h d -> p (t h) d")[:, :, 0:DH],
                                     c_in[:, j].rearrange("p t (h d) -> p (t h) d", h=NH)).then_inc(s["c_copied"], 1)

                return [rstds, stage]

            def tail(g, j, half):
                def head_rstd():
                    pool.wait_ge(s["sq_done"], g + 1)
                    pool.tensor_tensor(hrstd[:, :], msq[:, :], eps_h[:, :], ALU.add)
                    pool.drain()
                    pool.tensor_tensor(hrstd[:, :], hrstd[:, :], half_h[:, :], ALU.pow).then_inc(s["hrstd_done"], 1)

                return [None, head_rstd]

            pipelined(pool, front, lambda g, j, half: [], tail)

        @block.vector
        def _(dve):
            dve.sem_inc(s["x_used"], 2)
            dve.sem_inc(s["y_turned"], 2)
            dve.sem_inc(s["c_done"], K)
            dve.sem_inc(s["msum_done"], 1)
            dve.sem_inc(s["h_read"], 1)
            dve.sem_inc(stored[0], 16)
            dve.sem_inc(stored[1], 16)
            dve.memset(mt[:, :, :], 0.0)
            dve.memset(qz[:, :, :, :], 0.0)
            dve.wait_ge(s["w_loaded"], 16 * n_loads)
            dve.tensor_scalar(norm_w[:, :], norm_w[:, :], float(DH) ** 0.5, None, ALU.mult)
            dve.drain().then_inc(s["w_ready"], 1)

            def front(g, j, half):
                def norm_stats():
                    dve.wait_ge(s["res_kept"], g - 1) if not isinstance(g, int) or g > 1 else None
                    dve.wait_ge(x_loaded[j], half * 16 + 16)
                    if y_in is None:
                        dve.tensor_copy(xr[:, j], x_in[:, j])
                    else:
                        dve.wait_ge(s["y_turned"], g + 3)
                        dve.tensor_tensor(xr[:, j], x_in[:, j], pt0[:, :].rearrange("p (t d) -> p t d", t=T), ALU.add)
                    dve.drain().then_inc(s["x_used"], 1)
                    ln_stats(dve, xr[:, j], stats, mean_var)
                    dve.drain().then_inc(s["stats_done"], 1)

                def normalise():
                    dve.wait_ge(s["q_turned"], g) if not isinstance(g, int) or g else None
                    dve.wait_ge(s["rstd_done"], g + 1)
                    ln_apply(dve, qn, xr[:, j], mean_var, rstd)
                    dve.drain().then_inc(s["normed"], 1)

                def add_bias():
                    dve.wait_ge(s["gates_in"], g + 1)
                    dve.tensor_tensor(gates[:, :, :], pg[:, 0:T * 2 * NH].rearrange("p (t h) -> p t h", t=T),
                                      gate_b[:, :, :], ALU.add)
                    dve.drain().then_inc(s["gates_done"], 1)

                def log_forget():
                    dve.wait_ge(s["log_done"], g + 1)
                    dve.scalar_tensor_tensor(logf[:, :, :], gates[:, :, NH:], 0.0, soft[:, :, :], ALU.min, ALU.subtract)
                    dve.drain().then_inc(s["logf_done"], 1)

                def input_minus_sum():
                    dve.wait_ge(s["cs_ready"], g + 1)
                    run = pg[:, 32:32 + T * NH].rearrange("p (t h) -> p t h", t=T)
                    dve.tensor_copy(cs[:, j], run)
                    dve.tensor_tensor(u[:, j], gates[:, :, 0:NH], run, ALU.subtract)
                    dve.drain().then_inc(s["u_ready"], 1)

                def maxima():
                    dve.wait_ge(s["ut_ready"], g + 1)
                    dve.tensor_copy(ut[:, :], pg[0:T * NH, 64:64 + P])
                    dve.drain()
                    for q in range(P // S):
                        c = slice(q * S, (q + 1) * S)
                        dve.tensor_tensor_scan(mt[0:T * NH, j, c], ut[:, c], ut[:, c], -3e38, ALU.max, ALU.max)
                    dve.drain().then_inc(s["m_ready"], 1)

                def sums_of_maxima():
                    dve.wait_ge(s["mt_ready"], g + 1)
                    dve.wait_ge(s["floor_done"], g) if not isinstance(g, int) or g else None
                    dve.tensor_tensor(msum[:, :, :], cs[:, j], pg[:, 192:192 + T * NH].rearrange("p (t h) -> p t h", t=T),
                                      ALU.add)
                    dve.drain().then_inc(s["msum_done"], 1)

                return [norm_stats, normalise, add_bias, log_forget, input_minus_sum, maxima, sums_of_maxima]

            def back(g, j, half):
                def head(h):
                    dve.wait_ge(s["pv_done"], g * NH + (h + 1))
                    dve.wait_ge(s["q_ready"], g * NH + (h + 1))
                    dve.wait_ge(s["exp_done"], g * NH + (h + 3))
                    dve.scalar_tensor_tensor(cm[:, h % 2], pq[:, :], SCALE, dm[:, h % 2], ALU.mult, ALU.mult)\
                       .then_inc(s["c_done"], 1)

                return [lambda: head(0), lambda: head(1), lambda: head(2), lambda: head(3)]

            def tail(g, j, half):
                def each(a, k=T * NH):
                    return a.rearrange("p (k o) -> p k o", o=1).broadcast_to((P, k, DH))

                def divide():
                    dve.wait_ge(s["pv_done"], g * NH + (NH + 2))
                    dve.wait_ge(s["floor_done"], g + 1)
                    heads = [ph_[:, b, 0:2 * NH * (DH + 1)].rearrange("p (k d) -> p k d", d=DH + 1) for b in range(2)]
                    part = [slice(b * 2 * NH, (b + 1) * 2 * NH) for b in range(2)]
                    for b in range(2):
                        dve.scalar_tensor_tensor(den[:, part[b]], heads[b][:, :, DH], -1.0, floor[:, j, part[b]],
                                                 ALU.mult, ALU.max)
                    dve.drain()
                    for b in range(2):
                        dve.tensor_tensor(den[:, part[b]], heads[b][:, :, DH], den[:, part[b]], ALU.max)
                    dve.drain()
                    dve.tensor_scalar(den[:, :], den[:, :], 1e-6, None, ALU.add)
                    dve.drain()
                    dve.reciprocal(den[:, :], den[:, :])
                    dve.drain()
                    for b in range(2):
                        dve.tensor_tensor(hb[:, part[b]], heads[b][:, :, 0:DH], each(den[:, part[b]], 2 * NH), ALU.mult)
                    dve.drain().then_inc(s["h_read"], 1)

                def variance():
                    dve.tensor_reduce(msq[:, :], hb[:, :, :], AX.X, ALU.add)
                    dve.drain()
                    dve.tensor_scalar(msq[:, :], msq[:, :], 1.0 / DH, None, ALU.mult)
                    dve.drain()
                    dve.tensor_tensor(hb[:, :, :], hb[:, :, :], each(msq[:, :]), ALU.subtract)
                    dve.drain()
                    dve.tensor_tensor(sq[:, :, :], hb[:, :, :], hb[:, :, :], ALU.mult)
                    dve.drain()
                    dve.tensor_reduce(msq[:, :], sq[:, :, :], AX.X, ALU.add)
                    dve.drain().then_inc(s["sq_done"], 1)

                def by_tile():
                    return hb[:, :, :].rearrange("p (t h) d -> p t (h d)", t=T)

                def weigh():
                    wide = norm_w[:, :].rearrange("p (o d) -> p o d", o=1).broadcast_to((P, T, D))
                    dve.tensor_tensor(by_tile(), by_tile(), wide, ALU.mult)
                    dve.drain()

                def head_norm():
                    dve.wait_ge(s["hrstd_done"], g + 1)
                    dve.tensor_tensor(hb[:, :, :], hb[:, :, :], each(hrstd[:, :]), ALU.mult)
                    dve.drain()
                    dve.wait_ge(s["res_kept"], g + 1)
                    dve.tensor_tensor(xo[:, j], xo[:, j], by_tile(), ALU.add)
                    dve.drain().then_inc(s["summed"], 1)

                return [divide, variance, weigh, head_norm]

            pipelined(dve, front, back, tail)


def column_groups(x):
    return x.rearrange("a (g t) d -> g a t d", t=T)


def phase_experts(nc, w, tag, x, out, const, routed, w1, w2):
    with Phase(nc, tag) as ph:
        w1h = ph.sb("w1h", [D, E, F])
        w1l = ph.sb("w1l", [D, E, F])
        b1 = ph.sb("b1", [P, E, FT])
        b2 = ph.sb("b2", [E, D])
        iota = ph.sb("iota", [P, E])
        if routed:
            rw1 = ph.sb("rw1", [D, F])
            rb1 = ph.sb("rb1", [P, FT])
            rw2 = ph.sb("rw2", [P, FT, E])
            rb2 = ph.sb("rb2", [P, T, E])
            rh = ph.sb("rh", [P, FT, GT])
        else:
            cent = ph.sb("cent", [D, E])
            ln_g = ph.sb("ln_g", [D, E])
            ln_b = ph.sb("ln_b", [D, E])
            z = ph.sb("z", [P, T, D])
            zt = ph.sb("zt", [D, 2, GT])
        x_in = ph.sb("x_in", [P, 2, T, D])
        xf = ph.sb("xf", [P, 2, T, D])
        xft = ph.sb("xft", [D, 2, GT])
        xh = ph.sb("xh", [D, 2, GT])
        xl = ph.sb("xl", [D, 2, GT])
        stats, mean_var, rstd = ph.sb("stats", [P, T, 6]), ph.sb("mean_var", [P, T, 2]), ph.sb("rstd", [P, T])
        score = ph.sb("score", [P, T, E])
        top = ph.sb("top", [P, T, 8])
        top_i = ph.sb("top_i", [P, T, 8], U32)
        top_f = ph.sb("top_f", [P, T, 8])
        share = ph.sb("share", [P, 3, T])
        gate = ph.sb("gate", [P, 2, T, E])
        gate2 = ph.sb("gate2", [P, T, E])
        gate_t = ph.sb("gate_t", [E, 2, GT])
        hid = ph.sb("hid", [P, 2, FT, GT])
        xo = ph.sb("xo", [P, 2, T, D])
        pf, py = ph.psum("pf", [P, 2, GT]), ph.psum("py", [P, 2, GT])
        pt, pr, pg = ph.psum("pt", [P, GT]), ph.psum("pr", [P, 2, GT]), ph.psum("pg", [P, GT])
        x_loaded = [ph.sem("x_loaded0"), ph.sem("x_loaded1")]
        stored = [ph.sem("stored0"), ph.sem("stored1")]
        s = ph.sems("w_loaded", "w_bias", "b_ready", "w_ready", "x_used", "stats_done", "rstd_done", "normed", "turned", "kept", "split",
                    "r_ready", "r_kept", "scored", "gap_done", "exp_done", "gated", "gate_turned", "gate_kept",
                    "h_ready", "h_kept", "y_ready", "y_used", "summed")
        NLN = 1 if routed else 2
        src, dst = column_groups(x), column_groups(out)
        block = ph.block()
        loads = [(b1[:, :, :], w["b1"]), (b2[:, :], w["b2"]),
                 (iota[:, :], w["iota"])]
        if routed:
            loads += [(rw1[:, :], w["rw1"]), (rb1[:, :], w["rb1"]), (rw2[:, :, :], w["rw2"]), (rb2[:, :, :], w["rb2"])]
        else:
            loads += [(cent[:, :], w["cent"]), (ln_g[:, :], w["ln_g"]), (ln_b[:, :], w["ln_b"])]

        def in_step(back, front):
            def body(g, j, half, nxt):
                steps = front(*nxt) if nxt else []
                for e in range(E + 1):
                    back(g, j, half, e)
                    if e < len(steps):
                        steps[e]()
            return body

        def run(engine, front, back, second=None, prepared=None):
            body = in_step(back, front)
            for k, step in enumerate(front(0, 0, 0)):
                step()
                if k == 0 and second:
                    second()
            if prepared:
                prepared()
            with engine.Fori(0, G // 2 - 1) as i:
                for j in range(2):
                    body(i * 2 + j, j, i, (i * 2 + (j + 1), 1 - j, i + j))
            body(G - 2, 0, G // 2 - 1, (G - 1, 1, G // 2 - 1))
            body(G - 1, 1, G // 2 - 1, None)

        @block.sync
        def _(sp):
            def load(g, j):
                sp.wait_ge(s["x_used"], g + 1)
                sp.dma_start(x_in[:, j], src[g]).then_inc(x_loaded[j], 16)

            load(0, 0)
            for to, frm in loads:
                sp.dma_start(to, frm).then_inc(s["w_loaded"], 16)
            load(1, 1)

            def store(g, j):
                sp.wait_ge(s["summed"], g + 1)
                sp.dma_start(dst[g], xo[:, j]).then_inc(stored[j], 16)

            with sp.Fori(0, G // 2 - 1) as i:
                for j in range(2):
                    store(i * 2 + j, j)
                    load(i * 2 + (j + 2), j)
            store(G - 2, 0)
            store(G - 1, 1)
            for j in range(2):
                sp.wait_ge(stored[j], 16 * (G // 2 + 1))

        @block.gpsimd
        def _(pool):
            def front(g, j, half):
                def step():
                    for k in range(NLN):
                        pool.wait_ge(s["stats_done"], g * NLN + (k + 1))
                        ln_rstd(pool, mean_var[:, :, :], const["eps5"], const["minus_half"], rstd[:, :])\
                            .then_inc(s["rstd_done"], 1)
                return [step]

            run(pool, front, lambda g, j, half, e: None)

        @block.tensor
        def _(pe):
            pe.sem_inc(s["turned"], 1)
            pe.sem_inc(s["y_ready"], 1)
            pe.wait_ge(s["w_loaded"], 16 * len(loads))
            if not routed:
                for e in range(E):
                    for f in range(FT):
                        last = pe.matmul(pg[:, e * FT + f:e * FT + f + 1], w1[:, e, f * P:(f + 1) * P],
                                         ln_b[:, e:e + 1], start=True, stop=True)
                last.then_inc(s["w_bias"], 1)
                pe.wait_ge(s["b_ready"], 1)

            def front(g, j, half):
                def turn():
                    pe.wait_ge(s["gate_kept"], g + 1)
                    pe.wait_ge(s["normed"], g + 1)
                    for t in range(T):
                        last = pe.transpose(pt[:, t * P:(t + 1) * P], xf[:, j, t, :], const["ident"])
                    if not routed:
                        pe.wait_ge(s["kept"], g + 1)
                        for t in range(T):
                            last = pe.transpose(pr[:, 0, t * P:(t + 1) * P], z[:, t, :], const["ident"])
                    last.then_inc(s["turned"], 1)

                def route(f):
                    pe.wait_ge(s["kept"], g + 2)
                    pe.wait_ge(s["r_kept"], g * FT + (f + 1))
                    pe.matmul(pr[:, f % 2], rw1[:, f * P:(f + 1) * P], xft[:, j], start=True, stop=True)\
                      .then_inc(s["r_ready"], 1)

                def scores():
                    if routed:
                        pe.wait_ge(s["r_kept"], g * FT + (FT + 2))
                    else:
                        pe.wait_ge(s["kept"], g + 2)
                    pe.wait_ge(s["gated"], g + 1)
                    for t in range(T):
                        tok = slice(t * P, (t + 1) * P)
                        o = pg[:, t * E:(t + 1) * E]
                        if routed:
                            for f in range(FT):
                                last = pe.matmul(o, rh[:, f, tok], rw2[:, f, :], start=(f == 0), stop=(f == FT - 1))
                        else:
                            last = pe.matmul(o, xft[:, j, tok], cent[:, :], start=True, stop=True)
                    last.then_inc(s["scored"], 1)

                def turn_gates():
                    pe.wait_ge(s["gated"], g + 2)
                    for t in range(T):
                        last = pe.transpose(pt[0:E, t * P:(t + 1) * P], gate[:, j, t, :], const["ident"])
                    last.then_inc(s["gate_turned"], 1)

                if routed:
                    return [lambda: None, turn, lambda: (route(0), route(1)), lambda: (route(2), route(3)), scores,
                            lambda: None, turn_gates]
                return [lambda: None, turn, scores, lambda: None, turn_gates]

            def back(g, j, half, e):
                def second(v):
                    pe.wait_ge(s["y_used"], g * (E + 1) + (v + 1))
                    if v == 0:
                        pe.wait_ge(s["gate_kept"], g + 2)
                    else:
                        pe.wait_ge(s["h_kept"], g * E * FT + ((v - 1) * FT + FT + 2))
                    for t in range(T):
                        tok = slice(t * P, (t + 1) * P)
                        o = py[:, (g_par(j) + v) % 2, tok]
                        if v == 0:
                            last = pe.matmul(o, gate_t[:, j, tok], b2[:, :], start=True, stop=True)
                        else:
                            for f in range(FT):
                                last = pe.matmul(o, hid[:, (v - 1) % 2, f, tok], w2[:, v - 1, f, :],
                                                 start=(f == 0), stop=(f == FT - 1))
                    last.then_inc(s["y_ready"], 1)

                if e == 0:
                    pe.wait_ge(s["split"], g + 1)
                if e < E:
                    pe.wait_ge(s["w_ready"], e + 1)
                    for f in range(FT):
                        pe.wait_ge(s["h_kept"], g * E * FT + (e * FT + f + 1))
                        cols = slice(f * P, (f + 1) * P)
                        split_product(pe, pf[:, f % 2], w1h[:, e, cols], w1l[:, e, cols], xh[:, j], xl[:, j])\
                            .then_inc(s["h_ready"], 1)
                second(e)

            run(pe, front, back)

        @block.scalar
        def _(act):
            act.sem_inc(s["kept"], 1)
            act.sem_inc(s["gate_kept"], 1)
            act.sem_inc(s["r_kept"], 2)
            act.sem_inc(s["h_kept"], 2)

            def front(g, j, half):
                def keep():
                    act.wait_ge(s["turned"], g + 2)
                    if not routed:
                        act.activation(zt[:, j], pr[:, 0], ACT.Copy)
                    act.activation(xft[:, j], pt[:, :], ACT.Copy)
                    act.drain().then_inc(s["kept"], 1)

                def relu(f):
                    act.wait_ge(s["r_ready"], g * FT + (f + 1))
                    act.activation(rh[:, f], pr[:, f % 2], ACT.Relu, bias=rb1[:, f:f + 1]).then_inc(s["r_kept"], 1)

                def shares():
                    act.wait_ge(s["gap_done"], g + 1)
                    act.activation(share[:, 1], share[:, 0], ACT.Exp).then_inc(s["exp_done"], 1)

                def keep_gates():
                    act.wait_ge(s["gate_turned"], g + 1)
                    act.activation(gate_t[:, j], pt[0:E, :], ACT.Copy).then_inc(s["gate_kept"], 1)

                if routed:
                    return [lambda: None, keep, lambda: (relu(0), relu(1)), lambda: (relu(2), relu(3)),
                            lambda: None, shares, keep_gates]
                return [lambda: None, keep, lambda: None, shares, keep_gates]

            def back(g, j, half, e):
                if e == E:
                    return
                for f in range(FT):
                    if f == 0:
                        act.wait_ge(s["y_ready"], g * (E + 1) + e)if e or not isinstance(g, int) or g else None
                    act.wait_ge(s["h_ready"], g * E * FT + (e * FT + f + 1))
                    act.activation(hid[:, e % 2, f], pf[:, f % 2], ACT.Relu, bias=b1[:, e, f:f + 1])\
                       .then_inc(s["h_kept"], 1)

            act.wait_ge(s["w_loaded"], 16 * len(loads))
            if not routed:
                act.wait_ge(s["b_ready"], 1)
            run(act, front, back)

        @block.vector
        def _(dve):
            dve.sem_inc(s["x_used"], 2)
            dve.sem_inc(s["gated"], 1)
            dve.sem_inc(s["y_used"], 2)
            dve.sem_inc(stored[0], 16)
            dve.sem_inc(stored[1], 16)
            dve.wait_ge(s["w_loaded"], 16 * len(loads))

            def add_bias():
                dve.wait_ge(s["w_bias"], 1)
                b1_all = b1[:, :, :].rearrange("p e f -> p (e f)")
                dve.tensor_tensor(b1_all, b1_all, pg[:, 0:E * FT], ALU.add)
                dve.drain().then_inc(s["b_ready"], 1)

            def prepare():
                for e in range(E):
                    if not routed:
                        dve.tensor_scalar(w1[:, e, :], w1[:, e, :], ln_g[:, e:e + 1], None, ALU.mult)
                        dve.drain()
                    split_12(dve, w1h[:, e, :], w1l[:, e, :], w1[:, e, :])
                    dve.drain().then_inc(s["w_ready"], 1)

            def front(g, j, half):
                def norm():
                    dve.wait_ge(x_loaded[j], half * 16 + 16)
                    ln_stats(dve, x_in[:, j], stats, mean_var)
                    dve.drain().then_inc(s["stats_done"], 1)
                    dve.wait_ge(s["rstd_done"], g * NLN + 1)
                    ln_apply(dve, xf[:, j], x_in[:, j], mean_var, rstd)
                    dve.drain()
                    if not routed:
                        ln_stats(dve, xf[:, j], stats, mean_var)
                        dve.drain().then_inc(s["stats_done"], 1)
                        dve.wait_ge(s["rstd_done"], g * NLN + 2)
                        dve.wait_ge(s["turned"], g + 1)
                        ln_apply(dve, z, xf[:, j], mean_var, rstd)
                        dve.drain()
                    dve.drain().then_inc(s["normed"], 1)

                def split():
                    dve.wait_ge(s["kept"], g + 2)
                    split_12(dve, xh[:, j], xl[:, j], (xft if routed else zt)[:, j])
                    dve.drain().then_inc(s["split"], 1)

                def pick():
                    dve.wait_ge(s["scored"], g + 1)
                    now = pg[:, 0:T * E].rearrange("p (t e) -> p t e", t=T)
                    if routed:
                        dve.tensor_tensor(score[:, :, :], now, rb2[:, :, :], ALU.add)
                    else:
                        dve.tensor_copy(score[:, :, :], now)
                    dve.drain()
                    for t in range(T):
                        dve.max(top[:, t, :], score[:, t, :])
                    dve.drain()
                    for t in range(T):
                        dve.max_index(top_i[:, t, :], top[:, t, :], score[:, t, :])
                    if routed:
                        dve.tensor_tensor(share[:, 0], top[:, :, 1], top[:, :, 0], ALU.subtract)
                    else:
                        dve.tensor_scalar(share[:, 0], top[:, :, 0], -1.0, None, ALU.mult)
                    dve.drain().then_inc(s["gap_done"], 1)
                    dve.tensor_copy(top_f[:, :, :], top_i[:, :, :])
                    dve.drain()

                def gates():
                    dve.wait_ge(s["exp_done"], g + 1)
                    dve.tensor_scalar(share[:, 2], share[:, 1], 1.0, None, ALU.add)
                    dve.drain()
                    dve.reciprocal(share[:, 2], share[:, 2])
                    dve.drain()
                    if routed:
                        dve.tensor_tensor(share[:, 1], share[:, 1], share[:, 2], ALU.mult)
                        dve.drain()
                    for t in range(T):
                        dve.tensor_scalar(gate[:, j, t, :], iota[:, :], top_f[:, t, 0:1], share[:, 2, t:t + 1],
                                          ALU.is_equal, ALU.mult)
                        if routed:
                            dve.tensor_scalar(gate2[:, t, :], iota[:, :], top_f[:, t, 1:2], share[:, 1, t:t + 1],
                                              ALU.is_equal, ALU.mult)
                    dve.drain()
                    if routed:
                        dve.tensor_tensor(gate[:, j], gate[:, j], gate2[:, :, :], ALU.add)
                        dve.drain()
                    dve.drain().then_inc(s["gated"], 1)

                if routed:
                    return [norm, lambda: None, split, lambda: None, pick, gates]
                return [norm, lambda: None, lambda: (split(), pick()), gates]

            def back(g, j, half, e):
                v = e
                dve.wait_ge(s["y_ready"], g * (E + 1) + (v + 2))
                y = py[:, (g_par(j) + v) % 2].rearrange("p (t d) -> p t d", t=T)
                if v == 0:
                    hold(dve, stored[j], half * 16 + 16, const)
                    dve.tensor_tensor(xo[:, j], y, x_in[:, j], ALU.add)
                    dve.drain().then_inc(s["x_used"], 1)
                    if not routed:
                        dve.tensor_tensor(xo[:, j], xo[:, j], xf[:, j], ALU.add)
                        dve.drain()
                    dve.sem_inc(s["y_used"], 1)
                else:
                    for t in range(T):
                        dve.scalar_tensor_tensor(xo[:, j, t], y[:, t], gate[:, j, t, v - 1:v], xo[:, j, t],
                                                 ALU.mult, ALU.add)
                    dve.drain().then_inc(s["y_used"], 1)
                if v == E:
                    dve.sem_inc(s["summed"], 1)

            run(dve, front, back, None if routed else add_bias, prepare)


def g_par(j):
    return (E + 1) * j % 2


def phase_cope(nc, w, x, out, const):
    HG = 4
    NG = AH // HG
    W = P + 1
    ONE = 1 << 17
    NB = 6
    UK, UT, UZ = NG, 2 * NG, NG
    SCALE = float(AD) ** -0.5
    with Phase(nc, "at") as ph:
        wq, wk, wv, wo = (ph.sb(n, [D, D]) for n in ("wq", "wk", "wv", "wo"))
        cols = ph.sb("cols", [D, 4 + 2 * HG])
        bv = ph.sb("bv", [P, T, D])
        bo = ph.sb("bo", [P, T, D])
        pos = ph.sb("pos", [D, AH * P])
        tri = ph.sb("tri", [P, P])
        offset = ph.sb("offset", [3, HG * P], BF16)
        ones = ph.sb("ones", [3, P], BF16)
        least = ph.sb("least", [P, P])
        x_in = ph.sb("x_in", [P, 2, T, D])
        xb = ph.sb("xb", [P, 2, T, D])
        xa = ph.sb("xa", [P, T, D])
        xat = ph.sb("xat", [D, GT])
        stats, mean_var, rstd = ph.sb("stats", [P, T, 6]), ph.sb("mean_var", [P, T, 2]), ph.sb("rstd", [P, T])
        qf = ph.sb("qf", [D, 2, GT])
        qz = ph.sb("qz", [D, 2, HG, GT])
        kz = ph.sb("kz", [D, 2, NG, GT])
        va = ph.sb("va", [P, 2, T, AH, AD + 1])
        th = ph.sb("th", [P, AH, P])
        vint = ph.sb("vint", [P, AH, P], I32)
        frac = ph.sb("frac", [P, AH, P])
        sh = ph.sb("sh", [P, AH, W], I16)
        bit = ph.sb("bit", [P, 3, AH, W], I16)
        tab = ph.sb("tab", [P, 2, AH, W])
        lg = ph.sb("lg", [P, 2, AH, P])
        step = ph.sb("step", [P, AH, P])
        at = ph.sb("at", [P, 2, AH, P])
        mx = ph.sb("mx", [P, 2, AH])
        pr = ph.sb("pr", [P, 2, AH, P])
        prt = ph.sb("prt", [P, AH, P])
        rec = ph.sb("rec", [P, AH])
        o = ph.sb("o", [P, D])
        ot = ph.sb("ot", [D, P])
        xo = ph.sb("xo", [P, 2, T, D])
        pa, pv = ph.psum("pa", [P, 2, HG * P]), ph.psum("pv", [P, AH, P])
        pm, pz = ph.psum("pm", [P, GT]), ph.psum("pz", [P, GT])
        x_loaded = [ph.sem("x_loaded0"), ph.sem("x_loaded1")]
        stored = [ph.sem("stored0"), ph.sem("stored1")]
        s = ph.sems("w_loaded", "w_ready", "x_used", "xb_done", "stats_done", "rstd_done", "normed", "m_ready", "m_kept",
                    "v_added", "a_ready", "a_used", "tanh_done", "kept", "rounded", "v_ready", "v_read", "sh_done",
                    "frac_ready", "frac_done", "routed", "step_done", "upper_done", "lower_done", "at_done",
                    "max_done", "exp_done", "o_ready", "o_done", "ot_ready", "ot_kept", "wo_ready", "added")
        src, dst = column_groups(x), column_groups(out)
        block = ph.block()
        loads = [(wq[:, :], w["wq"]), (wk[:, :], w["wk"]), (wv[:, :], w["wv"]), (wo[:, :], w["wo"]),
                 (cols[:, 0:1], w["bq"]), (cols[:, 1:2], w["bk"]), (cols[:, 4:4 + HG], w["head_mask"]),
                 (bv[:, :, :], w["bv"]), (bo[:, :, :], w["bo"]), (pos[:, :], w["pos"]), (tri[:, :], w["tri"]),
                 (offset[:, :], w["offset"]), (ones[:, :], w["ones"]), (least[:, :], w["least"])]

        def run(engine, start, front, main):
            for k in range(T):
                front(0, 0, 0, k)
            start((0, 0, 0, 0), (0, 1, 0, 0))

            def group(g, gs, own, next_half, first=False, final=False):
                def column(t):
                    if t < 0:
                        return None if first else (g - 1, t + T, 1 - gs, None)
                    if t >= T:
                        return None if final else (g + 1, t - T, 1 - gs, next_half)
                    return g, t, gs, own

                for t in range(T):
                    if not final:
                        front(g + 1, 1 - gs, next_half, t)
                    main(*(column(t + d) for d in (0, 1, 2, -1, -2, -3)))

            group(0, 0, 0, 0, first=True)
            with engine.Fori(0, G // 2 - 1) as i:
                group(i * 2 + 1, 1, i, i + 1)
                group(i * 2 + 2, 0, i + 1, i + 1)
            group(G - 1, 1, G // 2 - 1, None, final=True)
            ends = [(G - 1, t, 1, None) for t in range(T)]
            main(None, None, None, ends[T - 1], ends[T - 2], ends[T - 3])
            main(None, None, None, None, ends[T - 1], ends[T - 2])
            main(None, None, None, None, None, ends[T - 1])

        def count(c, more):
            return c[0] * T + (c[1] + more)

        def uses(g, t):
            if isinstance(g, int):
                c = g * T + t
                return sum(UT * (0 < k + 1 < A_COLS) + UK * (k + 2 < A_COLS) + UZ * (k > 0) for k in range(c)) + \
                    2 * UK + UT
            return g * (T * (UK + UT + UZ)) + (t * (UK + UT + UZ) + UK + UT)

        def use_of(what, here, nxt, after, last=True):
            base = uses(here[0], here[1]) if here else uses(G, 0 if last else 1)
            return base + (what != "t") * (UT if nxt else 0) + (what == "z") * (UK if after else 0)

        @block.sync
        def _(sp):
            def load(g, j):
                sp.wait_ge(s["x_used"], g + 1)
                sp.wait_ge(s["xb_done"], g + 1)
                sp.dma_start(x_in[:, j], src[g]).then_inc(x_loaded[j], 16)

            load(0, 0)
            for to, frm in loads:
                sp.dma_start(to, frm).then_inc(s["w_loaded"], 16)
            load(1, 1)

            def store(g, j):
                sp.wait_ge(s["added"], g * T + (T + 1))
                sp.dma_start(dst[g], xo[:, j]).then_inc(stored[j], 16)

            with sp.Fori(0, G // 2 - 1) as i:
                for j in range(2):
                    load(i * 2 + (j + 2), j)
                    store(i * 2 + j, j)
            store(G - 2, 0)
            store(G - 1, 1)
            for j in range(2):
                sp.wait_ge(stored[j], 16 * (G // 2 + 1))

        @block.gpsimd
        def _(pool):
            pool.sem_inc(s["xb_done"], 2)
            pool.sem_inc(s["at_done"], 2)
            pool.memset(va[:, :, :, :, :].rearrange("p j t h d -> p (j t h) d")[:, :, AD:AD + 1], 1.0)
            pool.drain()
            pool.wait_ge(s["w_loaded"], 16 * len(loads))

            def front(g, gs, half, k):
                if k == 0:
                    pool.wait_ge(s["stats_done"], g + 1)
                    ln_rstd(pool, mean_var[:, :, :], const["eps5"], const["minus_half"], rstd[:, :])\
                        .then_inc(s["rstd_done"], 1)
                if k == 3:
                    pool.wait_ge(s["added"], g * T + (1 - T)) if not isinstance(g, int) or g > 1 else None
                    pool.tensor_tensor(xb[:, gs], x_in[:, gs], bo[:, :, :], ALU.add).then_inc(s["xb_done"], 1)

            def main(here, nxt, after, last, before, oldest):
                if here is None:
                    return
                c = here[1] % 2
                pool.wait_ge(s["routed"], count(here, 1))
                pool.tensor_tensor(step[:, :, :], tab[:, c, :, 0:P], tab[:, c, :, 1:W], ALU.subtract)\
                    .then_inc(s["step_done"], 1)
                pool.wait_ge(s["upper_done"], count(here, 1))
                pool.tensor_tensor(lg[:, c], lg[:, c], tab[:, c, :, 0:P], ALU.add)
                pool.wait_ge(s["frac_done"], count(here, 1))
                pool.wait_ge(s["lower_done"], count(here, 1))
                pool.tensor_tensor(step[:, :, :], step[:, :, :], frac[:, :, :], ALU.mult)
                pool.drain()
                pool.wait_ge(s["exp_done"], count(here, -1)) if not isinstance(here[0], int) or count(here, -1) > 0 else None
                pool.tensor_tensor(at[:, c], lg[:, c], step[:, :, :], ALU.add)
                pool.drain().then_inc(s["at_done"], 1)

            run(pool, lambda *a: None, front, main)

        @block.tensor
        def _(pe):
            pe.sem_inc(s["o_ready"], 1)
            pe.wait_ge(s["w_loaded"], 16 * len(loads))
            pe.wait_ge(s["w_ready"], 1)

            def front(g, gs, half, k):
                if k == 1:
                    pe.wait_ge(s["v_added"], g + 1)
                    pe.wait_ge(s["normed"], g + 1)
                    for t in range(T):
                        last = pe.transpose(pm[:, t * P:(t + 1) * P], xa[:, t, :], const["ident"])
                    last.then_inc(s["m_ready"], 1)
                    pe.wait_ge(s["m_kept"], g * 3 + 1)
                    pe.matmul(pm[:, :], wq[:, :], xat[:, :], start=True, stop=True).then_inc(s["m_ready"], 1)
                if k == 2:
                    pe.wait_ge(s["m_kept"], g * 3 + 2)
                    pe.matmul(pm[:, :], wk[:, :], xat[:, :], start=True, stop=True).then_inc(s["m_ready"], 1)
                    pe.wait_ge(s["m_kept"], g * 3 + 3)
                    for t in range(T):
                        tok = slice(t * P, (t + 1) * P)
                        last = pe.matmul(pm[:, tok], xat[:, tok], wv[:, :], start=True, stop=True)
                    last.then_inc(s["m_ready"], 1)

            def tok_of(c):
                return slice(c[1] * P, (c[1] + 1) * P)

            def gates(c, base):
                pe.wait_ge(s["m_kept"], c[0] * 3 + 3)
                for n in range(NG):
                    pe.wait_ge(s["a_used"], base + (n + 1))
                    pe.matmul(pa[:, n % 2].rearrange("p (h q) -> p h q", h=HG), kz[:, c[2], n, tok_of(c)],
                              qz[:, c[2], :, tok_of(c)], start=True, stop=True).then_inc(s["a_ready"], 1)

            def tables(c, base):
                for n in range(UT):
                    pe.wait_ge(s["a_used"], base + (n + 1))
                    if n < NG:
                        pe.matmul(pa[:, n % 2], qf[:, c[2], tok_of(c)], pos[:, n * HG * P:(n + 1) * HG * P],
                                  start=True, stop=True).then_inc(s["a_ready"], 1)
                    else:
                        pe.matmul(pa[:, n % 2].rearrange("p (h q) -> p h q", h=NG), qz[:, c[2], n - NG, tok_of(c)],
                                  kz[:, c[2], :, tok_of(c)], start=True, stop=True).then_inc(s["a_ready"], 1)

            def positions(c):
                pe.wait_ge(s["v_read"], count(c, 1))
                pe.wait_ge(s["rounded"], count(c, 1))
                for hg in range(NG):
                    bank = pv[:, hg * HG:(hg + 1) * HG, :]
                    pe.matmul(bank, ones[:, :], offset[:, :].rearrange("k (h t) -> k h t", h=HG), start=True, stop=False)
                    for h in range(HG):
                        last = pe.matmul(pv[:, hg * HG + h, :], th[:, hg * HG + h, :], tri[:, :], start=False,
                                         stop=(h == HG - 1))
                last.then_inc(s["v_ready"], 1)

            def start(first, second):
                gates(first, 0)
                tables(first, UK)
                positions(first)
                gates(second, UK + UT)

            def main(here, nxt, after, last, before, oldest):
                if oldest:
                    pe.wait_ge(s["o_done"], count(oldest, 1))
                    pe.transpose(pz[:, 0:P], o[:, :], const["ident"]).then_inc(s["ot_ready"], 1)
                    pe.wait_ge(s["ot_kept"], count(oldest, 1))
                    pe.matmul(pz[:, P:2 * P], ot[:, :], wo[:, :], start=True, stop=True).then_inc(s["wo_ready"], 1)
                if nxt:
                    positions(nxt)
                    tables(nxt, use_of("t", here, nxt, after))
                if after:
                    gates(after, use_of("k", here, nxt, after))
                if before:
                    pe.wait_ge(s["a_used"], use_of("t", here, nxt, after, last) + 2)
                    pe.wait_ge(s["added"], count(before, 1))
                    pe.wait_ge(s["v_added"], before[0] + 2)
                    for h in range(AH):
                        sums = pe.matmul(pz[:, h * (AD + 1):(h + 1) * (AD + 1)], prt[:, h, :],
                                         va[:, before[2], before[1], h, :], start=True, stop=True)
                    sums.then_inc(s["o_ready"], 1)
                if last:
                    base = use_of("z", here, nxt, after)
                    c = last[1] % 2
                    pe.wait_ge(s["exp_done"], count(last, 1))
                    for hg in range(NG):
                        pe.wait_ge(s["a_used"], base + (hg + 1))
                        for h in range(HG):
                            turned = pe.transpose(pa[:, hg % 2, h * P:(h + 1) * P], pr[:, c, hg * HG + h, :],
                                                  const["ident"])
                        turned.then_inc(s["a_ready"], 1)

            run(pe, start, front, main)

        @block.scalar
        def _(act):
            act.sem_inc(s["a_used"], 2)
            act.wait_ge(s["w_loaded"], 16 * len(loads))
            act.wait_ge(s["w_ready"], 1)

            def front(g, gs, half, k):
                if k == 1:
                    act.wait_ge(s["m_ready"], g * 4 + 1)
                    act.activation(xat[:, :], pm[:, :], ACT.Copy).then_inc(s["m_kept"], 1)
                    act.wait_ge(s["m_ready"], g * 4 + 2)
                    act.activation(qf[:, gs], pm[:, :], ACT.Identity, bias=cols[:, 0:1])
                    for h in range(HG):
                        last = act.activation(qz[:, gs, h, :], pm[:, :], ACT.Identity, scale=cols[:, 4 + h:5 + h],
                                              bias=cols[:, 4 + HG + h:5 + HG + h])
                    last.then_inc(s["m_kept"], 1)
                if k == 2:
                    act.wait_ge(s["m_ready"], g * 4 + 3)
                    for n in range(NG):
                        rows = slice(n * 32, n * 32 + 32)
                        last = act.activation(kz[rows, gs, n, :], pm[rows, :], ACT.Identity, scale=SCALE,
                                              bias=cols[rows, 2:3])
                    last.then_inc(s["m_kept"], 1)

            def gates(c, base):
                act.wait_ge(s["v_ready"], count(c, 0)) if not isinstance(c[0], int) or count(c, 0) else None
                for n in range(NG):
                    act.wait_ge(s["a_ready"], base + (n + 1))
                    act.activation(th[:, n * HG:(n + 1) * HG, :], pa[:, n % 2].rearrange("p (h q) -> p h q", h=HG),
                                   ACT.Tanh, scale=0.5).then_inc(s["a_used"], 1)
                act.drain().then_inc(s["tanh_done"], 1)

            def tables(c, base):
                hold(act, s["at_done"], count(c, 1), const)
                for n in range(UT):
                    act.wait_ge(s["a_ready"], base + (n + 1))
                    bank = pa[:, n % 2].rearrange("p (h q) -> p h q", h=HG)
                    if n < NG:
                        to = tab[:, c[1] % 2, n * HG:(n + 1) * HG, 1:W]
                    else:
                        to = lg[:, c[1] % 2, :, :].rearrange("p (n h) t -> p n h t", h=HG)[:, :, n - NG, :]
                    act.activation(to, bank, ACT.Copy).then_inc(s["a_used"], 1)
                act.drain().then_inc(s["kept"], 1)

            def shift(c):
                act.wait_ge(s["v_read"], count(c, 2))
                upper = vint[:, :, :].bitcast(I16).rearrange("p h (t w) -> p h t w", w=2)[:, :, :, 1]
                act.activation(sh[:, :, 1:W], upper, ACT.Copy)
                act.activation(sh[:, :, 0:1], upper[:, :, 0:1], ACT.Copy)
                act.drain().then_inc(s["sh_done"], 1)

            def start(first, second):
                gates(first, 0)
                tables(first, UK)
                shift(first)
                gates(second, UK + UT)

            def main(here, nxt, after, last, before, oldest):
                if here:
                    act.wait_ge(s["at_done"], count(here, 2))
                    act.wait_ge(s["frac_ready"], count(here, 1))
                    act.activation(frac[:, :, :], vint[:, :, :], ACT.Identity, scale=-1.0 / ONE,
                                   bias=cols[:, 3:4]).then_inc(s["frac_done"], 1)
                if oldest:
                    act.wait_ge(s["ot_ready"], count(oldest, 1))
                    act.activation(ot[:, :], pz[:, 0:P], ACT.Copy).then_inc(s["ot_kept"], 1)
                if nxt:
                    tables(nxt, use_of("t", here, nxt, after))
                    shift(nxt)
                if after:
                    gates(after, use_of("k", here, nxt, after))
                if last:
                    c = last[1] % 2
                    act.wait_ge(s["max_done"], count(last, 1))
                    for h in range(AH):
                        exps = act.activation(pr[:, c, h, :], at[:, c, h, :], ACT.Exp, bias=mx[:, c, h:h + 1])
                    exps.then_inc(s["exp_done"], 1)
                    base = use_of("z", here, nxt, after)
                    act.wait_ge(s["o_ready"], count(last, 1))
                    for hg in range(NG):
                        act.wait_ge(s["a_ready"], base + (hg + 1))
                        act.activation(prt[:, hg * HG:(hg + 1) * HG, :],
                                       pa[:, hg % 2].rearrange("p (h q) -> p h q", h=HG), ACT.Copy)\
                           .then_inc(s["a_used"], 1)

            run(act, start, front, main)

        @block.vector
        def _(dve):
            dve.sem_inc(s["x_used"], 2)
            dve.sem_inc(s["v_added"], 1)
            dve.sem_inc(s["v_read"], 1)
            dve.sem_inc(s["added"], 1)
            dve.sem_inc(stored[0], 16)
            dve.sem_inc(stored[1], 16)
            dve.memset(tab[:, :, :, 0:1].rearrange("p c h o -> p (c h) o"), 0.0)
            dve.memset(kz[:, :, :, :], 0.0)
            dve.wait_ge(s["w_loaded"], 16 * len(loads))
            dve.memset(cols[:, 3:4], -1.0 / ONE)
            dve.tensor_scalar(cols[:, 2:3], cols[:, 1:2], SCALE, None, ALU.mult)
            dve.tensor_scalar(cols[:, 4 + HG:4 + 2 * HG], cols[:, 4:4 + HG], cols[:, 0:1], None, ALU.mult)
            dve.drain().then_inc(s["w_ready"], 1)

            def front(g, gs, half, k):
                if k == 0:
                    dve.wait_ge(x_loaded[gs], half * 16 + 16)
                    ln_stats(dve, x_in[:, gs], stats, mean_var)
                    dve.drain().then_inc(s["stats_done"], 1)
                if k == 1:
                    dve.wait_ge(s["rstd_done"], g + 1)
                    ln_apply(dve, xa, x_in[:, gs], mean_var, rstd)
                    dve.drain().then_inc(s["normed"], 1)
                    dve.sem_inc(s["x_used"], 1)
                if k == 3:
                    dve.wait_ge(s["m_ready"], g * 4 + 4)
                    dve.tensor_tensor(va[:, gs].rearrange("p t h d -> p (t h) d")[:, :, 0:AD],
                                      pm[:, :].rearrange("p (k d) -> p k d", d=AD),
                                      bv[:, :, :].rearrange("p t (h d) -> p (t h) d", h=AH), ALU.add)
                    dve.drain().then_inc(s["v_added"], 1)

            def round_gates(c):
                dve.wait_ge(s["tanh_done"], count(c, 1))
                dve.tensor_scalar(th[:, :, :], th[:, :, :], 129.0, -129.0, ALU.add, ALU.add)
                dve.drain().then_inc(s["rounded"], 1)

            def fixed_point(c):
                dve.wait_ge(s["frac_done"], count(c, 0)) if not isinstance(c[0], int) or count(c, 0) else None
                dve.wait_ge(s["v_ready"], count(c, 1))
                dve.scalar_tensor_tensor(vint[:, :, :], pv[:, :, :], float(ONE),
                                         least[:, :].rearrange("p (o t) -> p o t", o=1).broadcast_to((P, AH, P)),
                                         ALU.mult, ALU.max)
                dve.drain().then_inc(s["v_read"], 1)

            def fraction(c):
                dve.wait_ge(s["sh_done"], count(c, 1))
                dve.tensor_scalar(vint[:, :, :], vint[:, :, :], ONE - 1, None, ALU.bitwise_and)
                dve.drain().then_inc(s["frac_ready"], 1)

            def start(first, second):
                round_gates(first)
                fixed_point(first)
                fraction(first)

            def bits(k):
                n = W - (1 << k)
                dve.tensor_scalar(bit[:, k % 2, :, 0:n], sh[:, :, 0:n], 2 << k, None, ALU.bitwise_and)

            def divide(c):
                dve.wait_ge(s["o_ready"], count(c, 2))
                got = pz[:, 0:AH * (AD + 1)].rearrange("p (h d) -> p h d", h=AH)
                dve.reciprocal(rec[:, :], got[:, :, AD])
                dve.drain()
                dve.tensor_tensor(o[:, :].rearrange("p (h d) -> p h d", h=AH), got[:, :, 0:AD],
                                  rec[:, :].rearrange("p (h o) -> p h o", o=1).broadcast_to((P, AH, AD)), ALU.mult)
                dve.drain().then_inc(s["o_done"], 1)

            def main(here, nxt, after, last, before, oldest):
                if nxt:
                    round_gates(nxt)
                if here:
                    c = here[1] % 2
                    dve.wait_ge(s["kept"], count(here, 1))
                    bits(NB)
                    dve.drain()
                    for k in range(NB, 0, -1):
                        n = W - (1 << k)
                        dve.copy_predicated(tab[:, c, :, 0:n], bit[:, k % 2, :, 0:n], tab[:, c, :, 1 << k:W])
                        if k > 1:
                            bits(k - 1)
                        dve.drain()
                        if k == NB and oldest:
                            divide(oldest)
                    dve.sem_inc(s["routed"], 1)
                    dve.tensor_scalar(bit[:, 2], sh[:, :, :], 2, None, ALU.bitwise_and)
                    dve.drain()
                elif oldest:
                    divide(oldest)
                if oldest:
                    dve.wait_ge(s["wo_ready"], count(oldest, 1))
                    if oldest[1] == 0:
                        hold(dve, stored[oldest[2]], oldest[3] * 16 + 16, const)
                    dve.tensor_tensor(xo[:, oldest[2], oldest[1], :], pz[:, P:2 * P], xb[:, oldest[2], oldest[1], :],
                                      ALU.add)
                    dve.drain().then_inc(s["added"], 1)
                if nxt:
                    fixed_point(nxt)
                if last:
                    dve.wait_ge(s["at_done"], count(last, 3))
                    dve.tensor_reduce(mx[:, last[1] % 2], at[:, last[1] % 2], AX.X, ALU.max, negate=True)
                    dve.drain().then_inc(s["max_done"], 1)
                if here:
                    hold(dve, s["step_done"], count(here, 1), const)
                    dve.copy_predicated(tab[:, c, :, 0:P], bit[:, 2, :, 1:W], tab[:, c, :, 1:W])
                    dve.drain().then_inc(s["upper_done"], 1)
                    dve.copy_predicated(step[:, :, 0:P - 1], bit[:, 2, :, 1:P], step[:, :, 1:P])
                    dve.drain().then_inc(s["lower_done"], 1)
                if nxt:
                    fraction(nxt)

            run(dve, start, front, main)


def build(nc, w, x, ctx, out):
    x2, x3, x4, x5 = (nc.dram_tensor(n, (A, S, D), F32, kind="Internal").ap() for n in ("x2", "x3", "x4", "x5"))
    with Phase(nc, "all") as keep:
        ident = keep.sb("ident", [P, P])
        small = keep.sb("small", [P, 3 * T])
        const = {"ident": ident[:, :], "minus_half": small[:, 0:T], "eps5": small[:, T:2 * T],
                 "eps6": small[:, 2 * T:3 * T]}
        ready = keep.sem("const_ready")
        const["passed"] = keep.sem("passed")
        with nc.Block() as block:
            @block.sync
            def _(sp):
                sp.dma_start(ident[:, :], w["ident"]).then_inc(ready, 16)
                sp.wait_ge(ready, 16)

            @block.vector
            def _(dve):
                dve.memset(const["minus_half"], -0.5)
                dve.memset(const["eps5"], 1e-5)
                dve.memset(const["eps6"], 1e-6)
                dve.drain()
        layer0, layer1 = expert_weights(w, "l0"), expert_weights(w, "l1")
        with Phase(nc, "W0") as weights:
            tiles, ahead = expert_tiles(weights, layer0)
            with Phase(nc, "L0") as l0:
                xn_t = l0.sb("xn_t", [D, TOK])
                phase_norm_in(nc, w, x, xn_t, const)
                with Phase(nc, "sk") as sk:
                    delta = sk.sb("delta", [D, TOK])
                    split = sk.sb("split", [6 * N, TOK], BF16)
                    guard = {k: sk.sb("g_" + k, [D, N]) for k in ("a_log", "a", "inv", "minus_inv", "near0", "far")}
                    guard["bc_pick"] = sk.sb("bc_pick", [6 * N, 2 * N * P], BF16)
                    with Phase(nc, "tmp") as tm:
                        tmp = tm.sb("tmp", [P, TOK])
                        phase_select(nc, w, xn_t, const, delta, split, guard, tmp)
                    phase_scan(nc, w, xn_t, const, delta, split, guard)
                phase_mlstm(nc, mlstm_weights(w, "l0"), "m0", x, ctx, x2, const, 1e-6, ahead, xn_t)
            phase_experts(nc, layer0, "f0", x2, x3, const, True, *tiles)
        phase_cope(nc, {k[3:]: v for k, v in w.items() if k.startswith("at_")}, x3, x4, const)
        with Phase(nc, "W1") as weights:
            tiles, ahead = expert_tiles(weights, layer1)
            phase_mlstm(nc, mlstm_weights(w, "l1"), "m1", x4, ctx, x5, const, 1e-5, ahead)
            phase_experts(nc, layer1, "f1", x5, out, const, False, *tiles)


def expert_tiles(ph, w):
    w1, w2 = ph.sb("w1", [D, E, F]), ph.sb("w2", [P, E, FT, D])
    return (w1, w2), [(w1[:, :, :], w["w1"]), (w2[:, :, :, :], w["w2"])]


def expert_weights(w, layer):
    return {k[len(layer) + 2:]: v for k, v in w.items() if k.startswith(layer + "f_")} | {"iota": w["iota"]}


def mlstm_weights(w, layer):
    own = {k: w[f"{layer}_{k}"] for k in ("gate_w", "gate_b", "norm_w")}
    return own | {k: w[k] for k in ("seq_tri", "mask", "ident_b", "minus_pick")}


def host_inputs(inputs):
    bf16 = np.dtype("bfloat16")
    f = {k: np.ascontiguousarray(v) for k, v in inputs.items()}
    col = lambda a: np.ascontiguousarray(a.reshape(-1, 1))
    tr = lambda a: np.ascontiguousarray(np.swapaxes(a, -1, -2))
    bc = np.concatenate([f["L0_attn_B_W"], f["L0_attn_C_W"]])
    bcb = np.concatenate([f["L0_attn_B_b"], f["L0_attn_C_b"]])
    pick = np.zeros((6 * N, 2 * N, P), bf16)
    for k in range(3):
        for n in range(2 * N):
            pick[k * 2 * N + n, n, :] = 1
    w = {
        "ident": np.eye(P, dtype=np.float32),
        "wi_t": tr(f["L0_attn_Wi_W"]), "wr_t": tr(f["L0_attn_Wr_W"]), "sel_t": tr(f["L0_attn_sel_W"]),
        "h0": col(f["L0_attn_h0"]), "tau": col(f["L0_attn_tau"]), "wi_b": col(f["L0_attn_Wi_b"]),
        "sel_b": col(f["L0_attn_sel_b"]), "delta_b": col(f["L0_attn_delta_b"]),
        "dt_bias": col(f["L0_attn_dt_bias"]), "delta_wt": tr(f["L0_attn_delta_W"]),
        "bc_wt": np.concatenate([tr(bc)] * 3, axis=1), "bc_bias": col(np.concatenate([bcb] * 3)),
        "a_log": f["L0_attn_A_log"], "bc_pick": pick.reshape(6 * N, 2 * N * P),
    }
    rows = lambda a, n: np.ascontiguousarray(np.broadcast_to(a.reshape(-1), (n, a.size)))
    for layer, pre, ig, fg, norm in (("l0", "L0_xattn_", "ig_", "fg_", "outnorm_weight"),
                                     ("l1", "L1_xattn_", "igate_", "fgate_", "outnorm_scale")):
        kern = np.concatenate([f[pre + ig + "kernel"], f[pre + fg + "kernel"]], axis=1)
        bias = np.concatenate([f[pre + ig + "bias"], f[pre + fg + "bias"]])
        w[layer + "_gate_w"] = np.ascontiguousarray(kern.reshape(3, D, 2 * NH).transpose(1, 0, 2))
        w[layer + "_gate_b"] = rows(np.tile(bias, T), P).reshape(P, T, 2 * NH)
        w[layer + "_norm_w"] = rows(f[pre + norm], P)
    by_f = lambda a: np.ascontiguousarray(a.reshape(*a.shape[:-1], FT, P).transpose(-1, *range(a.ndim)))
    w["iota"] = rows(np.arange(E, dtype=np.float32), P)
    w1, w2 = f["L0_ffn_W1"], f["L0_ffn_W2"]
    w["l0f_w1"] = np.ascontiguousarray(w1.transpose(1, 0, 2))
    w["l0f_w2"] = np.ascontiguousarray(w2.reshape(E, FT, P, D).transpose(2, 0, 1, 3))
    w["l0f_b1"], w["l0f_b2"] = by_f(f["L0_ffn_b1"]), f["L0_ffn_b2"]
    w["l0f_rw1"], w["l0f_rb1"] = f["L0_ffn_rw1"], by_f(f["L0_ffn_rb1"])
    w["l0f_rw2"] = np.ascontiguousarray(f["L0_ffn_rw2"].reshape(FT, P, E).transpose(1, 0, 2))
    w["l0f_rb2"] = rows(np.tile(f["L0_ffn_rb2"], T), P).reshape(P, T, E)
    w1, w2 = tr(f["L1_ffn_w1"]), tr(f["L1_ffn_w2"])
    w["l1f_w1"] = np.ascontiguousarray(w1.transpose(1, 0, 2))
    w["l1f_w2"] = np.ascontiguousarray(w2.reshape(E, FT, P, D).transpose(2, 0, 1, 3))
    w["l1f_b1"], w["l1f_b2"] = by_f(f["L1_ffn_b1"]), f["L1_ffn_b2"]
    w["l1f_cent"], w["l1f_ln_g"], w["l1f_ln_b"] = (tr(f["L1_ffn_" + k]) for k in ("centroids", "ln_g", "ln_b"))
    for k in ("q", "k", "v", "o"):
        w["at_w" + k] = f["L1_attn_W" + k]
    w["at_bq"], w["at_bk"] = col(f["L1_attn_bq"]), col(f["L1_attn_bk"])
    w["at_bv"], w["at_bo"] = (rows(np.tile(f["L1_attn_b" + k], T), P).reshape(P, T, D) for k in "vo")
    w["at_head_mask"] = (np.arange(D)[:, None] % 32 // AD == np.arange(4)[None, :]).astype(np.float32)
    pos = np.zeros((AH, AD, AH, P), np.float32)
    npos = f["L1_attn_pos_emb"].shape[-1]
    for h in range(AH):
        pos[h, :, h, P - npos:] = f["L1_attn_pos_emb"][0][:, ::-1]
    w["at_pos"] = pos.reshape(D, AH * P)
    t, s_ = np.arange(P)[:, None], np.arange(P)[None, :]
    w["at_tri"] = np.where(t >= s_, -0.5, 0.0).astype(np.float32)
    off = (P - np.arange(P)) / 2 - 2.0 ** -17
    parts = []
    for _ in range(3):
        parts.append(off.astype(bf16))
        off = off - parts[-1].astype(np.float64)
    w["at_offset"] = np.tile(np.stack(parts), (1, 4))
    w["at_ones"] = np.ones((3, P), bf16)
    w["at_least"] = rows((np.maximum(0, P - 1 - (npos - 2) - np.arange(P)) * 2.0 ** 17).astype(np.float32), P)
    t, s_ = np.arange(P)[:, None], np.arange(P)[None, :]
    seen = (t // S == s_ // S) & (t <= s_)
    w["seq_tri"] = seen.astype(np.float32)
    w["mask"] = np.tile(np.where(seen, 0.0, -1e30), (1, T)).astype(bf16)
    w["ident_b"] = np.eye(P).astype(bf16)
    w["minus_pick"] = -np.repeat(np.eye(P, T * NH, dtype=np.float32), P, axis=1)
    return {"x": f["x"], "ctx": f["ctx_1024"]}, w


def kernel(**inputs):
    import concourse.bacc as bacc
    from concourse.bass_utils import run_bass_kernel_spmd

    nc = bacc.Bacc("TRN2", target_bir_lowering=False, num_devices=1)
    data, w = host_inputs(inputs)
    arrays = {f"in_{k}": v for k, v in {**data, **w}.items()}
    aps = {k: nc.dram_tensor(k, v.shape, mybir.dt.from_np(v.dtype), kind="ExternalInput").ap() for k, v in arrays.items()}
    out = nc.dram_tensor("out_0", (A, S, D), F32, kind="ExternalOutput").ap()
    build(nc, {k: aps[f"in_{k}"] for k in w}, aps["in_x"], aps["in_ctx"], out)
    r = run_bass_kernel_spmd(nc, [arrays], core_ids=[0])
    return r.results[0]["out_0"]
```
